# Optimizing a Trainium2 kernel written in Bass

```python
import numpy as np
import jax
import jax.numpy as jnp

def _softmax(x, axis=-1):
    return jax.nn.softmax(x, axis=axis)
def _gelu(x):
    return jax.nn.gelu(x, approximate=True)
def _silu(x):
    return jax.nn.silu(x)
def _sigmoid(x):
    return jax.nn.sigmoid(x)
def _layernorm(x, axis=-1, eps=1e-5):
    m = jnp.mean(x, axis=axis, keepdims=True)
    v = jnp.var(x, axis=axis, keepdims=True)
    return (x - m) / jnp.sqrt(v + eps)
def _scatter_add(tgt, idx, src, axis=0):
    return tgt.at[idx].add(src)
def _segment_sum(src, seg, n):
    return jax.ops.segment_sum(src, seg, n)

kernel_name = 'mk_adj_resnorm_d4_adj_256_27ecf0'

def setup_inputs(seed: int = 0):
    np.random.seed(seed)
    _w = jnp.asarray
    def _rec_inputs():
        import jax
        import jax.numpy as jnp
        _gk = jax.random.key(seed)
        x = -0.0002928 + 1 * jax.random.normal(jax.random.fold_in(_gk, 1), (4096, 256), jnp.float32)
        _w = (1.0 + jnp.arange(4096, dtype=jnp.float32)) ** -0.5
        _w = _w / _w.mean()
        _pij = jnp.clip(0.00390625 * _w[:, None] * _w[None, :], 0.0, 1.0)
        _a = jax.random.uniform(jax.random.fold_in(_gk, 2), (4096, 4096)) < _pij
        _a = jnp.logical_or(_a, jnp.eye(4096, dtype=bool))
        _af = _a.astype(jnp.float32)
        _af = _af * jax.random.uniform(jax.random.fold_in(_gk, 3), (4096, 4096), jnp.float32, 0.05, 1)
        adj = _af
        return x, adj
    x, adj = _rec_inputs()
    def _L0_gnn_setup():
        import jax, jax.numpy as jnp
        import numpy as np
        N, D_IN, D_OUT = (16384, 256, 256)
        key = jax.random.key(seed)
        k1, k2, k3, k4 = jax.random.split(key, 4)
        x = jax.random.normal(k1, (N, D_IN), dtype=jnp.float32)
        adj = jax.random.uniform(k2, (N, N), dtype=jnp.float32)
        W = jax.random.normal(k3, (D_IN, D_OUT), dtype=jnp.float32) / np.sqrt(D_IN)
        b = jax.random.normal(k4, (D_OUT,), dtype=jnp.float32) * 0.01
        return {'x': x, 'adj': adj, 'W': W, 'b': b}
    _L0_gnn_all = _L0_gnn_setup()
    _L0_gnn_in = {k: v for k, v in _L0_gnn_all.items() if k in ('W', 'b', )}
    del _L0_gnn_all

    def _L1_gnn_setup():
        import jax, jax.numpy as jnp
        import numpy as np
        N = 20000
        D = 256
        F = 256
        K = F // 8
        key = jax.random.key(seed)
        k1, k2, k3, k4, k5 = jax.random.split(key, 5)
        h = jax.random.normal(k1, (N, D), dtype=jnp.float32)
        adj = jax.random.uniform(k2, (N, N), dtype=jnp.float32)
        W1 = jax.random.normal(k3, (D, K), dtype=jnp.float32) * 0.05
        W2 = jax.random.normal(k4, (K, D, F), dtype=jnp.float32) * 0.05
        b = jax.random.normal(k5, (K, F), dtype=jnp.float32) * 0.05
        return {'h': h, 'adj': adj, 'W1': W1, 'W2': W2, 'b': b}
    _L1_gnn_all = _L1_gnn_setup()
    _L1_gnn_in = {k: v for k, v in _L1_gnn_all.items() if k in ('W1', 'W2', 'b', )}
    del _L1_gnn_all

    def _L2_gnn_setup():
        import jax, jax.numpy as jnp
        import numpy as np
        N = 8192
        IN_F = 256
        OUT_F = 256
        ATTN_DIM = 2
        NEG_INF = -1e+18
        key = jax.random.key(seed)
        k1, k2, k3, k4, k5 = jax.random.split(key, 5)
        node_feats = jax.random.normal(k1, (N, IN_F), dtype=jnp.float32)
        Ahat = (jax.random.uniform(k2, (N, N)) < 0.01).astype(jnp.float32)
        Ahat = Ahat.at[jnp.arange(N), jnp.arange(N)].set(1.0)
        bound_w = 1.0 / np.sqrt(IN_F)
        bound_wa = 1.0 / np.sqrt(OUT_F)
        bound_a = 1.0 / np.sqrt(2 * ATTN_DIM)
        w = jax.random.uniform(k3, (IN_F, OUT_F), minval=-bound_w, maxval=bound_w, dtype=jnp.float32)
        w_a = jax.random.uniform(k4, (OUT_F, ATTN_DIM), minval=-bound_wa, maxval=bound_wa, dtype=jnp.float32)
        a = jax.random.uniform(k5, (2 * ATTN_DIM, 1), minval=-bound_a, maxval=bound_a, dtype=jnp.float32)
        return {'node_feats': node_feats, 'Ahat': Ahat, 'w': w, 'w_a': w_a, 'a': a}
    _L2_gnn_all = _L2_gnn_setup()
    _L2_gnn_in = {k: v for k, v in _L2_gnn_all.items() if k in ('w', 'w_a', 'a', )}
    del _L2_gnn_all

    def _L3_gnn_setup():
        import jax, jax.numpy as jnp
        import numpy as np
        N = 4096
        IN_F = 256
        OUT_F = 64
        H = 4
        NEG_SLOPE = 0.2
        key = jax.random.key(seed)
        k1, k2, k3, k4 = jax.random.split(key, 4)
        x = jax.random.normal(k1, (N, IN_F), dtype=jnp.float32)
        adj = jax.random.randint(k2, (N, N), 0, 2).astype(jnp.float32)
        limW = float(np.sqrt(6.0 / (IN_F + OUT_F)))
        W = jax.random.uniform(k3, (H, IN_F, OUT_F), minval=-limW, maxval=limW, dtype=jnp.float32)
        lima = float(np.sqrt(6.0 / (2 * OUT_F + 1)))
        a = jax.random.uniform(k4, (H, 2 * OUT_F, 1), minval=-lima, maxval=lima, dtype=jnp.float32)
        return {'x': x, 'adj': adj, 'W': W, 'a': a}
    _L3_gnn_all = _L3_gnn_setup()
    _L3_gnn_in = {k: v for k, v in _L3_gnn_all.items() if k in ('W', 'a', )}
    del _L3_gnn_all

    return {
        "x": x,
        "adj": adj,
        "L0_gnn_W": _L0_gnn_in["W"],
        "L0_gnn_b": _L0_gnn_in["b"],
        "L1_gnn_W1": _L1_gnn_in["W1"],
        "L1_gnn_W2": _L1_gnn_in["W2"],
        "L1_gnn_b": _L1_gnn_in["b"],
        "L2_gnn_w": _L2_gnn_in["w"],
        "L2_gnn_w_a": _L2_gnn_in["w_a"],
        "L2_gnn_a": _L2_gnn_in["a"],
        "L3_gnn_W": _L3_gnn_in["W"],
        "L3_gnn_a": _L3_gnn_in["a"],
    }

def reference(x, adj, L0_gnn_W, L0_gnn_b, L1_gnn_W1, L1_gnn_W2, L1_gnn_b, L2_gnn_w, L2_gnn_w_a, L2_gnn_a, L3_gnn_W, L3_gnn_a):
    import jax
    import jax.numpy as jnp
    def _L0_gnn_ref(x, adj, W, b):
        import jax, jax.numpy as jnp
        import numpy as np
        N, D_IN, D_OUT = (16384, 256, 256)
        support = jnp.matmul(x, W)
        out = jnp.matmul(adj, support) + b
        return jax.nn.relu(out)

    def _L1_gnn_ref(h, adj, W1, W2, b):
        import jax, jax.numpy as jnp
        import numpy as np
        N = 20000
        D = 256
        F = 256
        K = F // 8
        node = h @ W1
        hw = jnp.einsum('nc,kcf->nkf', h, W2)
        x = jnp.einsum('nk,nkf->nf', node, hw)
        x = adj @ x
        x = x + node @ b
        return jax.nn.relu(x)

    def _L2_gnn_ref(node_feats, Ahat, w, w_a, a):
        import jax, jax.numpy as jnp
        import numpy as np
        N = 8192
        IN_F = 256
        OUT_F = 256
        ATTN_DIM = 2
        NEG_INF = -1e+18
        h_prime = node_feats @ w
        h_reduced = h_prime @ w_a
        f_src = (h_reduced @ a[:ATTN_DIM]).squeeze(-1)
        f_dst = (h_reduced @ a[ATTN_DIM:]).squeeze(-1)
        e = f_src[:, None] + f_dst[None, :]
        masked_e = jnp.where(Ahat > 0, e, NEG_INF)
        attn_scores = jax.nn.softmax(masked_e, axis=-1)
        out = attn_scores @ h_prime
        return jax.nn.relu(out)

    def _L3_gnn_ref(x, adj, W, a):
        import jax, jax.numpy as jnp
        import numpy as np
        N = 4096
        IN_F = 256
        OUT_F = 64
        H = 4
        NEG_SLOPE = 0.2
        n = x.shape[0]
        h, _, fo = W.shape
        Wh = jnp.einsum('nd,hdo->nho', x, W)
        a_src = a[:, :fo, 0]
        a_dst = a[:, fo:, 0]
        s_i = jnp.einsum('nho,ho->nh', Wh, a_src)
        s_j = jnp.einsum('nho,ho->nh', Wh, a_dst)
        e = jax.nn.leaky_relu(s_i[:, None, :] + s_j[None, :, :], NEG_SLOPE)
        idx = jnp.arange(n)
        adj_sl = adj.at[idx, idx].set(1.0)
        mask = (adj_sl != 0)[:, :, None]
        e_masked = jnp.where(mask, e, -jnp.inf)
        attention = jax.nn.softmax(e_masked, axis=1)
        h_prime = jnp.einsum('ijh,jho->iho', attention, Wh)
        return h_prime.reshape(n, h * fo)

    x = _layernorm(x + _L0_gnn_ref(x, adj, L0_gnn_W, L0_gnn_b), axis=-1)
    x = _layernorm(x + _L1_gnn_ref(x, adj, L1_gnn_W1, L1_gnn_W2, L1_gnn_b), axis=-1)
    x = _layernorm(x + _L2_gnn_ref(x, adj, L2_gnn_w, L2_gnn_w_a, L2_gnn_a), axis=-1)
    x = _layernorm(x + _L3_gnn_ref(x, adj, L3_gnn_W, L3_gnn_a), axis=-1)
    return x


_drawn_inputs = setup_inputs


def setup_inputs(seed=0):
    import zlib

    import numpy as np

    out = dict(_drawn_inputs(seed))
    spreads = {}
    factors = {'L0_gnn_b': 8.0, 'L2_gnn_w_a': 3.975, 'L2_gnn_a': 7.937}
    for name, (base, spread) in spreads.items():
        noise = np.random.default_rng([zlib.crc32(name.encode()), seed]).standard_normal(out[name].shape)
        drawn = base * np.exp(spread * noise) if base else spread * noise
        out[name] = jnp.asarray(drawn.astype(out[name].dtype))
    for name, factor in factors.items():
        out[name] = (out[name] * factor).astype(out[name].dtype)
    return out
```

```python
from contextlib import ExitStack

import concourse.bass as bass
from concourse import mybir

F32 = mybir.dt.float32
F32R = mybir.dt.float32r
BF16 = mybir.dt.bfloat16
F16 = mybir.dt.float16
ALU = mybir.AluOpType
ACT = mybir.ActivationFunctionType
AX = mybir.AxisListType
RMAX = bass.bass_isa.ReduceOp.max
ds = bass.ds

P = 128
D = 256
DC = D // P
TB = 2
RB = TB * P
JC = 4
JM = 4
RAWS = 4
EPS = 1e-5
KQ = 32
H = 4
FO = D // H
FH = FO + 1
SLOPE = 0.2
BIG = 2.0 ** 60
LIFT2 = 60.0
LIFT3 = 4.0
IB = 1024
IT = IB // P
KB = 1024


class Steps:

    def __init__(self, engine, sem, base=0):
        self.engine, self.sem, self.base, self.n = engine, sem, base, 0

    def step(self, instruction):
        instruction.then_inc(self.sem, 1)
        self.n += 1

    def join(self):
        count = self.base + self.n
        if not isinstance(count, int) or count > 0:
            self.engine.wait_ge(self.sem, count)


class Net:

    def __init__(self, nc, n):
        self.nc, self.N, self.NT = nc, n, n // P
        self.NBLK = n // RB
        self.K = self.NT // JC
        nt = self.NT
        at = {}
        room = self.room = max(nt, 32)
        base = 16512
        at["X"] = base
        at["S"] = at["X"] + room * D * 4
        at["HT"] = at["S"] + 2 * room * D * 4
        at["strip"] = at["HT"] + 2 * room * D * 4
        at["small"] = at["strip"] + 36 * KB
        self.at = at
        self.a3_bc = None
        self.end = at["small"]
        self.serial = 0
        self.X = self.place("X", [P, nt, D], F32, at["X"])
        self.ident = self.small("ident", [P, P], F32)
        self.at["w"] = self.end
        self.w_hi = self.small("w_hi", [P, DC, D], F32R)
        self.w_lo = self.small("w_lo", [P, DC, D], F32R)
        self.a2_bc = self.small("a2_bc", [P, 1, D], F32)
        self.f_dst = self.small("f_dst", [P, nt], F32)
        self.s_src = self.small("s_src", [P, nt, H], F32)
        self.s_dst = self.small("s_dst", [P, nt, H], F32)
        self.scratch = self.end
        self.ps = nc.alloc_psum_tensor("ps", [P, 8, 512], F32)

    def place(self, name, shape, dt, offset):
        self.serial += 1
        return self.nc.alloc_sbuf_tensor_at(f"{name}_{self.serial}", shape, dt, offset=offset)

    def small(self, name, shape, dt):
        size = 1
        for s in shape[1:]:
            size *= s
        size *= 2 if dt in (BF16, F16) else 4
        t = self.place(name, shape, dt, self.end)
        self.end += (size + 31) // 32 * 32
        assert self.end <= 229344, (name, self.end)
        return t


def sems(ctx, nc, stage, names):
    return [ctx.enter_context(nc.semaphore(f"{stage}_{n}")) for n in names.split()]


def stage_project0(net, x, w0):
    nc, ps = net.nc, net.ps
    nb = net.NBLK
    net.end = net.scratch
    xin = net.place("xin", [P, 2, TB, D], F32, net.at["HT"])
    xt_hi = net.place("xt_hi", [P, TB, DC, P], F32R, net.at["HT"] + 4 * KB)
    xt_lo = net.place("xt_lo", [P, TB, DC, P], F32R, net.at["HT"] + 6 * KB)
    w_raw = net.place("w_raw", [P, DC, D], F32, net.at["strip"])
    S = net.place("S0", [P, net.NT, 2 * D], F32R, net.at["S"])
    net.S = S
    with ExitStack() as ctx:
        (w_in, x_in, xin0, xin1, zeroed, ident_ready, whi_ready, wlo_ready, turned, hi_ready, lo_ready,
         projected, shi_done, slo_done) = sems(
            ctx, nc, "p0", "w_in x_in xin0 xin1 zeroed ident whi wlo turned hi lo projected shi slo")
        xin_ready = [xin0, xin1]
        blk = ctx.enter_context(nc.Block())
        xv = x.rearrange("(b t p) f -> b p t f", t=TB, p=P)

        @blk.sync
        def _(sp):
            sp.dma_start(w_raw[:], w0.rearrange("(c p) f -> p c f", p=P)).then_inc(w_in, 16)

            def load(b, par):
                sp.dma_start(xin[:, par], xv[b]).then_inc(xin_ready[par], 16)

            load(0, 0)
            load(1, 1)
            sp.dma_start(net.X[:], x.rearrange("(t p) f -> p t f", p=P)).then_inc(x_in, 16)
            for b in range(2, nb):
                sp.wait_ge(turned, b - 1)
                load(b, b % 2)
            sp.wait_ge(x_in, 16)

        @blk.gpsimd
        def _(pool):
            pool.memset(net.ident[:], 0.0).then_inc(zeroed, 1)
            pool.wait_ge(zeroed, 1)
            pool.affine_select(out=net.ident[:], in_=net.ident[:], compare_op=ALU.not_equal, fill=1.0,
                               base=0, pattern=[[-1, P]], channel_multiplier=1).then_inc(ident_ready, 1)

        @blk.scalar
        def _(act):
            act.wait_ge(w_in, 16)
            act.activation(net.w_hi[:], w_raw[:], ACT.Copy).then_inc(whi_ready, 1)
            for b in range(nb):
                act.wait_ge(turned, b + 1)
                if b >= 1:
                    act.wait_ge(projected, b)
                act.activation(xt_hi[:], ps[:, b % 2].rearrange("p (t c n) -> p t c n", t=TB, c=DC),
                               ACT.Copy).then_inc(hi_ready, 1)
                act.wait_ge(projected, b + 1)
                act.activation(S[:, TB * b:TB * b + TB, 0:D],
                               ps[:, 2 + b % 2].rearrange("p (t f) -> p t f", t=TB),
                               ACT.Copy).then_inc(shi_done, 1)

        @blk.vector
        def _(dve):
            dve.wait_ge(whi_ready, 1)
            dve.tensor_tensor(net.w_lo[:], w_raw[:], net.w_hi[:].bitcast(F32), ALU.subtract).then_inc(wlo_ready, 1)
            for b in range(nb):
                dve.wait_ge(hi_ready, b + 1)
                dve.tensor_tensor(xt_lo[:], ps[:, b % 2].rearrange("p (t c n) -> p t c n", t=TB, c=DC),
                                  xt_hi[:].bitcast(F32), ALU.subtract).then_inc(lo_ready, 1)
                dve.wait_ge(shi_done, b + 1)
                dve.tensor_tensor(S[:, TB * b:TB * b + TB, D:2 * D],
                                  ps[:, 2 + b % 2].rearrange("p (t f) -> p t f", t=TB),
                                  S[:, TB * b:TB * b + TB, 0:D].bitcast(F32), ALU.subtract).then_inc(slo_done, 1)

        @blk.tensor
        def _(pe):
            def turn(b):
                pe.wait_ge(xin_ready[b % 2], 16 * (b // 2 + 1))
                if b >= 2:
                    pe.wait_ge(lo_ready, b - 1)
                for t in range(TB):
                    for c in range(DC):
                        at = (t * DC + c) * P
                        last = pe.transpose(ps[:, b % 2, at:at + P], xin[:, b % 2, t, c * P:c * P + P],
                                            net.ident[:])
                last.then_inc(turned, 1)

            pe.wait_ge(ident_ready, 1)
            pe.wait_ge(wlo_ready, 1)
            turn(0)
            for b in range(nb):
                if b + 1 < nb:
                    turn(b + 1)
                pe.wait_ge(lo_ready, b + 1)
                if b >= 2:
                    pe.wait_ge(slo_done, b - 1)
                project(pe, net, 2 + b % 2, xt_hi, xt_lo).then_inc(projected, 1)


def project(pe, net, bank, xt_hi, xt_lo):
    for t in range(TB):
        out = net.ps[:, bank, t * D:(t + 1) * D]
        n = 0
        for c in range(DC):
            for a, w in ((xt_hi, net.w_hi), (xt_hi, net.w_lo), (xt_lo, net.w_hi)):
                last = pe.matmul(out, a[:, t, c, :], w[:, c, :], start=(n == 0), stop=(n == 3 * DC - 1))
                n += 1
    return last


def stage_aggregate(net, kind, adj_t, mask, w_next, vec_next, bias):
    nc, ps, K, nb = net.nc, net.ps, net.K, net.NBLK
    dense = kind < 2
    jc = JC if dense else JM
    K = net.NT // jc
    net.end = net.scratch
    strip = net.at["strip"]
    csize = jc * RB
    if dense:
        raw = net.place("raw", [P, RAWS, jc, RB], F32, strip)
        hi = net.place("hi", [P, 2, jc, RB], F32R, strip + RAWS * csize * 4)
        lo = net.place("lo", [P, 2, jc, RB], F32R, strip + (RAWS + 2) * csize * 4)
        if kind == 0:
            m16 = net.place("m16", [P, 2, jc, RB], BF16, strip + (RAWS + 4) * csize * 4)
        S = net.S
        columns = D
    else:
        raw = net.place("raw_mask", [P, RAWS, jc, RB], BF16, strip)
        V = net.V
        columns = D + 1
    y = net.small("y", [P, TB, D], F32)
    xn = net.small("xn", [P, TB, D], F32)
    ev = xn
    stats = net.small("stats", [P, TB, 6], F32)
    mv = net.small("mv", [P, TB, 2], F32)
    sd = net.small("sd", [P, TB], F32)
    r0 = net.small("r0", [P, TB], F32)
    r1 = net.small("r1", [P, TB], F32)
    eps = net.small("eps", [P, 1], F32)
    if kind == 0:
        HT_hi = net.place("HT_hi", [P, DC, net.N], F32R, net.at["HT"])
        HT_lo = net.place("HT_lo", [P, DC, net.N], F32R, net.at["HT"] + net.NT * D * 4)
        net.HT_hi, net.HT_lo = HT_hi, HT_lo
        bias_bc = net.place("bias_bc", [P, D], F32, net.at["w"])
    else:
        xt_hi = net.place("xt_hi", [P, TB, DC, P], F32R, strip + 32 * KB)
        xt_lo = net.place("xt_lo", [P, TB, DC, P], F32R, strip + 34 * KB)
        nv, grp = (1, 1) if kind == 1 else (2, H)
        prod = y
        a_bc = net.a2_bc if kind == 1 else net.a3_bc
        out_h = net.place("Hn", [P, net.NT, D], F32, net.at["S"] + (0 if kind == 1 else net.room * D * 4))
        net.Hn = out_h
    a_t, a_p = K // 2 - 1, 3 * K // 4 - 1
    if not dense:
        a_t, a_p = K // 2 - 1, K // 2

    with ExitStack() as ctx:
        raw_ready = sems(ctx, nc, f"a{kind}", "raw0 raw1 raw2 raw3")
        mask_out = sems(ctx, nc, f"a{kind}", "mout0 mout1")
        (const_in, wgt, eps_ready, whi_ready, wlo_ready, hi_ready, lo_ready, mask_ready, pe_done, evac_done, sd_ready,
         chain, turned, xhi_ready, projected, kept, resident) = sems(
            ctx, nc, f"a{kind}",
            "const wgt eps whi wlo hi lo mask pe evac sd chain turned xhi projected kept resident")
        blk = ctx.enter_context(nc.Block())
        A1 = 1 if dense else 3
        A2 = (2 if dense else 1)
        A3 = 2 * TB + 5 + TB
        B = 1
        C = 0 if kind == 0 else 2 * nv
        E = A1 + A2 + A3 + B + C

        if dense:
            src = adj_t.rearrange("(k j p) (b r) -> b k p j r", j=jc, p=P, r=RB)
        else:
            src = mask.rearrange("(k j p) (b r) -> b k p j r", j=jc, p=P, r=RB)
        if kind == 0:
            mdst = mask.rearrange("(k j p) (b r) -> b k p j r", j=jc, p=P, r=RB)

        @blk.sync
        def _(sp):
            if kind == 0:
                sp.dma_start(bias_bc[:], bias.rearrange("(a f) -> a f", a=1).broadcast_to([P, D]))\
                    .then_inc(const_in, 16)
            else:
                sp.dma_start(xn[:], w_next.rearrange("(c p) f -> p c f", p=P)).then_inc(wgt, 16)
            per = K // RAWS if K >= RAWS else 1

            def slot(k):
                return k % RAWS

            def fill(g):
                return g // RAWS + 1

            def load(b, k):
                sp.dma_start(raw[:, slot(k)], src[b, k]).then_inc(raw_ready[slot(k)], 16)

            def store_and_load(b, k, more):
                g = b * K + k
                if kind == 0:
                    sp.wait_ge(mask_ready, g + 1)
                    sp.nop(nofuse=True)
                    sp.dma_start(mdst[b, k], m16[:, k % 2]).then_inc(mask_out[k % 2], 16)
                elif kind == 1:
                    sp.wait_ge(lo_ready, g + 1)
                else:
                    sp.wait_ge(pe_done, g + 1)
                if more:
                    if k + RAWS < K:
                        load(b, k + RAWS)
                    else:
                        load(b + 1, k + RAWS - K)

            for k in range(RAWS):
                load(0, k)
            with sp.Fori(0, nb - 1) as b:
                for k in range(K):
                    store_and_load(b, k, True)
            for k in range(K):
                store_and_load(nb - 1, k, k + RAWS < K)
            if kind == 0:
                for q in mask_out:
                    sp.wait_ge(q, 16 * (nb * K // 2))

        def taken(g_over_raws):
            return 16 * (g_over_raws + 1)

        def raw_wait(eng, b, k):
            eng.wait_ge(raw_ready[k % RAWS], (b * (K // RAWS) + k // RAWS + 1) * 16)

        @blk.gpsimd
        def _(pool):
            pool.memset(eps[:], EPS).then_inc(eps_ready, 1)

            def keep(b):
                pool.wait_ge(chain, b * E + A1 + A2 + A3)
                pool.tensor_copy(net.X[:, ds(TB * b, TB), :], xn[:]).then_inc(kept, 1)

            with pool.Fori(0, nb) as b:
                keep(b)

        @blk.scalar
        def _(act):
            if kind:
                act.wait_ge(wgt, 16)
                act.activation(net.w_hi[:], xn[:], ACT.Copy).then_inc(whi_ready, 1)
            act.wait_ge(eps_ready, 1)

            def split(b, k, first):
                raw_wait(act, b, k)
                if not first or k >= 2:
                    act.wait_ge(pe_done, b * K + k - 1)
                act.activation(hi[:, k % 2], raw[:, k % RAWS], ACT.Copy).then_inc(hi_ready, 1)

            def evacuate(b, par, first=False):
                act.wait_ge(pe_done, b * K + K)
                if not first:
                    act.wait_ge(kept, b)
                    act.wait_ge(turned, b)
                act.activation(ev[:], ps[:, TB * par:TB * par + TB, D:2 * D], ACT.Copy).then_inc(evac_done, 1)

            def deviation(b):
                act.wait_ge(chain, b * E + A1 + A2 + 2 * TB)
                act.activation(sd[:], mv[:, :, 1], ACT.Sqrt, bias=eps[:]).then_inc(sd_ready, 1)

            def turned_parts(b, first):
                act.wait_ge(turned, b + 1)
                tv = ps[:, 4].rearrange("p (t c n) -> p t c n", t=TB, c=DC)
                if kind == 0:
                    act.activation(HT_hi[:, :, ds(RB * b, RB)].rearrange("p c (t n) -> p t c n", t=TB),
                                   tv, ACT.Copy).then_inc(xhi_ready, 1)
                else:
                    if not first:
                        act.wait_ge(projected, b)
                    act.activation(xt_hi[:], tv, ACT.Copy).then_inc(xhi_ready, 1)

            def resident_h(b):
                act.wait_ge(projected, b + 1)
                act.activation(out_h[:, ds(TB * b, TB), :], ps[:, 5].rearrange("p (t f) -> p t f", t=TB),
                               ACT.Copy).then_inc(resident, 1)

            def block(b, par, first=False, before=True):
                for k in range(K):
                    if dense:
                        split(b, k, first)
                    if not before:
                        continue
                    if k == 0 and dense:
                        evacuate(b - 1, 1 - par, isinstance(b, int))
                    if k == (2 if dense else 0):
                        deviation(b - 1)
                    if k == a_t + 1:
                        turned_parts(b - 1, first)
                    if k == min(a_p + 1, K - 1) and kind:
                        resident_h(b - 1)

            block(0, 0, True, False)
            block(1, 1, False)
            with act.Fori(1, nb // 2) as bb:
                block(bb * 2, 0)
                block(bb * 2 + 1, 1)
            if dense:
                evacuate(nb - 1, 1)
            deviation(nb - 1)
            turned_parts(nb - 1, False)
            if kind:
                resident_h(nb - 1)

        @blk.vector
        def _(dve):
            if kind == 0:
                dve.wait_ge(const_in, 16)
            else:
                dve.wait_ge(whi_ready, 1)
                dve.tensor_tensor(net.w_lo[:], xn[:], net.w_hi[:].bitcast(F32), ALU.subtract)\
                    .then_inc(wlo_ready, 1)
                dve.wait_ge(wlo_ready, 1)

            def split(b, k, first):
                g = b * K + k
                dve.wait_ge(hi_ready, g + 1)
                raw_wait(dve, b, k)
                if not first or k >= 2:
                    dve.wait_ge(pe_done, g - 1)
                dve.tensor_tensor(lo[:, k % 2], raw[:, k % RAWS], hi[:, k % 2].bitcast(F32), ALU.subtract)\
                    .then_inc(lo_ready, 1)
                if kind == 0:
                    if not first or k >= 2:
                        dve.wait_ge(mask_out[k % 2], (b * (K // 2) + k // 2) * 16)
                    dve.tensor_scalar(m16[:, k % 2], raw[:, k % RAWS], 0.0, None, ALU.is_gt)\
                        .then_inc(mask_ready, 1)

            def sums(b, par):
                c = Steps(dve, chain, b * E)
                banks = ps[:, TB * par:TB * par + TB]
                dve.wait_ge(pe_done, b * K + K)
                if dense:
                    dve.wait_ge(evac_done, b + 1)
                    c.join()
                    c.step(dve.tensor_tensor(y[:], banks[:, :, 0:D], ev[:], ALU.add))
                else:
                    c.join()
                    c.step(dve.reciprocal(r0[:], banks[:, :, D]))
                    for t in range(TB):
                        c.join()
                        c.step(dve.tensor_scalar(y[:, t], banks[:, t, 0:D], r0[:, t:t + 1], 0.0,
                                                 ALU.mult, ALU.max))
                assert c.n == A1

            def residual(b):
                c = Steps(dve, chain, b * E + A1)
                tiles = net.X[:, ds(TB * b, TB), :]
                if dense:
                    c.join()
                    add = bias_bc[:, :].rearrange("p (o f) -> p o f", o=1).broadcast_to([P, TB, D]) if kind == 0 \
                        else net.NB[:, ds(TB * b, TB), :]
                    c.step(dve.tensor_tensor(y[:], y[:], add, ALU.add))
                    c.join()
                    c.step(dve.scalar_tensor_tensor(y[:], y[:], 0.0, tiles, ALU.max, ALU.add))
                else:
                    c.join()
                    c.step(dve.tensor_tensor(y[:], y[:], tiles, ALU.add))
                assert c.n == A2

            def norm(b, first):
                c = Steps(dve, chain, b * E + A1 + A2)
                c.join()
                for t in range(TB):
                    c.step(dve.bn_stats(stats[:, t], y[:, t]))
                c.join()
                dve.nop(nofuse=True)
                for t in range(TB):
                    c.step(dve.bn_aggr(mv[:, t], stats[:, t]))
                dve.wait_ge(sd_ready, b + 1)
                c.join()
                c.step(dve.reciprocal(r0[:], sd[:]))
                c.join()
                c.step(dve.tensor_tensor(r1[:], r0[:], r0[:], ALU.mult))
                c.join()
                c.step(dve.scalar_tensor_tensor(r1[:], mv[:, :, 1], eps[:], r1[:], ALU.add, ALU.mult))
                c.join()
                c.step(dve.tensor_scalar(r1[:], r1[:], -0.5, 1.5, ALU.mult, ALU.add))
                c.join()
                c.step(dve.tensor_tensor(r1[:], r1[:], r0[:], ALU.mult))
                c.join()
                if not first and not dense:
                    dve.wait_ge(kept, b)
                    dve.wait_ge(turned, b)
                for t in range(TB):
                    c.step(dve.tensor_scalar(xn[:, t], y[:, t], mv[:, t, 0:1], r1[:, t:t + 1],
                                             ALU.subtract, ALU.mult))
                assert c.n == A3

            def turned_parts(b):
                c = Steps(dve, chain, b * E + A1 + A2 + A3)
                dve.wait_ge(xhi_ready, b + 1)
                tv = ps[:, 4].rearrange("p (t c n) -> p t c n", t=TB, c=DC)
                c.join()
                if kind == 0:
                    pick = lambda m: m[:, :, ds(RB * b, RB)].rearrange("p c (t n) -> p t c n", t=TB)
                    c.step(dve.tensor_tensor(pick(HT_lo), tv, pick(HT_hi).bitcast(F32), ALU.subtract))
                else:
                    c.step(dve.tensor_tensor(xt_lo[:], tv, xt_hi[:].bitcast(F32), ALU.subtract))

            def scores(b):
                c = Steps(dve, chain, b * E + A1 + A2 + A3 + B)
                dve.wait_ge(resident, b + 1)
                hp = out_h[:, ds(TB * b, TB), :]
                for v in range(nv):
                    c.join()
                    vec = a_bc[:, v:v + 1, :].broadcast_to([P, TB, D])
                    c.step(dve.tensor_tensor(prod[:], hp, vec, ALU.mult))
                    c.join()
                    dst = net.f_dst[:, ds(TB * b, TB)] if kind == 1 else \
                        (net.s_src, net.s_dst)[v][:, ds(TB * b, TB), :].rearrange("p t h -> p (t h)")
                    c.step(dve.tensor_reduce(dst, prod[:].rearrange("p t (h f) -> p (t h) f", h=grp), AX.X, ALU.add))

            def block(b, par, first=False, before=True):
                for k in range(K):
                    if dense:
                        split(b, k, first)
                    if not before:
                        continue
                    if k == 0:
                        sums(b - 1, 1 - par)
                    if k == (1 if dense else 0):
                        residual(b - 1)
                    if k == (2 if dense else 0):
                        norm(b - 1, first is None)
                    if k == a_t + 1:
                        turned_parts(b - 1)
                    if k == min(a_p + 1, K - 1) and kind:
                        scores(b - 1)

            block(0, 0, True, False)
            block(1, 1, None if not dense else False)
            with dve.Fori(1, nb // 2) as bb:
                block(bb * 2, 0)
                block(bb * 2 + 1, 1)
            sums(nb - 1, 1)
            residual(nb - 1)
            norm(nb - 1, False)
            turned_parts(nb - 1)
            if kind:
                scores(nb - 1)

        @blk.tensor
        def _(pe):
            if kind:
                pe.wait_ge(wlo_ready, 1)

            def chunk(b, k, par, first):
                if dense:
                    pe.wait_ge(lo_ready, b * K + k + 1)
                else:
                    raw_wait(pe, b, k)
                if k == 0 and not first:
                    pe.wait_ge(chain, (b - 2) * E + A1)
                for j in range(jc):
                    jt = k * jc + j
                    go, end = jt == 0, jt == net.NT - 1
                    for t in range(TB):
                        bank = TB * par + t
                        rows = slice(t * P, t * P + P)
                        if dense:
                            if not end:
                                pe.matmul(ps[:, bank, :], hi[:, k % 2, j, rows], S[:, jt, :], start=go, stop=False)
                            last = pe.matmul(ps[:, bank, 0:D], lo[:, k % 2, j, rows], S[:, jt, 0:D],
                                             start=False, stop=False)
                            if end:
                                last = pe.matmul(ps[:, bank, :], hi[:, k % 2, j, rows], S[:, jt, :],
                                                 start=False, stop=True)
                        else:
                            for q in range(3):
                                last = pe.matmul(ps[:, bank, 0:D + 1], raw[:, k % RAWS, j, rows], V[:, jt, q, :],
                                                 start=go and q == 0, stop=end and q == 2)
                last.then_inc(pe_done, 1)

            def turn(b):
                pe.wait_ge(chain, b * E + A1 + A2 + A3)
                for t in range(TB):
                    for c in range(DC):
                        at = (t * DC + c) * P
                        last = pe.transpose(ps[:, 4, at:at + P], xn[:, t, c * P:c * P + P], net.ident[:])
                last.then_inc(turned, 1)

            def project_block(b, first):
                pe.wait_ge(chain, b * E + A1 + A2 + A3 + B)
                if not first:
                    pe.wait_ge(resident, b)
                project(pe, net, 5, xt_hi, xt_lo).then_inc(projected, 1)

            def block(b, par, first=False, before=True, second=False):
                for k in range(K):
                    chunk(b, k, par, first)
                    if not before:
                        continue
                    if k == a_t:
                        turn(b - 1)
                    if k == a_p and kind:
                        project_block(b - 1, second)

            block(0, 0, True, False)
            block(1, 1, True, True, True)
            with pe.Fori(1, nb // 2) as bb:
                block(bb * 2, 0)
                block(bb * 2 + 1, 1)
            turn(nb - 1)
            if kind:
                project_block(nb - 1, False)


def stage_quadratic(net, w1, w1_t, w2, b1):
    nc, ps, nt = net.nc, net.ps, net.NT
    net.end = net.scratch
    acc = net.place("acc", [P, nt, D], F32, net.at["S"])
    NB = net.place("NB", [P, nt, D], F32, net.at["S"] + net.room * D * 4)
    net.NB, net.acc = NB, acc
    strip = net.at["strip"]
    sz = DC * 2 * D * 4
    raw = net.place("w2raw", [P, 2, DC, 2, D], F32, strip)
    whi = net.place("w2hi", [P, 2, DC, 2 * D], F32R, strip + 2 * sz)
    wlo = net.place("w2lo", [P, 2, DC, 2 * D], F32R, strip + 4 * sz)
    node = net.small("node", [P, nt, KQ], F32)
    C1 = KQ + D
    first_raw = net.place("w1raw", [P, DC, C1], F32, strip + 6 * sz)
    first_hi = net.place("w1hi", [P, DC, C1], F32R, strip + 7 * sz + 512)
    first_lo = net.place("w1lo", [P, DC, C1], F32R, strip + 7 * sz + 512 + DC * C1 * 4)
    assert strip + 7 * sz + 512 + 2 * DC * C1 * 4 <= net.at["small"]
    w1t_sb = net.place("w1t", [KQ, D], F32, net.at["w"])
    b1_sb = net.place("b1", [KQ, D], F32, net.at["w"] + D * 4)
    pairs = KQ // 2
    PF = 2 * DC * 3
    with ExitStack() as ctx:
        raw_ready = sems(ctx, nc, "q", "raw0 raw1")
        (w1_in, wb_in, wb, wb_sb, f_hi, f_lo, zeroed, hi_ready, lo_ready, nodes, node_done, nb_done, mm, chain) = sems(
            ctx, nc, "q", "w1 wb wbm wbs fhi flo zero hi lo nodes noded nbd mm chain")
        blk = ctx.enter_context(nc.Block())
        HT_hi, HT_lo = net.HT_hi, net.HT_lo
        w2v = w2.rearrange("(q k) (c p) f -> q p c k f", k=2, p=P)

        @blk.sync
        def _(sp):
            sp.dma_start(w1t_sb[:], w1_t).then_inc(wb_in, 16)
            sp.dma_start(b1_sb[:], b1).then_inc(wb_in, 16)
            sp.dma_start(first_raw[:, :, 0:KQ], w1.rearrange("(c p) k -> p c k", p=P)).then_inc(w1_in, 16)

            def load(q, par):
                for k in range(2):
                    sp.dma_start(raw[:, par, :, k], w2v[q, :, :, k]).then_inc(raw_ready[par], 16)

            load(0, 0)
            load(1, 1)
            with sp.Fori(1, pairs // 2) as qq:
                for par in range(2):
                    q = qq * 2 + par
                    sp.wait_ge(lo_ready, q - 1)
                    load(q, par)

        @blk.gpsimd
        def _(pool):
            pool.memset(acc[:], 0.0).then_inc(zeroed, 1)

        @blk.scalar
        def _(act):
            act.wait_ge(wb, 1)
            act.activation(first_raw[:, :, KQ:C1], ps[:, 0, :].rearrange("p (c f) -> p c f", c=DC), ACT.Copy)\
                .then_inc(wb_sb, 1)
            act.wait_ge(w1_in, 16)
            act.wait_ge(wb_sb, 1)
            act.activation(first_hi[:], first_raw[:], ACT.Copy).then_inc(f_hi, 1)

            def split(q, par, first):
                act.wait_ge(raw_ready[par], (q - par) * 16 + 32)
                if not first:
                    act.wait_ge(mm, (q - 1) * nt)
                act.activation(whi[:, par].rearrange("p c (k f) -> p c k f", k=2), raw[:, par], ACT.Copy)\
                    .then_inc(hi_ready, 1)

            split(0, 0, True)
            split(1, 1, True)
            for n in range(nt):
                act.wait_ge(node_done, n + 1)
                act.activation(NB[:, n], ps[:, n % 8, KQ:C1], ACT.Copy).then_inc(nb_done, 1)
            with act.Fori(1, pairs // 2) as qq:
                for par in range(2):
                    split(qq * 2 + par, par, False)

        @blk.vector
        def _(dve):
            dve.wait_ge(f_hi, 1)
            dve.tensor_tensor(first_lo[:], first_raw[:], first_hi[:].bitcast(F32), ALU.subtract).then_inc(f_lo, 1)
            for par in range(2):
                dve.wait_ge(hi_ready, par + 1)
                dve.tensor_tensor(wlo[:, par].rearrange("p c (k f) -> p c k f", k=2), raw[:, par],
                                  whi[:, par].rearrange("p c (k f) -> p c k f", k=2).bitcast(F32),
                                  ALU.subtract).then_inc(lo_ready, 1)
            for n in range(nt):
                dve.wait_ge(nodes, n + 1)
                dve.tensor_copy(node[:, n], ps[:, n % 8, 0:KQ]).then_inc(node_done, 1)
            dve.wait_ge(zeroed, 1)
            dve.wait_ge(node_done, nt)

            def weigh(q, n, k):
                dve.scalar_tensor_tensor(acc[:, n], ps[:, n % 8, k * D:(k + 1) * D], node[:, n, ds(2 * q + k, 1)],
                                         acc[:, n], ALU.mult, ALU.add).then_inc(chain, 1)

            def split(q, par):
                dve.wait_ge(hi_ready, q + 1)
                dve.tensor_tensor(wlo[:, par].rearrange("p c (k f) -> p c k f", k=2), raw[:, par],
                                  whi[:, par].rearrange("p c (k f) -> p c k f", k=2).bitcast(F32),
                                  ALU.subtract).then_inc(lo_ready, 1)

            def weigh_all(q, par):
                base = q * nt * 2
                for n in range(nt):
                    if n == 2 and par is not None:
                        split(q + 1, par)
                    dve.wait_ge(mm, q * nt + n + 1)
                    if n or not isinstance(q, int) or q:
                        dve.wait_ge(chain, base + 2 * n)
                    weigh(q, n, 0)
                    dve.wait_ge(chain, base + 2 * n + 1)
                    weigh(q, n, 1)

            weigh_all(0, None)
            with dve.Fori(0, (pairs - 2) // 2) as qq:
                weigh_all(qq * 2 + 1, 0)
                weigh_all(qq * 2 + 2, 1)
            weigh_all(pairs - 1, None)

        @blk.tensor
        def _(pe):
            pe.wait_ge(wb_in, 32)
            for c in range(DC):
                last = pe.matmul(ps[:, 0, c * D:(c + 1) * D], w1t_sb[:, c * P:(c + 1) * P], b1_sb[:],
                                 start=True, stop=True)
            last.then_inc(wb, 1)
            pe.wait_ge(f_lo, 1)
            for n in range(nt):
                if n >= 8:
                    pe.wait_ge(nb_done, n - 7)
                m = 0
                for c in range(DC):
                    cols = slice(n * P, n * P + P)
                    for a, w in ((HT_hi, first_hi), (HT_hi, first_lo), (HT_lo, first_hi)):
                        last = pe.matmul(ps[:, n % 8, 0:C1], a[:, c, cols], w[:, c], start=(m == 0), stop=(m == 5))
                        m += 1
                last.then_inc(nodes, 1)

            def pair(q, par, first):
                pe.wait_ge(lo_ready, q + 1)
                for n in range(nt):
                    if first and n < 8:
                        pe.wait_ge(nb_done, nt - 8 + n + 1)
                    else:
                        pe.wait_ge(chain, (q * nt + n - 7) * 2)
                    m = 0
                    for c in range(DC):
                        cols = slice(n * P, n * P + P)
                        for a, w in ((HT_hi, whi), (HT_hi, wlo), (HT_lo, whi)):
                            last = pe.matmul(ps[:, n % 8, :], a[:, c, cols], w[:, par, c], start=(m == 0),
                                             stop=(m == 5))
                            m += 1
                    last.then_inc(mm, 1)

            pair(0, 0, True)
            pair(1, 1, False)
            with pe.Fori(1, pairs // 2) as qq:
                pair(qq * 2, 0, False)
                pair(qq * 2 + 1, 1, False)


def stage_split(net, w_a_t, a2):
    nc, ps, nt = net.nc, net.ps, net.NT
    net.end = net.scratch
    S = net.place("S1", [P, nt, 2 * D], F32R, net.at["HT"])
    net.S = S
    wat = net.place("wat", [2, D], F32, net.at["strip"])
    a_col = net.place("a_col", [2, 1], F32, net.at["strip"] + KB)
    ones = net.place("ones2", [2, P], F32, net.at["strip"] + 2 * KB)
    a_rep = net.place("a_rep", [2, P], F32, net.at["strip"] + 3 * KB)
    half = nt // 2
    with ExitStack() as ctx:
        v_in, hi_done, lo_done, ones_ready, rep, vec, vdone = sems(ctx, nc, "s", "vin hi lo ones rep vec vdone")
        blk = ctx.enter_context(nc.Block())

        @blk.sync
        def _(sp):
            sp.dma_start(wat[:], w_a_t).then_inc(v_in, 16)
            sp.dma_start(a_col[:], a2).then_inc(v_in, 16)

        @blk.scalar
        def _(act):
            for h in range(2):
                act.activation(S[:, h * half:(h + 1) * half, 0:D], net.acc[:, h * half:(h + 1) * half], ACT.Copy)\
                    .then_inc(hi_done, 1)

        @blk.vector
        def _(dve):
            dve.memset(ones[:], 1.0).then_inc(ones_ready, 1)
            dve.wait_ge(v_in, 32)
            dve.wait_ge(ones_ready, 1)
            dve.tensor_scalar(a_rep[:], ones[:], a_col[:], None, ALU.mult).then_inc(rep, 1)
            dve.wait_ge(vec, 1)
            dve.tensor_copy(net.a2_bc[:, 0, :], ps[:, 0, 0:D]).then_inc(vdone, 1)
            for h in range(2):
                dve.wait_ge(hi_done, h + 1)
                part = slice(h * half, (h + 1) * half)
                dve.tensor_tensor(S[:, part, D:2 * D], net.acc[:, part], S[:, part, 0:D].bitcast(F32),
                                  ALU.subtract).then_inc(lo_done, 1)

        @blk.tensor
        def _(pe):
            pe.wait_ge(rep, 1)
            pe.matmul(ps[:, 0, 0:D], a_rep[:], wat[:], start=True, stop=True).then_inc(vec, 1)


def stage_values2(net, a3_src, a3_dst):
    nc, nt = net.nc, net.NT
    net.end = net.scratch
    Hn = net.Hn
    V = net.place("V2", [P, nt, 3, D + 1], BF16, net.at["HT"])
    net.V = V
    net.a3_bc = net.place("a3_bc", [P, 2, D], F32, net.at["strip"] + 28 * KB)
    fm = net.small("fm", [P, 1], F32)
    fM = net.small("fM", [P, 1], F32)
    nf = net.small("nf", [P, 1], F32)
    e = net.small("e", [P, nt], F32)
    G = 4
    v32 = net.place("v32", [P, 2, G, D + 1], F32, net.at["strip"])
    v32b = net.place("v32b", [P, 2, G, D + 1], F32, net.at["strip"] + 2 * G * (D + 1) * 4)
    with ExitStack() as ctx:
        a_in, m1, m2, m3, e_done, chain, hi_done, mid_done = sems(ctx, nc, "v2", "a m1 m2 m3 e chain hi mid")
        blk = ctx.enter_context(nc.Block())

        @blk.gpsimd
        def _(pool):
            pool.wait_ge(m1, 1)
            pool.partition_all_reduce(fM[:], fm[:], P, RMAX).then_inc(m2, 1)

        @blk.sync
        def _(sp):
            for v, a in enumerate((a3_src, a3_dst)):
                sp.dma_start(net.a3_bc[:, v], a.rearrange("(o f) -> o f", o=1).broadcast_to([P, D])).then_inc(a_in, 16)
            sp.wait_ge(a_in, 32)

        @blk.scalar
        def _(act):
            act.wait_ge(m3, 1)
            act.activation(e[:], net.f_dst[:], ACT.Exp, bias=nf[:]).then_inc(e_done, 1)
            for g in range(nt // G):
                part = slice(g * G, (g + 1) * G)
                act.wait_ge(chain, (g + 1) * (G + 1))
                act.activation(V[:, part, 0], v32[:, g % 2], ACT.Copy).then_inc(hi_done, 1)
                act.wait_ge(mid_done, 2 * g + 1)
                act.activation(V[:, part, 1], v32b[:, g % 2], ACT.Copy).then_inc(hi_done, 1)

        @blk.vector
        def _(dve):
            dve.reduce_max(fm[:], net.f_dst[:], AX.X).then_inc(m1, 1)
            dve.wait_ge(m2, 1)
            dve.tensor_scalar(nf[:], fM[:], -1.0, LIFT2, ALU.mult, ALU.add).then_inc(m3, 1)
            dve.wait_ge(e_done, 1)
            n = 0
            for g in range(nt // G):
                part = slice(g * G, (g + 1) * G)
                if g >= 2:
                    dve.wait_ge(mid_done, 2 * g - 2)
                for t in range(G):
                    dve.tensor_scalar(v32[:, g % 2, t, 0:D], Hn[:, g * G + t], e[:, g * G + t:g * G + t + 1], None,
                                      ALU.mult).then_inc(chain, 1)
                dve.tensor_copy(v32[:, g % 2, :, D], e[:, part]).then_inc(chain, 1)
                n += G + 1
                dve.wait_ge(hi_done, 2 * g + 1)
                dve.wait_ge(chain, n)
                dve.tensor_tensor(v32b[:, g % 2], v32[:, g % 2], V[:, part, 0], ALU.subtract).then_inc(mid_done, 1)
                dve.wait_ge(hi_done, 2 * g + 2)
                dve.wait_ge(mid_done, 2 * g + 1)
                dve.tensor_tensor(V[:, part, 2], v32b[:, g % 2], V[:, part, 1], ALU.subtract).then_inc(mid_done, 1)



def stage_values3(net, s_rows):
    nc, nt = net.nc, net.NT
    net.end = net.scratch
    Wh = net.Hn
    V_pos = net.place("V_pos", [P, H, nt, 3, FH], BF16, net.at["HT"])
    V_neg = net.place("V_neg", [P, H, nt, 2, FH], F16, net.at["HT"] + H * nt * 3 * FH * 2)
    net.V_pos, net.V_neg = V_pos, V_neg
    net.v_end = net.at["HT"] + H * nt * 5 * FH * 2
    net.alpha = net.small("alpha", [P, nt, H], F32)
    net.beta = net.small("beta", [P, nt, H], F32)
    net.s_big = net.small("s_big", [P, nt, H], F32)
    net.scratch = net.end
    mx = net.small("mx", [P, H], F32)
    MX = net.small("MX", [P, H], F32)
    lift = net.small("lift", [P, 1], F32)
    unlift = net.small("unlift", [P, 1], F32)
    d, t0, t1, ep, en = (net.place(name, [P, nt, H], F32, net.at["S"] + 16 * KB + n * nt * H * 4)
                         for n, name in enumerate(("d", "t0", "t1", "ep", "en")))
    G = 2
    at = net.at["S"]
    v32 = net.place("v32p", [P, 2, G, H, FH], F32, at)
    v32n = net.place("v32n", [P, 2, G, H, FH], F32, at + 2 * G * H * FH * 4)
    rest = net.place("restp", [P, 2, G, H, FH], F32, at + 4 * G * H * FH * 4)
    rows = net.place("rows", [P, P], F32, at + 6 * G * H * FH * 4)
    R = nt * H
    with ExitStack() as ctx:
        (x_out, lifts, mx_done, MX_done, d_done, exps, chain, hi_done, mid_done, turned, rows_ready, rows_out,
         last_done) = sems(ctx, nc, "v3", "x lift mx MX d exp chain hi mid turned rows rout last")
        blk = ctx.enter_context(nc.Block())

        @blk.sync
        def _(sp):
            sp.dma_start(net.xres.rearrange("(t p) f -> p t f", p=P), net.X[:]).then_inc(x_out, 16)
            sp.wait_ge(rows_ready, 1)
            sp.dma_start(s_rows.rearrange("h (t p) -> t h p", p=P), rows[0:R, :]).then_inc(rows_out, 16)
            sp.wait_ge(x_out, 16)
            sp.wait_ge(rows_out, 16)

        @blk.gpsimd
        def _(pool):
            pool.memset(lift[:], LIFT3).then_inc(lifts, 1)
            pool.memset(unlift[:], -LIFT3).then_inc(lifts, 1)
            pool.wait_ge(mx_done, 1)
            pool.partition_all_reduce(MX[:], mx[:], P, RMAX).then_inc(MX_done, 1)

        @blk.tensor
        def _(pe):
            pe.transpose(net.ps[0:R, 0, 0:P], net.s_src[:].rearrange("p t h -> p (t h)"), net.ident[:])\
                .then_inc(turned, 1)

        @blk.scalar
        def _(act):
            act.wait_ge(turned, 1)
            act.activation(rows[0:R, :], net.ps[0:R, 0, 0:P], ACT.Copy).then_inc(rows_ready, 1)
            act.wait_ge(lifts, 2)
            act.wait_ge(d_done, 4)
            act.activation(ep[:], d[:], ACT.Exp).then_inc(exps, 1)
            act.activation(en[:], d[:], ACT.Exp, bias=lift[:], scale=SLOPE).then_inc(exps, 1)
            act.activation(net.alpha[:], t0[:], ACT.Exp, scale=1.0 - SLOPE).then_inc(exps, 1)
            act.activation(net.beta[:], t1[:], ACT.Exp, bias=unlift[:], scale=SLOPE - 1.0).then_inc(exps, 1)
            for g in range(nt // G):
                part = slice(g * G, (g + 1) * G)
                split = lambda v, q: v[:, :, part, q, :].rearrange("p h t f -> p t h f")
                act.wait_ge(chain, 4 * (g + 1))
                act.activation(split(V_pos, 0), v32[:, g % 2], ACT.Copy).then_inc(hi_done, 1)
                act.activation(split(V_neg, 0), v32n[:, g % 2], ACT.Copy).then_inc(hi_done, 1)
                act.wait_ge(mid_done, g + 1)
                act.activation(split(V_pos, 1), rest[:, g % 2], ACT.Copy).then_inc(hi_done, 1)

        @blk.vector
        def _(dve):
            dve.reduce_max(mx[:], net.s_dst[:].rearrange("p t h -> p h t"), AX.X).then_inc(mx_done, 1)
            dve.tensor_scalar(net.s_big[:], net.s_dst[:], BIG, None, ALU.mult)
            dve.wait_ge(MX_done, 1)
            top = MX[:].rearrange("p (o h) -> p o h", o=1).broadcast_to([P, nt, H])
            dve.tensor_tensor(d[:], net.s_dst[:], top, ALU.subtract).then_inc(d_done, 1)
            dve.tensor_tensor(t0[:], net.s_src[:], top, ALU.add).then_inc(d_done, 1)
            dve.wait_ge(d_done, 2)
            dve.tensor_scalar(t1[:], t0[:], 0.0, None, ALU.max).then_inc(d_done, 1)
            dve.wait_ge(d_done, 3)
            dve.tensor_scalar(t0[:], t0[:], 0.0, None, ALU.min).then_inc(d_done, 1)
            dve.wait_ge(exps, 4)
            wv = Wh[:].rearrange("p t (h f) -> p t h f", h=H)
            for g in range(nt // G):
                part = slice(g * G, (g + 1) * G)
                split = lambda v, q: v[:, :, part, q, :].rearrange("p h t f -> p t h f")
                wide = lambda m: m[:, part].rearrange("p t (h o) -> p t h o", o=1).broadcast_to([P, G, H, FO])
                if g >= 2:
                    dve.wait_ge(last_done, 2 * (g - 1))
                dve.tensor_tensor(v32[:, g % 2, :, :, 0:FO], wv[:, part], wide(ep), ALU.mult).then_inc(chain, 1)
                dve.tensor_copy(v32[:, g % 2, :, :, FO], ep[:, part]).then_inc(chain, 1)
                dve.tensor_tensor(v32n[:, g % 2, :, :, 0:FO], wv[:, part], wide(en), ALU.mult).then_inc(chain, 1)
                dve.tensor_copy(v32n[:, g % 2, :, :, FO], en[:, part]).then_inc(chain, 1)
                dve.wait_ge(chain, 4 * (g + 1))
                dve.wait_ge(hi_done, 3 * g + 1)
                dve.tensor_tensor(rest[:, g % 2], v32[:, g % 2], split(V_pos, 0), ALU.subtract).then_inc(mid_done, 1)
                dve.wait_ge(hi_done, 3 * g + 2)
                dve.tensor_tensor(split(V_neg, 1), v32n[:, g % 2], split(V_neg, 0), ALU.subtract).then_inc(last_done, 1)
                dve.wait_ge(hi_done, 3 * g + 3)
                dve.wait_ge(mid_done, g + 1)
                dve.tensor_tensor(split(V_pos, 2), rest[:, g % 2], split(V_pos, 1), ALU.subtract)\
                    .then_inc(last_done, 1)


def stage_attend(net, mask, s_rows, out):
    nc, nt, ps = net.nc, net.NT, net.ps
    net.end = net.scratch
    nib = net.N // IB
    CJ = 2
    nck = nt // CJ
    at = net.at["X"]
    csz = 2 * CJ * IB * 2
    step = net.place("step", [P, 2, CJ, IB], BF16, at)
    m_pos = net.place("m_pos", [P, 2, CJ, IB], BF16, at + csz)
    m_neg = net.place("m_neg", [P, 2, CJ, IB], BF16, at + 2 * csz)
    xblk = net.place("xblk", [P, IT, D], F32, at + 3 * csz)
    M = net.place("M", [P, nt, IB], BF16, net.at["S"])
    s_bc = net.place("s_bc", [P, 2, IB], F32, net.v_end)
    o_acc = net.place("o_acc", [P, IT, D], F32, net.v_end + 2 * IB * 4)
    assert at + 3 * csz + IT * D * 4 <= net.at["S"]
    assert net.v_end + 2 * IB * 4 + IT * D * 4 <= net.at["small"]
    u_pos = net.place("u_pos", [P, IT, FH], F32, net.at["w"])
    u_neg = net.place("u_neg", [P, IT, FH], F32, net.at["w"] + IT * FH * 4)
    rs = net.small("rs", [P, IT], F32)
    stats = net.small("stats3", [P, IT, 6], F32)
    mv = net.small("mv3", [P, IT, 2], F32)
    sd = net.small("sd3", [P, IT], F32)
    r1 = net.small("r13", [P, IT], F32)
    eps = net.small("eps3", [P, 1], F32)
    V_pos, V_neg = net.V_pos, net.V_neg
    with ExitStack() as ctx:
        m_in = [ctx.enter_context(nc.semaphore(f"t_m{i}")) for i in range(nck)]
        s_in = sems(ctx, nc, "t", "s0 s1")
        (x_in, eps_ready, step_ready, pos_ready, neg_ready, pe_done, chain, joined, sd_ready, o_out) = sems(
            ctx, nc, "t", "x eps step pos neg pe chain joined sd oout")
        blk = ctx.enter_context(nc.Block())
        EV = 2 * 2 + 2
        LN = IT + IT + 5 + IT
        EB = H * EV + LN
        mv_d = mask.rearrange("(k j p) (b r) -> b k p j r", j=CJ, p=P, r=IB)
        sr_d = s_rows.rearrange("h (b r) -> b h r", r=IB)
        x_d = net.xres.rearrange("(b t p) f -> b p t f", t=IT, p=P)
        o_d = out.rearrange("(b t p) f -> b p t f", t=IT, p=P)

        @blk.sync
        def _(sp):
            def load_mask(b, k):
                sp.dma_start(M[:, k * CJ:(k + 1) * CJ], mv_d[b, k]).then_inc(m_in[k], 16)

            def load_s(b, h):
                sp.dma_start(s_bc[:, h % 2], sr_d[b, h:h + 1].broadcast_to([P, IB])).then_inc(s_in[h % 2], 16)

            def load_x(b):
                sp.dma_start(xblk[:], x_d[b]).then_inc(x_in, 16)

            def rows(b, more):
                for h in range(2, H):
                    sp.wait_ge(step_ready, (b * H + h - 1) * nck)
                    load_s(b, h)
                if more:
                    for h in range(2):
                        sp.wait_ge(step_ready, (b * H + h + 3) * nck)
                        load_s(b + 1, h)
                    for k in range(nck):
                        sp.wait_ge(neg_ready, (b * H + H - 1) * nck + k + 1)
                        sp.nop(nofuse=True)
                        load_mask(b + 1, k)
                sp.wait_ge(chain, (b + 1) * EB)
                sp.dma_start(o_d[b], o_acc[:]).then_inc(o_out, 16)
                if more:
                    load_x(b + 1)

            load_s(0, 0)
            load_s(0, 1)
            for k in range(nck):
                load_mask(0, k)
            load_x(0)
            if nib > 1:
                with sp.Fori(0, nib - 1) as b:
                    rows(b, True)
            rows(nib - 1, False)
            sp.wait_ge(o_out, 16 * nib)

        @blk.scalar
        def _(act):
            act.wait_ge(eps_ready, 1)

            def steps(b, h, k, par, first):
                g = (b * H + h) * nck + k
                if not first:
                    act.wait_ge(pos_ready, g - 1)
                for j in range(CJ):
                    last = act.activation(step[:, par, j], s_bc[:, h % 2], ACT.Sigmoid,
                                          bias=net.s_big[:, ds(k * CJ + j, 1), h], scale=BIG)
                last.then_inc(step_ready, 1)

            def head(b, h, first):
                act.wait_ge(s_in[h % 2], (b * (H // 2) + h // 2 + 1) * 16)
                steps(b, h, 0, 0, first)
                steps(b, h, 1, 1, first)
                steps(b, h, 2, 0, False)
                steps(b, h, 3, 1, False)
                if h == 0 and not first:
                    deviation(b - 1)
                if nck > 4:
                    with act.Fori(2, nck // 2) as kk:
                        steps(b, h, kk * 2, 0, False)
                        steps(b, h, kk * 2 + 1, 1, False)

            def deviation(b):
                act.wait_ge(chain, b * EB + H * EV + 2 * IT)
                act.activation(sd[:], mv[:, :, 1], ACT.Sqrt, bias=eps[:]).then_inc(sd_ready, 1)

            head(0, 0, True)
            for h in range(1, H):
                head(0, h, False)
            if nib > 1:
                with act.Fori(1, nib) as b:
                    for h in range(H):
                        head(b, h, False)
            deviation(nib - 1)

        @blk.gpsimd
        def _(pool):
            pool.memset(eps[:], EPS).then_inc(eps_ready, 1)

            def join(b, h):
                u = b * H + h
                pool.wait_ge(chain, b * EB + h * EV + 4)
                fac = lambda m: m[:, ds(b * IT, IT), h:h + 1].broadcast_to([P, IT, FH])
                pool.tensor_tensor(u_pos[:], u_pos[:], fac(net.alpha), ALU.mult).then_inc(joined, 1)
                pool.tensor_tensor(u_neg[:], u_neg[:], fac(net.beta), ALU.mult).then_inc(joined, 1)
                pool.wait_ge(joined, u * 3 + 2)
                pool.tensor_tensor(u_pos[:], u_pos[:], u_neg[:], ALU.add).then_inc(joined, 1)

            with pool.Fori(0, nib) as b:
                for h in range(H):
                    join(b, h)

        @blk.vector
        def _(dve):
            def cut(b, h, k, kc, par, first):
                g = (b * H + h) * nck + k
                dve.wait_ge(step_ready, g + 1)
                if not first:
                    dve.wait_ge(pe_done, g - 1)
                mk = M[:, ds(k * CJ, CJ)] if not isinstance(k, int) else M[:, k * CJ:(k + 1) * CJ]
                dve.tensor_tensor(m_pos[:, par], step[:, par], mk, ALU.mult).then_inc(pos_ready, 1)
                dve.wait_ge(pos_ready, g + 1)
                dve.tensor_tensor(m_neg[:, par], mk, m_pos[:, par], ALU.subtract).then_inc(neg_ready, 1)

            def leave(b, h):
                c = Steps(dve, chain, b * EB + h * EV)
                dve.wait_ge(pe_done, (b * H + h + 1) * nck)
                c.join()
                hb = IT // 2
                for half in range(2):
                    bk = ps[:, half * hb:(half + 1) * hb]
                    c.step(dve.tensor_reduce(u_pos[:, half * hb:(half + 1) * hb],
                                             bk[:, :, 0:3 * FH].rearrange("p t (q f) -> p t f q", q=3), AX.X, ALU.add))
                    c.step(dve.tensor_reduce(u_neg[:, half * hb:(half + 1) * hb],
                                             bk[:, :, 3 * FH:5 * FH].rearrange("p t (q f) -> p t f q", q=2), AX.X,
                                             ALU.add))

            def divide(b, h):
                c = Steps(dve, chain, b * EB + h * EV + 4)
                dve.wait_ge(joined, (b * H + h) * 3 + 3)
                c.join()
                c.step(dve.reciprocal(rs[:], u_pos[:, :, FO]))
                c.join()
                if h == 0:
                    if isinstance(b, int):
                        if b > 0:
                            dve.wait_ge(o_out, 16 * b)
                    else:
                        dve.wait_ge(o_out, b * 16)
                c.step(dve.tensor_tensor(o_acc[:, :, h * FO:(h + 1) * FO], u_pos[:, :, 0:FO],
                                         rs[:].rearrange("p (t o) -> p t o", o=1).broadcast_to([P, IT, FO]),
                                         ALU.mult))

            def norm(b):
                c = Steps(dve, chain, b * EB + H * EV)
                dve.wait_ge(x_in, (b + 1) * 16)
                c.join()
                last = dve.tensor_tensor(xblk[:], o_acc[:], xblk[:], ALU.add)
                c.step(last)
                c.join()
                for t in range(IT):
                    s = dve.bn_stats(stats[:, t], xblk[:, t])
                    if t:
                        c.step(s)
                c.join()
                dve.nop(nofuse=True)
                for t in range(IT):
                    c.step(dve.bn_aggr(mv[:, t], stats[:, t]))
                dve.wait_ge(sd_ready, b + 1)
                c.join()
                c.step(dve.reciprocal(rs[:], sd[:]))
                c.join()
                c.step(dve.tensor_tensor(r1[:], rs[:], rs[:], ALU.mult))
                c.join()
                c.step(dve.scalar_tensor_tensor(r1[:], mv[:, :, 1], eps[:], r1[:], ALU.add, ALU.mult))
                c.join()
                c.step(dve.tensor_scalar(r1[:], r1[:], -0.5, 1.5, ALU.mult, ALU.add))
                c.join()
                c.step(dve.tensor_tensor(r1[:], r1[:], rs[:], ALU.mult))
                c.join()
                for t in range(IT):
                    c.step(dve.tensor_scalar(o_acc[:, t], xblk[:, t], mv[:, t, 0:1], r1[:, t:t + 1],
                                             ALU.subtract, ALU.mult))
                assert c.n == LN

            def head(b, h, first, masks):
                if masks:
                    for k in range(nck):
                        dve.wait_ge(m_in[k], (b + 1) * 16)
                cut(b, h, 0, 0, 0, first)
                if not first:
                    leave(*((b, h - 1) if h else (b - 1, H - 1)))
                cut(b, h, 1, 1, 1, first)
                with dve.Fori(1, 2) as kk:
                    cut(b, h, kk * 2, 0, 0, False)
                    cut(b, h, kk * 2 + 1, 0, 1, False)
                if not first:
                    divide(*((b, h - 1) if h else (b - 1, H - 1)))
                    if h == 0:
                        norm(b - 1)
                if nck > 4:
                    with dve.Fori(2, nck // 2) as kk:
                        cut(b, h, kk * 2, 0, 0, False)
                        cut(b, h, kk * 2 + 1, 0, 1, False)

            for h in range(H):
                head(0, h, h == 0, h == 0)
            if nib > 1:
                with dve.Fori(1, nib) as b:
                    for h in range(H):
                        head(b, h, False, h == 0)
            leave(nib - 1, H - 1)
            divide(nib - 1, H - 1)
            norm(nib - 1)

        @blk.tensor
        def _(pe):
            def chunk(b, h, k, par, start, end, first):
                g = (b * H + h) * nck + k
                pe.wait_ge(neg_ready, g + 1)
                for j in range(CJ):
                    jt = k * CJ + j
                    at_jt = ds(jt, 1)
                    vp = V_pos[:, h, at_jt].rearrange("p o q f -> p (o q f)")
                    vn = V_neg[:, h, at_jt].rearrange("p o q f -> p (o q f)")
                    for t in range(IT):
                        if start and j == 0 and not first and t in (0, IT // 2):
                            lb, lh = (b, h - 1) if h else (b - 1, H - 1)
                            pe.wait_ge(chain, lb * EB + lh * EV + (2 if t == 0 else 4))
                        rows = slice(t * P, t * P + P)
                        go = start and j == 0
                        stop = end and j == CJ - 1
                        pe.matmul(ps[:, t, 0:3 * FH], m_pos[:, par, j, rows], vp, start=go, stop=stop)
                        last = pe.matmul(ps[:, t, 3 * FH:5 * FH], m_neg[:, par, j, rows], vn, start=False,
                                         stop=stop, skip_group_check=True)
                last.then_inc(pe_done, 1)

            def head(b, h, first):
                chunk(b, h, 0, 0, True, False, first)
                chunk(b, h, 1, 1, False, False, first)
                if nck > 4:
                    with pe.Fori(1, nck // 2 - 1) as kk:
                        chunk(b, h, kk * 2, 0, False, False, False)
                        chunk(b, h, kk * 2 + 1, 1, False, False, False)
                chunk(b, h, nck - 2, 0, False, False, False)
                chunk(b, h, nck - 1, 1, False, True, False)

            for h in range(H):
                head(0, h, h == 0)
            if nib > 1:
                with pe.Fori(1, nib) as b:
                    for h in range(H):
                        head(b, h, False)


def network(nc, x, adj_t, w0, b0, w1, w1_t, w2, b1, w_gat, w_a_t, a_dst2, w_heads, a3_src, a3_dst, out, upto=9):
    n = x.shape[0]
    net = Net(nc, n)
    mask = nc.dram_tensor("mask", [n, n], BF16).ap()
    net.xres = nc.dram_tensor("xres", [n, D], F32).ap()
    s_rows = nc.dram_tensor("s_rows", [H, n], F32).ap()
    stage_project0(net, x, w0)
    stage_aggregate(net, 0, adj_t, mask, None, None, b0)
    if upto > 0:
        stage_quadratic(net, w1, w1_t, w2, b1)
        stage_split(net, w_a_t, a_dst2)
        stage_aggregate(net, 1, adj_t, None, w_gat, None, None)
    if upto > 1:
        stage_values2(net, a3_src, a3_dst)
        stage_aggregate(net, 2, None, mask, w_heads, None, None)
    if upto > 2:
        stage_values3(net, s_rows)
        stage_attend(net, mask, s_rows, out)
    return net


def kernel(x, adj, L0_gnn_W, L0_gnn_b, L1_gnn_W1, L1_gnn_W2, L1_gnn_b, L2_gnn_w, L2_gnn_w_a, L2_gnn_a,
           L3_gnn_W, L3_gnn_a):
    import numpy as _np
    import concourse.bacc as _bacc
    from concourse import mybir as _mybir
    from concourse.bass_utils import run_bass_kernel_spmd as _run

    heads, _, fo = L3_gnn_W.shape
    laid = {
        "x": x,
        "adj_t": _np.transpose(adj),
        "w0": L0_gnn_W,
        "b0": L0_gnn_b,
        "w1": L1_gnn_W1,
        "w1_t": _np.transpose(L1_gnn_W1),
        "w2": L1_gnn_W2,
        "b1": L1_gnn_b,
        "w_gat": L2_gnn_w,
        "w_a_t": _np.transpose(L2_gnn_w_a),
        "a_dst2": L2_gnn_a[L2_gnn_a.shape[0] // 2:],
        "w_heads": _np.transpose(L3_gnn_W, (1, 0, 2)).reshape(-1, heads * fo),
        "a3_src": L3_gnn_a[:, :fo, 0].reshape(-1),
        "a3_dst": L3_gnn_a[:, fo:, 0].reshape(-1),
    }
    nc = _bacc.Bacc("TRN2", target_bir_lowering=False, num_devices=1)
    arrays, args = {}, []
    for name, a in laid.items():
        a = _np.ascontiguousarray(a)
        arrays[f"in_{name}"] = a
        args.append(nc.dram_tensor(f"in_{name}", a.shape, _mybir.dt.from_np(a.dtype), kind="ExternalInput").ap())
    args.append(nc.dram_tensor("out_0", x.shape, _mybir.dt.from_np(_np.dtype("float32")), kind="ExternalOutput").ap())
    network(nc, *args)
    return _run(nc, [arrays], core_ids=[0]).results[0]["out_0"]
```

```python
from contextlib import ExitStack

import concourse.bass as bass
from concourse import mybir

F32 = mybir.dt.float32
F32R = mybir.dt.float32r
BF16 = mybir.dt.bfloat16
F16 = mybir.dt.float16
I32 = mybir.dt.int32
ALU = mybir.AluOpType
ACT = mybir.ActivationFunctionType
AX = mybir.AxisListType
RMAX = bass.bass_isa.ReduceOp.max
ds = bass.ds

P = 128
D = 256
DC = D // P
TB = 2
RB = TB * P
JC = 4
RING = 4
EPS = 1e-5
KQ = 32
H = 4
FO = D // H
FH = FO + 1
SLOPE = 0.2
BIG = 2.0 ** 60
LOG2E = 1.4426950408889634
LN2 = 0.6931471805599453
ROUND = 1.5 * 2.0 ** 23
LIFT2 = 60
LIFT3 = 4.0
IB = 1024
IT = IB // P
CJ = 2
KB = 1024


def at_least(engine, sem, count):
    if not isinstance(count, int) or count > 0:
        engine.wait_ge(sem, count)


class Steps:

    def __init__(self, engine, sem, base=0):
        self.engine, self.sem, self.base, self.n = engine, sem, base, 0

    def step(self, instruction):
        instruction.then_inc(self.sem, 1)
        self.n += 1

    def join(self):
        at_least(self.engine, self.sem, self.base + self.n)


class Net:

    def __init__(self, nc, n):
        self.nc, self.N, self.NT = nc, n, n // P
        self.NBLK = n // RB
        self.K = self.NT // JC
        nt = self.NT
        self.room = max(nt, 32)
        self.serial = 0
        self.top = 16512
        self.ident = self.fixed("ident", [P, P], F32)
        self.eps = self.fixed("eps", [P, 1], F32)
        self.spare = self.top
        self.w_hi = self.fixed("w_hi", [P, DC, D], F32R)
        self.w_lo = self.fixed("w_lo", [P, DC, D], F32R)
        self.a2_bc = self.fixed("a2_bc", [P, 1, D], F32)
        self.k2 = self.fixed("k2", [P, nt], F32)
        self.q2 = self.fixed("q2", [P, nt], F32)
        self.s_src = self.fixed("s_src", [P, nt, H], F32)
        self.s_dst = self.fixed("s_dst", [P, nt, H], F32)
        self.alpha = self.fixed("alpha", [P, nt, H], F32)
        self.beta = self.fixed("beta", [P, nt, H], F32)
        self.s_big = self.fixed("s_big", [P, nt, H], F32)
        self.arena = self.top
        rows = self.room * D * 4
        self.AT_ACC = self.AT_V2 = self.AT_S0 = self.AT_V3 = 0
        self.AT_NB = rows + KB
        self.AT_HT = self.AT_S1 = 2 * rows + 2 * KB
        self.AT_FREE = 4 * rows + 2 * KB
        self.AT_WH = self.AT_FREE + 20 * KB
        self.ps = nc.alloc_psum_tensor("ps", [P, 8, 512], F32)

    def place(self, name, shape, dt, offset):
        self.serial += 1
        size = self.size(shape, dt)
        assert offset + size <= 229344, (name, offset + size)
        return self.nc.alloc_sbuf_tensor_at(f"{name}_{self.serial}", shape, dt, offset=offset)

    def size(self, shape, dt):
        size = 2 if dt in (BF16, F16) else 4
        for s in shape[1:]:
            size *= s
        return (size + 31) // 32 * 32

    def fixed(self, name, shape, dt):
        t = self.place(name, shape, dt, self.top)
        self.top += self.size(shape, dt)
        return t

    def start(self, offset):
        self.at = self.arena + offset

    def take(self, name, shape, dt):
        t = self.place(name, shape, dt, self.at)
        self.at += self.size(shape, dt)
        return t


def sems(ctx, nc, stage, names, unused=""):
    return [None if n in unused.split() else ctx.enter_context(nc.semaphore(f"{stage}_{n}"))
            for n in names.split()]


def project(pe, net, bank, xt_hi, xt_lo):
    for t in range(TB):
        out = net.ps[:, bank, t * D:(t + 1) * D]
        n = 0
        for c in range(DC):
            for a, w in ((xt_hi, net.w_hi), (xt_hi, net.w_lo), (xt_lo, net.w_hi)):
                last = pe.matmul(out, a[:, t, c, :], w[:, c, :], start=(n == 0), stop=(n == 3 * DC - 1))
                n += 1
    return last


def stage_project0(net, x, w0):
    nc, ps, nb = net.nc, net.ps, net.NBLK
    net.start(net.AT_S0)
    S = net.S = net.take("S0", [P, net.NT, 2 * D], F32R)
    xin = net.take("xin", [P, 2, TB, D], F32)
    xt_hi = net.take("xt_hi", [P, 2, TB, DC, P], F32R)
    xt_lo = net.take("xt_lo", [P, 2, TB, DC, P], F32R)
    w_raw = net.take("w_raw", [P, DC, D], F32)
    with ExitStack() as ctx:
        (w_in, xin0, xin1, zeroed, ident_ready, eps_ready, whi_ready, wlo_ready, turned, hi_ready, lo_ready,
         projected, shi_done, slo_done) = sems(
            ctx, nc, "p0", "w_in xin0 xin1 zeroed ident eps whi wlo turned hi lo projected shi slo")
        xin_ready = [xin0, xin1]
        blk = ctx.enter_context(nc.Block())
        xv = x.rearrange("(b t p) f -> b p t f", t=TB, p=P)
        turned_tiles = lambda b: ps[:, b % 4].rearrange("p (t c n) -> p t c n", t=TB, c=DC)
        sums = lambda b: ps[:, 4 + b % 4].rearrange("p (t f) -> p t f", t=TB)

        @blk.sync
        def _(sp):
            def load(b):
                sp.dma_start(xin[:, b % 2], xv[b]).then_inc(xin_ready[b % 2], 16)

            load(0)
            sp.dma_start(w_raw[:], w0.rearrange("(c p) f -> p c f", p=P)).then_inc(w_in, 16)
            load(1)
            for b in range(2, nb):
                sp.wait_ge(turned, b - 1)
                load(b)

        @blk.gpsimd
        def _(pool):
            pool.memset(net.ident[:], 0.0).then_inc(zeroed, 1)
            pool.wait_ge(zeroed, 1)
            pool.affine_select(out=net.ident[:], in_=net.ident[:], compare_op=ALU.not_equal, fill=1.0,
                               base=0, pattern=[[-1, P]], channel_multiplier=1).then_inc(ident_ready, 1)
            pool.memset(net.eps[:], EPS).then_inc(eps_ready, 1)

        @blk.scalar
        def _(act):
            def turned_hi(b):
                act.wait_ge(turned, b + 1)
                at_least(act, projected, b - 1)
                act.activation(xt_hi[:, b % 2], turned_tiles(b), ACT.Copy).then_inc(hi_ready, 1)

            act.wait_ge(w_in, 16)
            act.activation(net.w_hi[:], w_raw[:], ACT.Copy).then_inc(whi_ready, 1)
            turned_hi(0)
            for b in range(nb):
                if b + 1 < nb:
                    turned_hi(b + 1)
                act.wait_ge(projected, b + 1)
                act.activation(S[:, TB * b:TB * b + TB, 0:D], sums(b), ACT.Copy).then_inc(shi_done, 1)

        @blk.vector
        def _(dve):
            def turned_lo(b):
                dve.wait_ge(hi_ready, b + 1)
                dve.tensor_tensor(xt_lo[:, b % 2], turned_tiles(b), xt_hi[:, b % 2].bitcast(F32),
                                  ALU.subtract).then_inc(lo_ready, 1)

            dve.wait_ge(whi_ready, 1)
            dve.tensor_tensor(net.w_lo[:], w_raw[:], net.w_hi[:].bitcast(F32), ALU.subtract).then_inc(wlo_ready, 1)
            turned_lo(0)
            for b in range(nb):
                if b + 1 < nb:
                    turned_lo(b + 1)
                dve.wait_ge(shi_done, b + 1)
                dve.tensor_tensor(S[:, TB * b:TB * b + TB, D:2 * D], sums(b),
                                  S[:, TB * b:TB * b + TB, 0:D].bitcast(F32), ALU.subtract).then_inc(slo_done, 1)

        @blk.tensor
        def _(pe):
            def turn(b):
                pe.wait_ge(xin_ready[b % 2], 16 * (b // 2 + 1))
                at_least(pe, lo_ready, b - 3)
                for t in range(TB):
                    for c in range(DC):
                        at = (t * DC + c) * P
                        last = pe.transpose(ps[:, b % 4, at:at + P], xin[:, b % 2, t, c * P:c * P + P],
                                            net.ident[:])
                last.then_inc(turned, 1)

            pe.wait_ge(ident_ready, 1)
            turn(0)
            turn(1)
            pe.wait_ge(wlo_ready, 1)
            for b in range(nb):
                if b + 2 < nb:
                    turn(b + 2)
                pe.wait_ge(lo_ready, b + 1)
                at_least(pe, slo_done, b - 3)
                project(pe, net, 4 + b % 4, xt_hi[:, b % 2], xt_lo[:, b % 2]).then_inc(projected, 1)


class Row:

    def __init__(self, pair, par):
        self.b, self.par, self.pair = pair * 2 + par, par, pair

    def back(self, n):
        return Row(self.pair - (n - self.par + 1) // 2, (self.par - n) % 2)


def stage_aggregate(net, kind, adj_t, mask, x_old, x_new, w_next, bias):
    nc, ps, K, nb = net.nc, net.ps, net.K, net.NBLK
    dense = kind < 2
    net.start((net.AT_FREE, net.AT_FREE, net.AT_NB)[kind])
    if dense:
        raw = net.take("raw", [P, RING, JC, RB], F32)
        hi = net.take("hi", [P, RING, JC, RB], F32R)
        lo = net.take("lo", [P, RING, JC, RB], F32R)
        m16 = net.take("m16", [P, 2, JC, RB], BF16) if kind == 0 else None
        S = net.S
    else:
        raw = net.take("raw_mask", [P, RING, JC, RB], BF16)
        lo = net.take("scaled_mask", [P, RING, JC, RB], BF16)
        V = net.V
    y = net.take("y", [P, TB, D], F32)
    ev = net.take("ev", [P, TB, D], F32)
    xn = net.take("xn", [P, 2, TB, D], F32)
    xr = net.take("xr", [P, 2, TB, D], F32)
    stats = net.take("stats", [P, TB, 6], F32)
    mv = net.take("mv", [P, TB, 2], F32)
    sd, r0, r1 = (net.take(name, [P, TB], F32) for name in ("sd", "r0", "r1"))
    if kind == 0:
        bias_bc = net.place("bias_bc", [P, 1, D], F32, net.spare)
        net.start(net.AT_HT)
        HT_hi = net.HT_hi = net.take("HT_hi", [P, DC, net.N], F32R)
        HT_lo = net.HT_lo = net.take("HT_lo", [P, DC, net.N], F32R)
    else:
        xt_hi = net.take("xt_hi", [P, TB, DC, P], F32R)
        xt_lo = net.take("xt_lo", [P, TB, DC, P], F32R)
    if kind == 1:
        h = net.take("h", [P, TB, D], F32)
        v32 = net.take("v32", [P, TB, D + 1], F32)
        f, g, rr = (net.take(name, [P, TB], F32) for name in ("f", "g", "rr"))
        net.start(net.AT_V2)
        V2 = net.V = net.take("V2", [P, net.NT, 2, D + 1], F16)
    if kind == 2:
        a3_bc = net.take("a3_bc", [P, 2, D], F32)
        prod = net.take("prod", [P, 2, TB, D], F32)
        net.start(net.AT_WH)
        WhX = net.WhX = net.take("WhX", [P, net.NT, H, FH], F32)

    SUMS = 1 if dense else 1 + TB
    RESID = 2 if dense else 1
    STATS, ROOT, APPLY, TURNED = 2 * TB, 5, TB, 1
    E = SUMS + RESID + STATS + ROOT + APPLY + TURNED
    AT_RESID = SUMS
    AT_STATS = AT_RESID + RESID
    AT_ROOT = AT_STATS + STATS
    AT_APPLY = AT_ROOT + ROOT
    AT_TURNED = AT_APPLY + APPLY
    SC = (0, 4, 2)[kind]

    strips = (adj_t if dense else mask).rearrange("(k j p) (b r) -> b k p j r", j=JC, p=P, r=RB)
    rows = lambda x: x.rearrange("(b t p) f -> b p t f", t=TB, p=P)
    tiles = lambda m, row: m[:, ds(TB * row.b, TB)]
    turned_tiles = ps[:, 4].rearrange("p (t c n) -> p t c n", t=TB, c=DC)

    with ExitStack() as ctx:
        unused = ("whi wlo projected resident prod scored root v vhi vlo ones", "mask ones",
                  "hi evac mask root v vhi vlo")[kind]
        raw_ready = sems(ctx, nc, f"a{kind}", "raw0 raw1 raw2 raw3")
        mask_out = sems(ctx, nc, f"a{kind}", "mout0 mout1", "" if kind == 0 else "mout0 mout1")
        xr_ready = sems(ctx, nc, f"a{kind}", "xr0 xr1")
        kept = sems(ctx, nc, f"a{kind}", "kept0 kept1")
        (const_in, whi_ready, wlo_ready, hi_ready, lo_ready, mask_ready, pe_done, evac_done, sd_ready, chain,
         turned, xhi_ready, projected, resident, prod_ready, scored, root_ready, v_ready, vhi_ready,
         vlo_ready, ones_ready) = sems(
            ctx, nc, f"a{kind}", "const whi wlo hi lo mask pe evac sd chain turned xhi projected resident "
                                 "prod scored root v vhi vlo ones", unused)
        blk = ctx.enter_context(nc.Block())

        @blk.sync
        def _(sp):
            def load(row, k):
                sp.dma_start(raw[:, k % RING], strips[row.b, k]).then_inc(raw_ready[k % RING], 16)

            def block(row, last=False):
                at_least(sp, chain, (row.b - 2) * E + AT_STATS)
                sp.nop(nofuse=True)
                sp.dma_start(xr[:, row.par], rows(x_old)[row.b]).then_inc(xr_ready[row.par], 16)
                for k in range(K):
                    if kind == 0:
                        sp.wait_ge(mask_ready, row.b * K + k + 1)
                        sp.nop(nofuse=True)
                        sp.dma_start(mask.rearrange("(k j p) (b r) -> b k p j r", j=JC, p=P, r=RB)[row.b, k],
                                     m16[:, k % 2]).then_inc(mask_out[k % 2], 16)
                    elif k + RING < K or not last:
                        sp.wait_ge(lo_ready, row.b * K + k + 1)
                        sp.nop(nofuse=True)
                    if k + RING < K:
                        load(row, k + RING)
                    elif not last:
                        load(row.back(-1), k + RING - K)
                    if k == K - 1 and not (isinstance(row.b, int) and row.b == 0):
                        keep(row.back(1))

            def keep(row):
                sp.wait_ge(chain, row.b * E + AT_TURNED)
                sp.nop(nofuse=True)
                sp.dma_start(rows(x_new)[row.b], xn[:, row.par]).then_inc(kept[row.par], 16)

            if kind == 0:
                sp.dma_start(bias_bc[:, 0], bias.rearrange("(a f) -> a f", a=1).broadcast_to([P, D]))\
                    .then_inc(const_in, 16)
            else:
                sp.dma_start(y[:], w_next.rearrange("(c p) f -> p c f", p=P)).then_inc(const_in, 16)
            for k in range(RING):
                load(Row(0, 0), k)
            if kind == 2:
                for v, a in enumerate(bias):
                    sp.dma_start(a3_bc[:, v], a.rearrange("(o f) -> o f", o=1).broadcast_to([P, D]))\
                        .then_inc(ones_ready, 16)
            block(Row(0, 0))
            block(Row(0, 1))
            with sp.Fori(1, nb // 2 - 1) as pair:
                block(Row(pair, 0))
                block(Row(pair, 1))
            block(Row(nb // 2 - 1, 0))
            block(Row(nb // 2 - 1, 1), last=True)
            keep(Row(nb // 2 - 1, 1))
            for q in kept:
                sp.wait_ge(q, 16 * (nb // 2))
            if kind == 0:
                for q in mask_out:
                    sp.wait_ge(q, 16 * (nb * K // 2))

        def raw_wait(engine, row, k):
            engine.wait_ge(raw_ready[k % RING], (row.b * (K // RING) + k // RING + 1) * 16)

        @blk.gpsimd
        def _(pool):
            def products(row):
                b = row.b
                pool.wait_ge(resident, b + 1)
                at_least(pool, scored, b * SC)
                if kind == 1:
                    at_least(pool, vlo_ready, b)
                    pool.tensor_tensor(v32[:, :, 0:D], h[:], net.a2_bc[:].broadcast_to([P, TB, D]), ALU.mult)\
                        .then_inc(prod_ready, 1)
                else:
                    for v in range(2):
                        vec = a3_bc[:, v:v + 1].rearrange("p o (h f) -> p o h f", h=H)
                        pool.tensor_tensor(prod[:, v].rearrange("p t (h f) -> p t h f", h=H),
                                           tiles(WhX, row)[:, :, :, 0:FO], vec.broadcast_to([P, TB, H, FO]),
                                           ALU.mult).then_inc(prod_ready, 1)

            def values(row):
                pool.wait_ge(root_ready, row.b + 1)
                r = rr[:].rearrange("p (t o) -> p t o", o=1)
                pool.tensor_tensor(v32[:, :, 0:D], h[:], r.broadcast_to([P, TB, D]), ALU.mult).then_inc(v_ready, 1)
                pool.tensor_copy(v32[:, :, D:D + 1], r).then_inc(v_ready, 1)

            if kind == 2:
                pool.memset(WhX[:, :, :, FO:FH], 1.0).then_inc(prod_ready, 1)
                pool.wait_ge(ones_ready, 32)
            if kind:
                pool.wait_ge(wlo_ready, 1)
                products(Row(0, 0))
                if kind == 1:
                    values(Row(0, 0))
                products(Row(0, 1))
                if kind == 1:
                    values(Row(0, 1))
                with pool.Fori(1, nb // 2) as pair:
                    for par in range(2):
                        products(Row(pair, par))
                        if kind == 1:
                            values(Row(pair, par))

        @blk.scalar
        def _(act):
            def split(row, k):
                raw_wait(act, row, k)
                at_least(act, pe_done, row.b * K + k + 1 - RING)
                act.activation(hi[:, k % RING], raw[:, k % RING], ACT.Copy).then_inc(hi_ready, 1)

            def evacuate(row):
                bank = TB * row.par
                act.wait_ge(pe_done, row.b * K + K)
                at_least(act, chain, (row.b - 1) * E + AT_RESID)
                act.activation(ev[:], ps[:, bank:bank + TB, D:2 * D], ACT.Copy).then_inc(evac_done, 1)

            def deviation(row):
                act.wait_ge(chain, row.b * E + AT_ROOT)
                act.activation(sd[:], mv[:, :, 1], ACT.Sqrt, bias=net.eps[:]).then_inc(sd_ready, 1)

            def turned_hi(row):
                act.wait_ge(turned, row.b + 1)
                if kind == 0:
                    part = HT_hi[:, :, ds(RB * row.b, RB)].rearrange("p c (t n) -> p t c n", t=TB)
                    act.activation(part, turned_tiles, ACT.Copy).then_inc(xhi_ready, 1)
                else:
                    at_least(act, projected, row.b)
                    act.activation(xt_hi[:], turned_tiles, ACT.Copy).then_inc(xhi_ready, 1)

            def projection(row):
                act.wait_ge(projected, row.b + 1)
                bank = ps[:, 5].rearrange("p (t f) -> p t f", t=TB)
                if kind == 1:
                    at_least(act, v_ready, 2 * row.b)
                    act.activation(h[:], bank, ACT.Copy).then_inc(resident, 1)
                else:
                    act.wait_ge(prod_ready, 1)
                    act.activation(tiles(WhX, row)[:, :, :, 0:FO],
                                   ps[:, 5].rearrange("p (t h f) -> p t h f", t=TB, h=H), ACT.Copy)\
                        .then_inc(resident, 1)

            def mantissa(row):
                act.wait_ge(scored, (row.b + 1) * SC)
                at_least(act, v_ready, 2 * row.b)
                act.activation(rr[:], g[:], ACT.Exp).then_inc(root_ready, 1)

            def values_hi(row):
                act.wait_ge(v_ready, 2 * row.b + 2)
                act.activation(tiles(V2, row)[:, :, 0], v32[:], ACT.Copy).then_inc(vhi_ready, 1)

            def block(row, before=2):
                for k in range(K):
                    if dense:
                        split(row, k)
                    if k == 2:
                        if before > 1 and kind:
                            projection(row.back(2))
                        if before and dense:
                            evacuate(row.back(1))
                    if k == 4:
                        if before > 1 and kind == 1:
                            mantissa(row.back(2))
                        if before:
                            deviation(row.back(1))
                    if k == 6 and before > 1 and kind == 1:
                        values_hi(row.back(2))
                    if k == 7 and before:
                        turned_hi(row.back(1))

            if kind:
                act.wait_ge(const_in, 16)
                act.activation(net.w_hi[:], y[:], ACT.Copy).then_inc(whi_ready, 1)
            block(Row(0, 0), 0)
            block(Row(0, 1), 1)
            with act.Fori(1, nb // 2) as pair:
                block(Row(pair, 0))
                block(Row(pair, 1))
            last, end = Row(nb // 2 - 1, 0), Row(nb // 2 - 1, 1)
            if kind:
                projection(last)
            if dense:
                evacuate(end)
            if kind == 1:
                mantissa(last)
            deviation(end)
            if kind == 1:
                values_hi(last)
            turned_hi(end)
            if kind:
                projection(end)
            if kind == 1:
                mantissa(end)
                values_hi(end)

        @blk.vector
        def _(dve):
            def split(row, k):
                g_ = row.b * K + k
                if dense:
                    dve.wait_ge(hi_ready, g_ + 1)
                raw_wait(dve, row, k)
                at_least(dve, pe_done, g_ + 1 - RING)
                if dense:
                    dve.tensor_tensor(lo[:, k % RING], raw[:, k % RING], hi[:, k % RING].bitcast(F32),
                                      ALU.subtract).then_inc(lo_ready, 1)
                else:
                    for j in range(JC):
                        last = dve.tensor_scalar(lo[:, k % RING, j], raw[:, k % RING, j],
                                                 net.q2[:, k * JC + j:k * JC + j + 1], None, ALU.mult)
                    last.then_inc(lo_ready, 1)
                if kind == 0:
                    at_least(dve, mask_out[k % 2], (row.b * (K // 2) + k // 2) * 16)
                    dve.tensor_scalar(m16[:, k % 2], raw[:, k % RING], 0.0, None, ALU.is_gt)\
                        .then_inc(mask_ready, 1)

            def sums(row):
                c = Steps(dve, chain, row.b * E)
                banks = ps[:, TB * row.par:TB * row.par + TB]
                dve.wait_ge(pe_done, row.b * K + K)
                if dense:
                    dve.wait_ge(evac_done, row.b + 1)
                c.join()
                if dense:
                    c.step(dve.tensor_tensor(y[:], banks[:, :, 0:D], ev[:], ALU.add))
                else:
                    c.step(dve.reciprocal(r0[:], banks[:, :, D]))
                    c.join()
                    for t in range(TB):
                        c.step(dve.tensor_scalar(y[:, t], banks[:, t, 0:D], r0[:, t:t + 1], 0.0,
                                                 ALU.mult, ALU.max))
                assert c.n == SUMS

            def residual(row):
                c = Steps(dve, chain, row.b * E + AT_RESID)
                c.join()
                if dense:
                    add = bias_bc[:].broadcast_to([P, TB, D]) if kind == 0 else tiles(net.NB, row)
                    c.step(dve.tensor_tensor(y[:], y[:], add, ALU.add))
                    dve.wait_ge(xr_ready[row.par], (row.pair + 1) * 16)
                    c.join()
                    c.step(dve.scalar_tensor_tensor(y[:], y[:], 0.0, xr[:, row.par], ALU.max, ALU.add))
                else:
                    dve.wait_ge(xr_ready[row.par], (row.pair + 1) * 16)
                    c.step(dve.tensor_tensor(y[:], y[:], xr[:, row.par], ALU.add))
                assert c.n == RESID

            def statistics(row):
                c = Steps(dve, chain, row.b * E + AT_STATS)
                c.join()
                for t in range(TB):
                    c.step(dve.bn_stats(stats[:, t], y[:, t]))
                c.join()
                dve.nop(nofuse=True)
                for t in range(TB):
                    c.step(dve.bn_aggr(mv[:, t], stats[:, t]))

            def root(row):
                c = Steps(dve, chain, row.b * E + AT_ROOT)
                dve.wait_ge(sd_ready, row.b + 1)
                c.join()
                c.step(dve.reciprocal(r0[:], sd[:]))
                c.join()
                c.step(dve.tensor_tensor(r1[:], r0[:], r0[:], ALU.mult))
                c.join()
                c.step(dve.scalar_tensor_tensor(r1[:], mv[:, :, 1], net.eps[:], r1[:], ALU.add, ALU.mult))
                c.join()
                c.step(dve.tensor_scalar(r1[:], r1[:], -0.5, 1.5, ALU.mult, ALU.add))
                c.join()
                c.step(dve.tensor_tensor(r1[:], r1[:], r0[:], ALU.mult))
                assert c.n == ROOT

            def apply(row):
                c = Steps(dve, chain, row.b * E + AT_APPLY)
                at_least(dve, kept[row.par], row.pair * 16)
                at_least(dve, turned, row.b - 1)
                c.join()
                for t in range(TB):
                    c.step(dve.tensor_scalar(xn[:, row.par, t], y[:, t], mv[:, t, 0:1], r1[:, t:t + 1],
                                             ALU.subtract, ALU.mult))

            def turned_lo(row):
                c = Steps(dve, chain, row.b * E + AT_TURNED)
                dve.wait_ge(xhi_ready, row.b + 1)
                c.join()
                if kind == 0:
                    pick = lambda m: m[:, :, ds(RB * row.b, RB)].rearrange("p c (t n) -> p t c n", t=TB)
                    c.step(dve.tensor_tensor(pick(HT_lo), turned_tiles, pick(HT_hi).bitcast(F32), ALU.subtract))
                else:
                    c.step(dve.tensor_tensor(xt_lo[:], turned_tiles, xt_hi[:].bitcast(F32), ALU.subtract))

            def scores(row):
                c = Steps(dve, scored, row.b * SC)
                if kind == 1:
                    dve.wait_ge(prod_ready, row.b + 1)
                    c.join()
                    c.step(dve.tensor_reduce(f[:], v32[:, :, 0:D], AX.X, ALU.add))
                    c.join()
                    c.step(dve.tensor_scalar(tiles(net.k2, row), f[:], LOG2E, ROUND, ALU.mult, ALU.add))
                    c.join()
                    c.step(dve.tensor_scalar(tiles(net.k2, row), tiles(net.k2, row), ROUND, None, ALU.subtract))
                    at_least(dve, root_ready, row.b)
                    c.join()
                    c.step(dve.scalar_tensor_tensor(g[:], tiles(net.k2, row), -LN2, f[:], ALU.mult, ALU.add))
                else:
                    dve.wait_ge(prod_ready, 2 * row.b + 3)
                    for v, to in enumerate((net.s_src, net.s_dst)):
                        c.step(dve.tensor_reduce(tiles(to, row).rearrange("p t h -> p (t h)"),
                                                 prod[:, v].rearrange("p t (h f) -> p (t h) f", h=H), AX.X, ALU.add))
                assert c.n == SC

            def values_lo(row):
                dve.wait_ge(vhi_ready, row.b + 1)
                dve.wait_ge(v_ready, 2 * row.b + 2)
                dve.tensor_tensor(tiles(V2, row)[:, :, 1], v32[:], tiles(V2, row)[:, :, 0], ALU.subtract)\
                    .then_inc(vlo_ready, 1)

            def block(row, before=2):
                for k in range(K):
                    split(row, k)
                    if k == 2 and before:
                        sums(row.back(1))
                        residual(row.back(1))
                    if k == 3:
                        if before:
                            statistics(row.back(1))
                        if before > 1 and kind:
                            scores(row.back(2))
                    if k == 5 and before:
                        root(row.back(1))
                        apply(row.back(1))
                    if k == 7:
                        if before:
                            turned_lo(row.back(1))
                        if before > 1 and kind == 1:
                            values_lo(row.back(2))

            if kind == 0:
                dve.wait_ge(const_in, 16)
            else:
                dve.wait_ge(whi_ready, 1)
                dve.tensor_tensor(net.w_lo[:], y[:], net.w_hi[:].bitcast(F32), ALU.subtract)\
                    .then_inc(wlo_ready, 1)
                dve.wait_ge(wlo_ready, 1)
            block(Row(0, 0), 0)
            block(Row(0, 1), 1)
            with dve.Fori(1, nb // 2) as pair:
                block(Row(pair, 0))
                block(Row(pair, 1))
            last, end = Row(nb // 2 - 1, 0), Row(nb // 2 - 1, 1)
            sums(end)
            residual(end)
            statistics(end)
            if kind:
                scores(last)
            root(end)
            apply(end)
            if kind == 1:
                values_lo(last)
            turned_lo(end)
            if kind:
                scores(end)
            if kind == 1:
                values_lo(end)

        @blk.tensor
        def _(pe):
            def chunk(row, k):
                pe.wait_ge(lo_ready, row.b * K + k + 1)
                if k == 0:
                    at_least(pe, chain, (row.b - 2) * E + AT_RESID)
                for j in range(JC):
                    jt = k * JC + j
                    go, end = jt == 0, jt == net.NT - 1
                    for t in range(TB):
                        bank = TB * row.par + t
                        part = slice(t * P, t * P + P)
                        if dense:
                            if not end:
                                pe.matmul(ps[:, bank, :], hi[:, k % RING, j, part], S[:, jt, :],
                                          start=go, stop=False)
                            last = pe.matmul(ps[:, bank, 0:D], lo[:, k % RING, j, part], S[:, jt, 0:D],
                                             start=False, stop=False)
                            if end:
                                last = pe.matmul(ps[:, bank, :], hi[:, k % RING, j, part], S[:, jt, :],
                                                 start=False, stop=True)
                        else:
                            for q in range(2):
                                last = pe.matmul(ps[:, bank, 0:D + 1], lo[:, k % RING, j, part], V[:, jt, q],
                                                 start=go and q == 0, stop=end and q == 1)
                last.then_inc(pe_done, 1)

            def turn(row):
                pe.wait_ge(chain, row.b * E + AT_TURNED)
                for t in range(TB):
                    for c in range(DC):
                        at = (t * DC + c) * P
                        last = pe.transpose(ps[:, 4, at:at + P], xn[:, row.par, t, c * P:c * P + P], net.ident[:])
                last.then_inc(turned, 1)

            def project_block(row):
                pe.wait_ge(chain, row.b * E + E)
                at_least(pe, resident, row.b)
                project(pe, net, 5, xt_hi, xt_lo).then_inc(projected, 1)

            def block(row, before=True):
                for k in range(K):
                    chunk(row, k)
                    if k == 4 and before:
                        turn(row.back(1))
                    if k == 6 and before and kind:
                        project_block(row.back(1))

            if kind:
                pe.wait_ge(wlo_ready, 1)
            block(Row(0, 0), False)
            block(Row(0, 1))
            with pe.Fori(1, nb // 2) as pair:
                block(Row(pair, 0))
                block(Row(pair, 1))
            end = Row(nb // 2 - 1, 1)
            turn(end)
            if kind:
                project_block(end)


def stage_quadratic(net, w1, w1_t, w2, b1):
    nc, ps, nt = net.nc, net.ps, net.NT
    net.start(net.AT_ACC)
    acc = net.acc = net.take("acc", [P, nt, D], F32)
    net.start(net.AT_NB)
    NB = net.NB = net.take("NB", [P, nt, D], F32)
    net.start(net.AT_FREE)
    raw = net.take("w2raw", [P, 2, DC, 2, D], F32)
    whi = net.take("w2hi", [P, 2, DC, 2 * D], F32R)
    wlo = net.take("w2lo", [P, 2, DC, 2 * D], F32R)
    node = net.take("node", [P, nt, KQ], F32)
    C1 = KQ + D
    first_raw = net.take("w1raw", [P, DC, C1], F32)
    first_hi = net.take("w1hi", [P, DC, C1], F32R)
    first_lo = net.take("w1lo", [P, DC, C1], F32R)
    w1t_sb = net.take("w1t", [KQ, D], F32)
    b1_sb = net.take("b1", [KQ, D], F32)
    pairs = KQ // 2
    PF = 2 * DC * 3
    with ExitStack() as ctx:
        raw_ready = sems(ctx, nc, "q", "raw0 raw1")
        (w1_in, wb_in, wb, wb_sb, f_hi, f_lo, zeroed, hi_ready, lo_ready, nodes, node_done, nb_done, mm, chain) = sems(
            ctx, nc, "q", "w1 wb wbm wbs fhi flo zero hi lo nodes noded nbd mm chain")
        blk = ctx.enter_context(nc.Block())
        HT_hi, HT_lo = net.HT_hi, net.HT_lo
        w2v = w2.rearrange("(q k) (c p) f -> q p c k f", k=2, p=P)

        @blk.sync
        def _(sp):
            sp.dma_start(w1t_sb[:], w1_t).then_inc(wb_in, 16)
            sp.dma_start(b1_sb[:], b1).then_inc(wb_in, 16)
            sp.dma_start(first_raw[:, :, 0:KQ], w1.rearrange("(c p) k -> p c k", p=P)).then_inc(w1_in, 16)

            def load(q, par):
                for k in range(2):
                    sp.dma_start(raw[:, par, :, k], w2v[q, :, :, k]).then_inc(raw_ready[par], 16)

            load(0, 0)
            load(1, 1)
            with sp.Fori(1, pairs // 2) as qq:
                for par in range(2):
                    q = qq * 2 + par
                    sp.wait_ge(lo_ready, q - 1)
                    load(q, par)

        @blk.gpsimd
        def _(pool):
            pool.memset(acc[:], 0.0).then_inc(zeroed, 1)

        @blk.scalar
        def _(act):
            act.wait_ge(wb, 1)
            act.activation(first_raw[:, :, KQ:C1], ps[:, 0, :].rearrange("p (c f) -> p c f", c=DC), ACT.Copy)\
                .then_inc(wb_sb, 1)
            act.wait_ge(w1_in, 16)
            act.wait_ge(wb_sb, 1)
            act.activation(first_hi[:], first_raw[:], ACT.Copy).then_inc(f_hi, 1)

            def split(q, par, first):
                act.wait_ge(raw_ready[par], (q - par) * 16 + 32)
                if not first:
                    act.wait_ge(mm, (q - 1) * nt)
                act.activation(whi[:, par].rearrange("p c (k f) -> p c k f", k=2), raw[:, par], ACT.Copy)\
                    .then_inc(hi_ready, 1)

            split(0, 0, True)
            split(1, 1, True)
            for n in range(nt):
                act.wait_ge(node_done, n + 1)
                act.activation(NB[:, n], ps[:, n % 8, KQ:C1], ACT.Copy).then_inc(nb_done, 1)
            with act.Fori(1, pairs // 2) as qq:
                for par in range(2):
                    split(qq * 2 + par, par, False)

        @blk.vector
        def _(dve):
            dve.wait_ge(f_hi, 1)
            dve.tensor_tensor(first_lo[:], first_raw[:], first_hi[:].bitcast(F32), ALU.subtract).then_inc(f_lo, 1)
            for par in range(2):
                dve.wait_ge(hi_ready, par + 1)
                dve.tensor_tensor(wlo[:, par].rearrange("p c (k f) -> p c k f", k=2), raw[:, par],
                                  whi[:, par].rearrange("p c (k f) -> p c k f", k=2).bitcast(F32),
                                  ALU.subtract).then_inc(lo_ready, 1)
            for n in range(nt):
                dve.wait_ge(nodes, n + 1)
                dve.tensor_copy(node[:, n], ps[:, n % 8, 0:KQ]).then_inc(node_done, 1)
            dve.wait_ge(zeroed, 1)
            dve.wait_ge(node_done, nt)

            def weigh(q, n, k):
                dve.scalar_tensor_tensor(acc[:, n], ps[:, n % 8, k * D:(k + 1) * D], node[:, n, ds(2 * q + k, 1)],
                                         acc[:, n], ALU.mult, ALU.add).then_inc(chain, 1)

            def split(q, par):
                dve.wait_ge(hi_ready, q + 1)
                dve.tensor_tensor(wlo[:, par].rearrange("p c (k f) -> p c k f", k=2), raw[:, par],
                                  whi[:, par].rearrange("p c (k f) -> p c k f", k=2).bitcast(F32),
                                  ALU.subtract).then_inc(lo_ready, 1)

            def weigh_all(q, par):
                base = q * nt * 2
                for n in range(nt):
                    if n == 2 and par is not None:
                        split(q + 1, par)
                    dve.wait_ge(mm, q * nt + n + 1)
                    if n or not isinstance(q, int) or q:
                        dve.wait_ge(chain, base + 2 * n)
                    weigh(q, n, 0)
                    dve.wait_ge(chain, base + 2 * n + 1)
                    weigh(q, n, 1)

            weigh_all(0, None)
            with dve.Fori(0, (pairs - 2) // 2) as qq:
                weigh_all(qq * 2 + 1, 0)
                weigh_all(qq * 2 + 2, 1)
            weigh_all(pairs - 1, None)

        @blk.tensor
        def _(pe):
            pe.wait_ge(wb_in, 32)
            for c in range(DC):
                last = pe.matmul(ps[:, 0, c * D:(c + 1) * D], w1t_sb[:, c * P:(c + 1) * P], b1_sb[:],
                                 start=True, stop=True)
            last.then_inc(wb, 1)
            pe.wait_ge(f_lo, 1)
            for n in range(nt):
                if n >= 8:
                    pe.wait_ge(nb_done, n - 7)
                m = 0
                for c in range(DC):
                    cols = slice(n * P, n * P + P)
                    for a, w in ((HT_hi, first_hi), (HT_hi, first_lo), (HT_lo, first_hi)):
                        last = pe.matmul(ps[:, n % 8, 0:C1], a[:, c, cols], w[:, c], start=(m == 0), stop=(m == 5))
                        m += 1
                last.then_inc(nodes, 1)

            def pair(q, par, first):
                pe.wait_ge(lo_ready, q + 1)
                for n in range(nt):
                    if first and n < 8:
                        pe.wait_ge(nb_done, nt - 8 + n + 1)
                    else:
                        pe.wait_ge(chain, (q * nt + n - 7) * 2)
                    m = 0
                    for c in range(DC):
                        cols = slice(n * P, n * P + P)
                        for a, w in ((HT_hi, whi), (HT_hi, wlo), (HT_lo, whi)):
                            last = pe.matmul(ps[:, n % 8, :], a[:, c, cols], w[:, par, c], start=(m == 0),
                                             stop=(m == 5))
                            m += 1
                    last.then_inc(mm, 1)

            pair(0, 0, True)
            pair(1, 1, False)
            with pe.Fori(1, pairs // 2) as qq:
                pair(qq * 2, 0, False)
                pair(qq * 2 + 1, 1, False)


def stage_split(net, w_a_t, a2):
    nc, ps, nt = net.nc, net.ps, net.NT
    net.start(net.AT_S1)
    S = net.S = net.take("S1", [P, nt, 2 * D], F32R)
    wat = net.take("wat", [2, D], F32)
    a_col = net.take("a_col", [2, 1], F32)
    ones = net.take("ones2", [2, P], F32)
    a_rep = net.take("a_rep", [2, P], F32)
    half = nt // 2
    with ExitStack() as ctx:
        v_in, hi_done, lo_done, ones_ready, rep, vec, vdone = sems(ctx, nc, "s", "vin hi lo ones rep vec vdone")
        blk = ctx.enter_context(nc.Block())

        @blk.sync
        def _(sp):
            sp.dma_start(wat[:], w_a_t).then_inc(v_in, 16)
            sp.dma_start(a_col[:], a2).then_inc(v_in, 16)

        @blk.scalar
        def _(act):
            for h in range(2):
                act.activation(S[:, h * half:(h + 1) * half, 0:D], net.acc[:, h * half:(h + 1) * half], ACT.Copy)\
                    .then_inc(hi_done, 1)

        @blk.vector
        def _(dve):
            dve.memset(ones[:], 1.0).then_inc(ones_ready, 1)
            dve.wait_ge(v_in, 32)
            dve.wait_ge(ones_ready, 1)
            dve.tensor_scalar(a_rep[:], ones[:], a_col[:], None, ALU.mult).then_inc(rep, 1)
            dve.wait_ge(vec, 1)
            dve.tensor_copy(net.a2_bc[:, 0, :], ps[:, 0, 0:D]).then_inc(vdone, 1)
            for h in range(2):
                dve.wait_ge(hi_done, h + 1)
                part = slice(h * half, (h + 1) * half)
                dve.tensor_tensor(S[:, part, D:2 * D], net.acc[:, part], S[:, part, 0:D].bitcast(F32),
                                  ALU.subtract).then_inc(lo_done, 1)

        @blk.tensor
        def _(pe):
            pe.wait_ge(rep, 1)
            pe.matmul(ps[:, 0, 0:D], a_rep[:], wat[:], start=True, stop=True).then_inc(vec, 1)


def stage_weights2(net):
    nc, nt = net.nc, net.NT
    net.start(net.AT_FREE)
    m = net.take("m", [P, 1], F32)
    top = net.take("top", [P, 1], F32)
    e = net.take("e", [P, nt], F32)
    bits = net.take("bits", [P, nt], I32)
    with ExitStack() as ctx:
        m_done, top_done, chain = sems(ctx, nc, "w2", "m top chain")
        blk = ctx.enter_context(nc.Block())

        @blk.gpsimd
        def _(pool):
            pool.wait_ge(m_done, 1)
            pool.partition_all_reduce(top[:], m[:], P, RMAX).then_inc(top_done, 1)

        @blk.vector
        def _(dve):
            dve.reduce_max(m[:], net.k2[:], AX.X).then_inc(m_done, 1)
            dve.wait_ge(top_done, 1)
            dve.tensor_scalar(e[:], net.k2[:], top[:], float(127 + LIFT2), ALU.subtract, ALU.add).then_inc(chain, 1)
            dve.wait_ge(chain, 1)
            dve.tensor_scalar(bits[:], e[:], 0.0, None, ALU.max).then_inc(chain, 1)
            dve.wait_ge(chain, 2)
            dve.tensor_scalar(net.q2[:].bitcast(I32), bits[:], 23, None, ALU.logical_shift_left).then_inc(chain, 1)


def stage_values3(net, s_rows):
    nc, nt = net.nc, net.NT
    WhX = net.WhX
    net.start(net.AT_V3)
    V_pos = net.V_pos = net.take("V_pos", [P, H, nt, 3, FH], BF16)
    V_neg = net.V_neg = net.take("V_neg", [P, H, nt, 2, FH], F16)
    net.AT_ATTEND = net.at - net.arena
    G = nt // 2
    UNITS = 2 * H
    v_p = net.take("v_p", [P, 2, G, FH], F32)
    v_n = net.take("v_n", [P, 2, G, FH], F32)
    rest = net.take("rest", [P, 2, G, FH], F32)
    rows = net.take("rows", [P, P], F32)
    mx = net.take("mx", [P, H], F32)
    top = net.take("top3", [P, H], F32)
    lift = net.take("lift", [P, 1], F32)
    unlift = net.take("unlift", [P, 1], F32)
    d, t0, t1, ep, en = (net.take(name, [P, nt, H], F32) for name in ("d", "t0", "t1", "ep", "en"))
    assert net.at - net.arena <= net.AT_WH
    R = nt * H

    with ExitStack() as ctx:
        (lifts, mx_done, top_done, d_done, exps, vp_ready, vn_ready, hi_done, mid_done, low_done, turned, rows_ready,
         rows_out) = sems(ctx, nc, "v3", "lift mx top d exp vp vn hi mid low turned rows rout")
        blk = ctx.enter_context(nc.Block())

        def unit(u):
            return u // 2, slice(u % 2 * G, u % 2 * G + G), u % 2

        def factor(m, u):
            h, part, _ = unit(u)
            return m[:, part, h:h + 1].broadcast_to([P, G, FH])

        @blk.sync
        def _(sp):
            sp.wait_ge(rows_ready, 1)
            sp.dma_start(s_rows.rearrange("h (t p) -> t h p", p=P), rows[0:R, :]).then_inc(rows_out, 16)
            sp.wait_ge(rows_out, 16)

        @blk.gpsimd
        def _(pool):
            pool.memset(lift[:], LIFT3).then_inc(lifts, 1)
            pool.memset(unlift[:], -LIFT3).then_inc(lifts, 1)
            pool.wait_ge(mx_done, 1)
            pool.partition_all_reduce(top[:], mx[:], P, RMAX).then_inc(top_done, 1)
            pool.wait_ge(exps, 2)
            for u in range(UNITS):
                h, part, s = unit(u)
                at_least(pool, low_done, 2 * (u - 1))
                pool.tensor_tensor(v_n[:, s], WhX[:, part, h], factor(en, u), ALU.mult).then_inc(vn_ready, 1)

        @blk.tensor
        def _(pe):
            pe.transpose(net.ps[0:R, 0, 0:P], net.s_src[:].rearrange("p t h -> p (t h)"), net.ident[:])\
                .then_inc(turned, 1)

        @blk.scalar
        def _(act):
            act.wait_ge(turned, 1)
            act.activation(rows[0:R, :], net.ps[0:R, 0, 0:P], ACT.Copy).then_inc(rows_ready, 1)
            act.wait_ge(lifts, 2)
            act.wait_ge(d_done, 1)
            act.activation(ep[:], d[:], ACT.Exp).then_inc(exps, 1)
            act.activation(en[:], d[:], ACT.Exp, bias=lift[:], scale=SLOPE).then_inc(exps, 1)
            act.wait_ge(d_done, 4)
            act.activation(net.alpha[:], t0[:], ACT.Exp, scale=1.0 - SLOPE).then_inc(exps, 1)
            act.activation(net.beta[:], t1[:], ACT.Exp, bias=unlift[:], scale=SLOPE - 1.0).then_inc(exps, 1)
            for u in range(UNITS):
                h, part, s = unit(u)
                act.wait_ge(vp_ready, u + 1)
                act.activation(V_pos[:, h, part, 0], v_p[:, s], ACT.Copy).then_inc(hi_done, 1)
                act.wait_ge(vn_ready, u + 1)
                act.activation(V_neg[:, h, part, 0], v_n[:, s], ACT.Copy).then_inc(hi_done, 1)
                act.wait_ge(mid_done, u + 1)
                act.activation(V_pos[:, h, part, 1], rest[:, s], ACT.Copy).then_inc(hi_done, 1)

        @blk.vector
        def _(dve):
            def scale(u):
                h, part, s = unit(u)
                dve.tensor_tensor(v_p[:, s], WhX[:, part, h], factor(ep, u), ALU.mult).then_inc(vp_ready, 1)

            dve.reduce_max(mx[:], net.s_dst[:].rearrange("p t h -> p h t"), AX.X).then_inc(mx_done, 1)
            dve.wait_ge(top_done, 1)
            top_bc = top[:].rearrange("p (o h) -> p o h", o=1).broadcast_to([P, nt, H])
            dve.tensor_tensor(d[:], net.s_dst[:], top_bc, ALU.subtract).then_inc(d_done, 1)
            dve.tensor_tensor(t0[:], net.s_src[:], top_bc, ALU.add).then_inc(d_done, 1)
            dve.wait_ge(d_done, 2)
            dve.tensor_scalar(t1[:], t0[:], 0.0, None, ALU.max).then_inc(d_done, 1)
            dve.wait_ge(d_done, 3)
            dve.tensor_scalar(t0[:], t0[:], 0.0, None, ALU.min).then_inc(d_done, 1)
            dve.tensor_scalar(net.s_big[:], net.s_dst[:], BIG, None, ALU.mult).then_inc(d_done, 1)
            dve.wait_ge(exps, 1)
            scale(0)
            for u in range(UNITS):
                h, part, s = unit(u)
                dve.wait_ge(hi_done, 3 * u + 1)
                dve.wait_ge(vp_ready, u + 1)
                dve.tensor_tensor(rest[:, s], v_p[:, s], V_pos[:, h, part, 0], ALU.subtract).then_inc(mid_done, 1)
                if u + 1 < UNITS:
                    dve.wait_ge(mid_done, u)
                    scale(u + 1)
                dve.wait_ge(hi_done, 3 * u + 2)
                dve.tensor_tensor(V_neg[:, h, part, 1], v_n[:, s], V_neg[:, h, part, 0], ALU.subtract)\
                    .then_inc(low_done, 1)
                dve.wait_ge(hi_done, 3 * u + 3)
                dve.wait_ge(mid_done, u + 1)
                dve.tensor_tensor(V_pos[:, h, part, 2], rest[:, s], V_pos[:, h, part, 1], ALU.subtract)\
                    .then_inc(low_done, 1)


def stage_attend(net, mask, s_rows, x_old, out):
    nc, nt, ps = net.nc, net.NT, net.ps
    nib = net.N // IB
    nck = nt // CJ
    net.start(net.AT_ATTEND)
    M = net.take("M", [P, nt, IB], BF16)
    step = net.take("step", [P, 2, CJ, IB], BF16)
    m_pos = net.take("m_pos", [P, 4, CJ, IB], BF16)
    m_neg = net.take("m_neg", [P, 2, CJ, IB], BF16)
    xblk = net.take("xblk", [P, IT, D], F32)
    s_bc = net.take("s_bc", [P, 2, IB], F32)
    q_out = net.take("q_out", [P, IT, FO], F32)
    stats = net.take("stats3", [P, IT, 6], F32)
    mv = net.take("mv3", [P, IT, 2], F32)
    sd, rs, r1 = (net.take(name, [P, IT], F32) for name in ("sd3", "rs3", "r13"))
    u_pos = net.place("u_pos", [P, IT, FH], F32, net.spare)
    u_neg = net.place("u_neg", [P, IT, FH], F32, net.spare + net.size([P, IT, FH], F32))
    V_pos, V_neg = net.V_pos, net.V_neg
    u_less = net.take("u_less", [P, IT, FH], F32)
    WHOLE = 4
    LEAVE = 6
    HEAD = LEAVE + 3
    HALF = IT // 2
    NORM = 2 * IT + 5 + IT
    ROWS = H * HEAD + NORM
    JOIN = 4

    with ExitStack() as ctx:
        m_in = [ctx.enter_context(nc.semaphore(f"t_m{i}")) for i in range(nck)]
        s_in = sems(ctx, nc, "t", "s0 s1")
        (x_in, step_ready, pos_ready, neg_ready, pe_done, chain, joined, sd_ready, o_out) = sems(
            ctx, nc, "t", "x step pos neg pe chain joined sd oout")
        blk = ctx.enter_context(nc.Block())
        mask_src = mask.rearrange("(k j p) (b r) -> b k p j r", j=CJ, p=P, r=IB)
        s_src = s_rows.rearrange("h (b r) -> b h r", r=IB)
        x_src = x_old.rearrange("(b t p) f -> b p t f", t=IT, p=P)
        o_dst = out.rearrange("(b t p) f -> b p t f", t=IT, p=P)
        NEG = nck - WHOLE

        def before(b, h):
            return (b, h - 1) if h else (b - 1, H - 1)

        @blk.sync
        def _(sp):
            def load_mask(b, k):
                sp.dma_start(M[:, k * CJ:(k + 1) * CJ], mask_src[b, k]).then_inc(m_in[k], 16)

            def load_s(b, h):
                sp.dma_start(s_bc[:, h % 2], s_src[b, h:h + 1].broadcast_to([P, IB])).then_inc(s_in[h % 2], 16)

            def block(b, more):
                for h in range(2, H):
                    sp.wait_ge(step_ready, (b * H + h - 1) * nck)
                    sp.nop(nofuse=True)
                    load_s(b, h)
                if more:
                    for h in range(2):
                        sp.wait_ge(step_ready, (b * H + h + 3) * nck)
                        sp.nop(nofuse=True)
                        load_s(b + 1, h)
                        for k in range(nck // 2 * h, nck // 2 * (h + 1)):
                            sp.wait_ge(pe_done, (b * H + H - 1) * nck + k + 1)
                            sp.nop(nofuse=True)
                            load_mask(b + 1, k)
                sp.wait_ge(chain, (b + 1) * ROWS)
                sp.nop(nofuse=True)
                sp.dma_start(o_dst[b], xblk[:]).then_inc(o_out, 16)
                if more:
                    sp.wait_ge(o_out, (b + 1) * 16)
                    sp.nop(nofuse=True)
                    sp.dma_start(xblk[:], x_src[b + 1]).then_inc(x_in, 16)

            load_s(0, 0)
            load_s(0, 1)
            for k in range(nck):
                load_mask(0, k)
            sp.dma_start(xblk[:], x_src[0]).then_inc(x_in, 16)
            with sp.Fori(0, nib - 1) as b:
                block(b, True)
            block(nib - 1, False)
            sp.wait_ge(o_out, 16 * nib)

        @blk.scalar
        def _(act):
            def steps(b, h, k, s):
                g = (b * H + h) * nck + k
                if h or not isinstance(b, int) or b or not isinstance(k, int) or k > 1:
                    act.wait_ge(pos_ready, g - 1)
                for j in range(CJ):
                    last = act.activation(step[:, s, j], s_bc[:, h % 2], ACT.Sigmoid,
                                          bias=net.s_big[:, ds(k * CJ + j, 1), h], scale=BIG)
                last.then_inc(step_ready, 1)

            def deviation(b):
                act.wait_ge(chain, b * ROWS + H * HEAD + 2 * IT)
                act.activation(sd[:], mv[:, :, 1], ACT.Sqrt, bias=net.eps[:]).then_inc(sd_ready, 1)

            def head(b, h, norm):
                act.wait_ge(s_in[h % 2], (b * (H // 2) + h // 2 + 1) * 16)
                for k in range(6):
                    steps(b, h, k, k % 2)
                if norm:
                    deviation(b - 1)
                with act.Fori(3, nck // 2) as kk:
                    steps(b, h, kk * 2, 0)
                    steps(b, h, kk * 2 + 1, 1)

            for h in range(H):
                head(0, h, False)
            with act.Fori(1, nib) as b:
                for h in range(H):
                    head(b, h, h == 0)
            deviation(nib - 1)

        @blk.gpsimd
        def _(pool):
            def join(b, h):
                u = b * H + h
                pool.wait_ge(chain, b * ROWS + h * HEAD + LEAVE)
                row = lambda m: m[:, ds(b * IT, IT), h:h + 1].broadcast_to([P, IT, FH])
                pool.tensor_tensor(u_neg[:], u_neg[:], u_less[:], ALU.subtract).then_inc(joined, 1)
                pool.tensor_tensor(u_pos[:], u_pos[:], row(net.alpha), ALU.mult).then_inc(joined, 1)
                pool.wait_ge(joined, u * JOIN + 1)
                pool.tensor_tensor(u_neg[:], u_neg[:], row(net.beta), ALU.mult).then_inc(joined, 1)
                pool.wait_ge(joined, u * JOIN + 3)
                pool.tensor_tensor(u_pos[:], u_pos[:], u_neg[:], ALU.add).then_inc(joined, 1)

            with pool.Fori(0, nib) as b:
                for h in range(H):
                    join(b, h)

        @blk.vector
        def _(dve):
            def chunk_mask(k):
                return M[:, k * CJ:(k + 1) * CJ] if isinstance(k, int) else M[:, ds(k * CJ, CJ)]

            def steep(b, h, k, s):
                g = (b * H + h) * nck + k
                dve.wait_ge(step_ready, g + 1)
                if not isinstance(g, int) or g >= 4:
                    dve.wait_ge(pe_done, g - 3)
                dve.tensor_tensor(m_pos[:, s], step[:, s % 2], chunk_mask(k), ALU.mult).then_inc(pos_ready, 1)

            def gentle(b, h, k, s):
                g = (b * H + h) * nck + k
                dve.wait_ge(pos_ready, g + 1)
                dve.wait_ge(pe_done, g - 1)
                dve.tensor_tensor(m_neg[:, s % 2], chunk_mask(k), m_pos[:, s], ALU.subtract).then_inc(neg_ready, 1)

            def leave(b, h):
                c = Steps(dve, chain, b * ROWS + h * HEAD)
                dve.wait_ge(pe_done, (b * H + h + 1) * nck)
                c.join()
                for half in range(2):
                    t = slice(half * HALF, (half + 1) * HALF)
                    c.step(dve.tensor_reduce(u_pos[:, t], ps[:, t, 0:3 * FH].rearrange("p t (q f) -> p t f q", q=3),
                                             AX.X, ALU.add))
                    c.step(dve.tensor_reduce(u_less[:, t],
                                             ps[:, t, 5 * FH:7 * FH].rearrange("p t (q f) -> p t f q", q=2),
                                             AX.X, ALU.add))
                    c.step(dve.tensor_reduce(u_neg[:, t],
                                             ps[:, t, 3 * FH:5 * FH].rearrange("p t (q f) -> p t f q", q=2),
                                             AX.X, ALU.add))
                assert c.n == LEAVE

            def divide(b, h):
                c = Steps(dve, chain, b * ROWS + h * HEAD + LEAVE)
                dve.wait_ge(joined, (b * H + h + 1) * JOIN)
                c.join()
                c.step(dve.reciprocal(rs[:], u_pos[:, :, FO]))
                c.join()
                c.step(dve.tensor_tensor(q_out[:], u_pos[:, :, 0:FO],
                                         rs[:].rearrange("p (t o) -> p t o", o=1).broadcast_to([P, IT, FO]),
                                         ALU.mult))
                if h == 0:
                    dve.wait_ge(x_in, (b + 1) * 16)
                c.join()
                mine = xblk[:, :, h * FO:(h + 1) * FO]
                c.step(dve.tensor_tensor(mine, mine, q_out[:], ALU.add))

            def statistics(b):
                c = Steps(dve, chain, b * ROWS + H * HEAD)
                c.join()
                for t in range(IT):
                    c.step(dve.bn_stats(stats[:, t], xblk[:, t]))
                c.join()
                dve.nop(nofuse=True)
                for t in range(IT):
                    c.step(dve.bn_aggr(mv[:, t], stats[:, t]))

            def norm(b):
                c = Steps(dve, chain, b * ROWS + H * HEAD + 2 * IT)
                dve.wait_ge(sd_ready, b + 1)
                c.join()
                c.step(dve.reciprocal(rs[:], sd[:]))
                c.join()
                c.step(dve.tensor_tensor(r1[:], rs[:], rs[:], ALU.mult))
                c.join()
                c.step(dve.scalar_tensor_tensor(r1[:], mv[:, :, 1], net.eps[:], r1[:], ALU.add, ALU.mult))
                c.join()
                c.step(dve.tensor_scalar(r1[:], r1[:], -0.5, 1.5, ALU.mult, ALU.add))
                c.join()
                c.step(dve.tensor_tensor(r1[:], r1[:], rs[:], ALU.mult))
                c.join()
                for t in range(IT):
                    c.step(dve.tensor_scalar(xblk[:, t], xblk[:, t], mv[:, t, 0:1], r1[:, t:t + 1],
                                             ALU.subtract, ALU.mult))

            def head(b, h, first):
                last = None if first else before(b, h)
                for k in range(nck if h == 0 else 8):
                    if h == 0:
                        dve.wait_ge(m_in[k], (b + 1) * 16)
                    steep(b, h, k, k % 4)
                    if k > WHOLE:
                        gentle(b, h, k - 1, (k - 1) % 4)
                    if last:
                        if k == 1:
                            leave(*last)
                        if k == 4:
                            divide(*last)
                        if k == 5 and h == 0:
                            statistics(b - 1)
                        if k == 6 and h == 0:
                            norm(b - 1)
                if h:
                    with dve.Fori(2, nck // 4) as kk:
                        for s in range(4):
                            steep(b, h, kk * 4 + s, s)
                            gentle(b, h, kk * 4 + s - 1, (s - 1) % 4)
                gentle(b, h, nck - 1, (nck - 1) % 4)

            for h in range(H):
                head(0, h, h == 0)
            with dve.Fori(1, nib) as b:
                for h in range(H):
                    head(b, h, False)
            leave(nib - 1, H - 1)
            divide(nib - 1, H - 1)
            statistics(nib - 1)
            norm(nib - 1)

        @blk.tensor
        def _(pe):
            def tile(h, jt, t, j, k, s, go=False, stop=False):
                part = slice(t * P, t * P + P)
                vp = V_pos[:, h, ds(jt, 1)].rearrange("p o q f -> p (o q f)")
                vn = V_neg[:, h, ds(jt, 1)].rearrange("p o q f -> p (o q f)")
                last = pe.matmul(ps[:, t, 0:3 * FH], m_pos[:, s, j, part], vp, start=go, stop=stop)
                if k is None:
                    return pe.matmul(ps[:, t, 3 * FH:5 * FH], m_neg[:, s % 2, j, part], vn, start=False, stop=stop,
                                     skip_group_check=True)
                pe.matmul(ps[:, t, 3 * FH:5 * FH], M[:, jt, part], vn, start=False, stop=False, skip_group_check=True)
                return pe.matmul(ps[:, t, 5 * FH:7 * FH], m_pos[:, s, j, part], vn, start=False, stop=stop,
                                 skip_group_check=True)

            def opening(b, h, first):
                pe.wait_ge(pos_ready, (b * H + h) * nck + 1)
                for t in range(IT):
                    if not first and t in (0, HALF):
                        lb, lh = before(b, h)
                        pe.wait_ge(chain, lb * ROWS + lh * HEAD + (LEAVE // 2 if t == 0 else LEAVE))
                    for j in range(CJ):
                        last = tile(h, j, t, j, 0, 0, go=j == 0)
                last.then_inc(pe_done, 1)

            def whole(b, h, k, s):
                pe.wait_ge(pos_ready, (b * H + h) * nck + k + 1)
                for j in range(CJ):
                    for t in range(IT):
                        last = tile(h, k * CJ + j, t, j, k, s)
                last.then_inc(pe_done, 1)

            def cut(b, h, k, s, end=False):
                pe.wait_ge(neg_ready, (b * H + h) * NEG + k - WHOLE + 1)
                for j in range(CJ):
                    for t in range(IT):
                        last = tile(h, k * CJ + j, t, j, None, s, stop=end and j == CJ - 1)
                last.then_inc(pe_done, 1)

            def head(b, h, first):
                opening(b, h, first)
                for k in range(1, WHOLE):
                    whole(b, h, k, k)
                with pe.Fori(WHOLE // 4, nck // 4 - 1) as kk:
                    for s in range(4):
                        cut(b, h, kk * 4 + s, s)
                for k in range(nck - 4, nck):
                    cut(b, h, k, k % 4, end=k == nck - 1)

            for h in range(H):
                head(0, h, h == 0)
            with pe.Fori(1, nib) as b:
                for h in range(H):
                    head(b, h, False)


def network(nc, x, adj_t, w0, b0, w1, w1_t, w2, b1, w_gat, w_a_t, a_dst2, w_heads, a3_src, a3_dst, out, upto=9):
    n = x.shape[0]
    net = Net(nc, n)
    mask = nc.dram_tensor("mask", [n, n], BF16).ap()
    net.xs = xs = [nc.dram_tensor(f"x{i}", [n, D], F32).ap() for i in range(3)]
    s_rows = nc.dram_tensor("s_rows", [H, n], F32).ap()
    stage_project0(net, x, w0)
    stage_aggregate(net, 0, adj_t, mask, x, xs[0], None, b0)
    if upto > 0:
        stage_quadratic(net, w1, w1_t, w2, b1)
        stage_split(net, w_a_t, a_dst2)
        stage_aggregate(net, 1, adj_t, None, xs[0], xs[1], w_gat, None)
    if upto > 1:
        stage_weights2(net)
        stage_aggregate(net, 2, None, mask, xs[1], xs[2], w_heads, (a3_src, a3_dst))
    if upto > 2:
        stage_values3(net, s_rows)
        stage_attend(net, mask, s_rows, xs[2], out)
    return net



def kernel(x, adj, L0_gnn_W, L0_gnn_b, L1_gnn_W1, L1_gnn_W2, L1_gnn_b, L2_gnn_w, L2_gnn_w_a, L2_gnn_a,
           L3_gnn_W, L3_gnn_a):
    import numpy as _np
    import concourse.bacc as _bacc
    from concourse import mybir as _mybir
    from concourse.bass_utils import run_bass_kernel_spmd as _run

    heads, _, fo = L3_gnn_W.shape
    laid = {
        "x": x,
        "adj_t": _np.transpose(adj),
        "w0": L0_gnn_W,
        "b0": L0_gnn_b,
        "w1": L1_gnn_W1,
        "w1_t": _np.transpose(L1_gnn_W1),
        "w2": L1_gnn_W2,
        "b1": L1_gnn_b,
        "w_gat": L2_gnn_w,
        "w_a_t": _np.transpose(L2_gnn_w_a),
        "a_dst2": L2_gnn_a[L2_gnn_a.shape[0] // 2:],
        "w_heads": _np.transpose(L3_gnn_W, (1, 0, 2)).reshape(-1, heads * fo),
        "a3_src": L3_gnn_a[:, :fo, 0].reshape(-1),
        "a3_dst": L3_gnn_a[:, fo:, 0].reshape(-1),
    }
    nc = _bacc.Bacc("TRN2", target_bir_lowering=False, num_devices=1)
    arrays, args = {}, []
    for name, a in laid.items():
        a = _np.ascontiguousarray(a)
        arrays[f"in_{name}"] = a
        args.append(nc.dram_tensor(f"in_{name}", a.shape, _mybir.dt.from_np(a.dtype), kind="ExternalInput").ap())
    args.append(nc.dram_tensor("out_0", x.shape, _mybir.dt.from_np(_np.dtype("float32")), kind="ExternalOutput").ap())
    network(nc, *args)
    return _run(nc, [arrays], core_ids=[0]).results[0]["out_0"]
```

```python
from contextlib import ExitStack

import concourse.bass as bass
from concourse import mybir

F32 = mybir.dt.float32
F32R = mybir.dt.float32r
BF16 = mybir.dt.bfloat16
F16 = mybir.dt.float16
I32 = mybir.dt.int32
ALU = mybir.AluOpType
ACT = mybir.ActivationFunctionType
AX = mybir.AxisListType
RMAX = bass.bass_isa.ReduceOp.max
ds = bass.ds

P = 128
D = 256
DC = D // P
TB = 2
RB = TB * P
JC = 4
RING = 4
EPS = 1e-5
KQ = 32
H = 4
FO = D // H
FH = FO + 1
SLOPE = 0.2
BIG = 2.0 ** 60
LOG2E = 1.4426950408889634
LN2 = 0.6931471805599453
ROUND = 1.5 * 2.0 ** 23
LIFT2 = 96
LIFT3 = 4.0
IB = 1024
IT = IB // P
CJ = 2
KB = 1024
END = 229344


def at_least(engine, sem, count):
    if not isinstance(count, int) or count > 0:
        engine.wait_ge(sem, count)


class Steps:

    def __init__(self, engine, sem, base=0):
        self.engine, self.sem, self.base, self.n = engine, sem, base, 0

    def step(self, instruction):
        instruction.then_inc(self.sem, 1)
        self.n += 1

    def join(self):
        at_least(self.engine, self.sem, self.base + self.n)


class Net:

    def __init__(self, nc, n):
        self.nc, self.N, self.NT = nc, n, n // P
        self.NBLK = n // RB
        self.K = self.NT // JC
        nt = self.NT
        self.room = max(nt, 32)
        self.serial = 0
        self.top = 16512
        self.ident = self.fixed("ident", [P, P], F32)
        self.eps = self.fixed("eps", [P, 1], F32)
        self.spare = self.top
        self.w_hi = self.fixed("w_hi", [P, DC, D], F32R)
        self.w_lo = self.fixed("w_lo", [P, DC, D], F32R)
        self.a2_bc = self.fixed("a2_bc", [P, 1, D], F32)
        self.k2 = self.fixed("k2", [P, nt], F32)
        self.q2 = self.fixed("q2", [P, nt], F32)
        self.s_src = self.fixed("s_src", [P, nt, H], F32)
        self.s_dst = self.fixed("s_dst", [P, nt, H], F32)
        self.alpha = self.fixed("alpha", [P, nt, H], F32)
        self.beta = self.fixed("beta", [P, nt, H], F32)
        self.s_big = self.fixed("s_big", [P, nt, H], F32)
        self.arena = self.top
        rows = self.room * D * 4
        self.AT_ACC = self.AT_V2 = self.AT_S0 = self.AT_V3 = 0
        self.AT_NB = rows + KB
        self.AT_HT = self.AT_S1 = 2 * rows + 2 * KB
        self.AT_FREE = 4 * rows + 2 * KB
        self.AT_RAW = self.AT_FREE + 40 * KB
        self.AT_WH = self.AT_FREE + 20 * KB
        self.AT_MASK = self.size([P, H, nt, 3, FH], BF16) + self.size([P, H, nt, 2, FH], F16)
        self.strips = {}
        self.ps = nc.alloc_psum_tensor("ps", [P, 8, 512], F32)

    def place(self, name, shape, dt, offset):
        self.serial += 1
        size = self.size(shape, dt)
        assert offset + size <= END, (name, offset + size)
        return self.nc.alloc_sbuf_tensor_at(f"{name}_{self.serial}", shape, dt, offset=offset)

    def size(self, shape, dt):
        size = 2 if dt in (BF16, F16) else 4
        for s in shape[1:]:
            size *= s
        return (size + 31) // 32 * 32

    def fixed(self, name, shape, dt):
        t = self.place(name, shape, dt, self.top)
        self.top += self.size(shape, dt)
        return t

    def start(self, offset):
        self.at = self.arena + offset

    def take(self, name, shape, dt):
        t = self.place(name, shape, dt, self.at)
        self.at += self.size(shape, dt)
        return t


def sems(ctx, nc, stage, names, unused=""):
    return [None if n in unused.split() else ctx.enter_context(nc.semaphore(f"{stage}_{n}"))
            for n in names.split()]


def plan_strips(ctx, net, kind, source):
    dt, at = (BF16, net.AT_NB) if kind == 2 else (F32, net.AT_RAW)
    raw = net.place("raw", [P, RING, JC, RB], dt, net.arena + at)
    ready = sems(ctx, net.nc, f"a{kind}", "raw0 raw1 raw2 raw3")
    net.strips[kind] = raw, source.rearrange("(k j p) (b r) -> b k p j r", j=JC, p=P, r=RB), ready


def load_first_strip(net, sp, kind):
    raw, strips, ready = net.strips[kind]
    for k in range(RING):
        sp.dma_start(raw[:, k], strips[0, k]).then_inc(ready[k], 16)


def project(pe, net, bank, xt_hi, xt_lo):
    for t in range(TB):
        out = net.ps[:, bank, t * D:(t + 1) * D]
        n = 0
        for c in range(DC):
            for a, w in ((xt_hi, net.w_hi), (xt_hi, net.w_lo), (xt_lo, net.w_hi)):
                last = pe.matmul(out, a[:, t, c, :], w[:, c, :], start=(n == 0), stop=(n == 3 * DC - 1))
                n += 1
    return last


def stage_project0(net, x, w0):
    nc, ps, nb = net.nc, net.ps, net.NBLK
    net.start(net.AT_S0)
    S = net.S = net.take("S0", [P, net.NT, 2 * D], F32R)
    xin = net.take("xin", [P, 2, TB, D], F32)
    xt_hi = net.take("xt_hi", [P, 2, TB, DC, P], F32R)
    xt_lo = net.take("xt_lo", [P, 2, TB, DC, P], F32R)
    w_raw = net.take("w_raw", [P, DC, D], F32)
    with ExitStack() as ctx:
        (w_in, xin0, xin1, zeroed, ident_ready, eps_ready, whi_ready, wlo_ready, turned, hi_ready, lo_ready,
         projected, shi_done, slo_done) = sems(
            ctx, nc, "p0", "w_in xin0 xin1 zeroed ident eps whi wlo turned hi lo projected shi slo")
        xin_ready = [xin0, xin1]
        blk = ctx.enter_context(nc.Block())
        xv = x.rearrange("(b t p) f -> b p t f", t=TB, p=P)
        turned_tiles = lambda b: ps[:, b % 4].rearrange("p (t c n) -> p t c n", t=TB, c=DC)
        sums = lambda b: ps[:, 4 + b % 4].rearrange("p (t f) -> p t f", t=TB)

        @blk.sync
        def _(sp):
            def load(b):
                sp.dma_start(xin[:, b % 2], xv[b]).then_inc(xin_ready[b % 2], 16)

            load(0)
            sp.dma_start(w_raw[:], w0.rearrange("(c p) f -> p c f", p=P)).then_inc(w_in, 16)
            load(1)
            for b in range(2, nb):
                sp.wait_ge(turned, b - 1)
                load(b)
            load_first_strip(net, sp, 0)

        @blk.gpsimd
        def _(pool):
            pool.memset(net.ident[:], 0.0).then_inc(zeroed, 1)
            pool.wait_ge(zeroed, 1)
            pool.affine_select(out=net.ident[:], in_=net.ident[:], compare_op=ALU.not_equal, fill=1.0,
                               base=0, pattern=[[-1, P]], channel_multiplier=1).then_inc(ident_ready, 1)
            pool.memset(net.eps[:], EPS).then_inc(eps_ready, 1)

        @blk.scalar
        def _(act):
            def turned_hi(b):
                act.wait_ge(turned, b + 1)
                at_least(act, projected, b - 1)
                act.activation(xt_hi[:, b % 2], turned_tiles(b), ACT.Copy).then_inc(hi_ready, 1)

            act.wait_ge(w_in, 16)
            act.activation(net.w_hi[:], w_raw[:], ACT.Copy).then_inc(whi_ready, 1)
            turned_hi(0)
            for b in range(nb):
                if b + 1 < nb:
                    turned_hi(b + 1)
                act.wait_ge(projected, b + 1)
                act.activation(S[:, TB * b:TB * b + TB, 0:D], sums(b), ACT.Copy).then_inc(shi_done, 1)

        @blk.vector
        def _(dve):
            def turned_lo(b):
                dve.wait_ge(hi_ready, b + 1)
                dve.tensor_tensor(xt_lo[:, b % 2], turned_tiles(b), xt_hi[:, b % 2].bitcast(F32),
                                  ALU.subtract).then_inc(lo_ready, 1)

            dve.wait_ge(whi_ready, 1)
            dve.tensor_tensor(net.w_lo[:], w_raw[:], net.w_hi[:].bitcast(F32), ALU.subtract).then_inc(wlo_ready, 1)
            turned_lo(0)
            for b in range(nb):
                if b + 1 < nb:
                    turned_lo(b + 1)
                dve.wait_ge(shi_done, b + 1)
                dve.tensor_tensor(S[:, TB * b:TB * b + TB, D:2 * D], sums(b),
                                  S[:, TB * b:TB * b + TB, 0:D].bitcast(F32), ALU.subtract).then_inc(slo_done, 1)

        @blk.tensor
        def _(pe):
            def turn(b):
                pe.wait_ge(xin_ready[b % 2], 16 * (b // 2 + 1))
                at_least(pe, lo_ready, b - 3)
                for t in range(TB):
                    for c in range(DC):
                        at = (t * DC + c) * P
                        last = pe.transpose(ps[:, b % 4, at:at + P], xin[:, b % 2, t, c * P:c * P + P],
                                            net.ident[:])
                last.then_inc(turned, 1)

            pe.wait_ge(ident_ready, 1)
            turn(0)
            turn(1)
            pe.wait_ge(wlo_ready, 1)
            for b in range(nb):
                if b + 2 < nb:
                    turn(b + 2)
                pe.wait_ge(lo_ready, b + 1)
                at_least(pe, slo_done, b - 3)
                project(pe, net, 4 + b % 4, xt_hi[:, b % 2], xt_lo[:, b % 2]).then_inc(projected, 1)


class Row:

    def __init__(self, pair, par):
        self.b, self.par, self.pair = pair * 2 + par, par, pair

    def back(self, n):
        return Row(self.pair - (n - self.par + 1) // 2, (self.par - n) % 2)


def stage_aggregate(net, kind, mask, x_old, x_new, w_next, bias):
    nc, ps, K, nb = net.nc, net.ps, net.K, net.NBLK
    dense = kind < 2
    net.start((net.AT_FREE, net.AT_FREE, net.AT_NB)[kind])
    raw, strips, raw_ready = net.strips[kind]
    if dense:
        hi = net.take("hi", [P, RING, JC, RB], F32R)
        lo = net.take("lo", [P, RING, JC, RB], F32R)
    else:
        net.at += net.size(raw.shape, BF16)
        lo = net.take("scaled_mask", [P, RING, JC, RB], BF16)
        V = net.V
    xn = net.take("xn", [P, 2, TB, D], F32)
    xr = net.take("xr", [P, 2, TB, D], F32)
    if dense:
        assert net.at == net.arena + net.AT_RAW
        net.at += net.size(raw.shape, F32)
        m16 = net.take("m16", [P, 2, JC, RB], BF16) if kind == 0 else None
    y = net.take("y", [P, TB, D], F32)
    ev = net.take("ev", [P, TB, D], F32)
    stats = net.take("stats", [P, TB, 6], F32)
    mv = net.take("mv", [P, TB, 2], F32)
    sd, r0, r1 = (net.take(name, [P, TB], F32) for name in ("sd", "r0", "r1"))
    if kind == 0:
        bias_bc = net.place("bias_bc", [P, 1, D], F32, net.spare)
        net.start(net.AT_HT)
        HT_hi = net.HT_hi = net.take("HT_hi", [P, DC, net.N], F32R)
        HT_lo = net.HT_lo = net.take("HT_lo", [P, DC, net.N], F32R)
    else:
        xt_hi = net.take("xt_hi", [P, TB, DC, P], F32R)
        xt_lo = net.take("xt_lo", [P, TB, DC, P], F32R)
    if kind == 1:
        at = net.at
        net.start(net.AT_S1)
        net.S = net.take("S1", [P, net.NT, 2 * D], F32R)
        net.at = at
        h = net.take("h", [P, TB, D], F32)
        v32 = net.take("v32", [P, TB, D + 1], F32)
        f, g, rr = (net.take(name, [P, TB], F32) for name in ("f", "g", "rr"))
        net.start(net.AT_V2)
        V2 = net.V = net.take("V2", [P, net.NT, 2, D + 1], F16)
    if kind == 2:
        k_top = net.take("k_top", [P, 1], F32)
        k_top_all = net.take("k_top_all", [P, 1], F32)
        e2 = net.take("e2", [P, net.NT], F32)
        bits = net.take("bits", [P, net.NT], I32)
        a3_bc = net.take("a3_bc", [P, 2, D], F32)
        prod = net.take("prod", [P, 2, TB, D], F32)
        net.start(net.AT_WH)
        WhX = net.WhX = net.take("WhX", [P, net.NT, H, FH], F32)

    S = net.S if dense else None

    SUMS = 1 if dense else 1 + TB
    RESID = 2 if dense else 1
    STATS, ROOT, APPLY, TURNED = 2 * TB, 5, TB, 1
    E = SUMS + RESID + STATS + ROOT + APPLY + TURNED
    AT_RESID = SUMS
    AT_STATS = AT_RESID + RESID
    AT_ROOT = AT_STATS + STATS
    AT_APPLY = AT_ROOT + ROOT
    AT_TURNED = AT_APPLY + APPLY
    SC = (0, 4, 2)[kind]
    WEIGHTS = K // 2

    rows = lambda x: x.rearrange("(b t p) f -> b p t f", t=TB, p=P)
    tiles = lambda m, row: m[:, ds(TB * row.b, TB)]
    turned_tiles = ps[:, 4].rearrange("p (t c n) -> p t c n", t=TB, c=DC)

    with ExitStack() as ctx:
        unused = ("whi wlo projected resident prod scored root v vhi vlo ones shi slo tpart top pow", "mask ones tpart top pow",
                  "hi evac mask root v vhi vlo shi slo")[kind]
        mask_out = sems(ctx, nc, f"a{kind}", "mout0 mout1", "" if kind == 0 else "mout0 mout1")
        xr_ready = sems(ctx, nc, f"a{kind}", "xr0 xr1")
        kept = sems(ctx, nc, f"a{kind}", "kept0 kept1")
        (const_in, whi_ready, wlo_ready, hi_ready, lo_ready, mask_ready, pe_done, evac_done, sd_ready, chain,
         turned, xhi_ready, projected, resident, prod_ready, scored, root_ready, v_ready, vhi_ready,
         vlo_ready, ones_ready, s_hi, s_lo, top_part, top_done, powers) = sems(
            ctx, nc, f"a{kind}", "const whi wlo hi lo mask pe evac sd chain turned xhi projected resident "
                                 "prod scored root v vhi vlo ones shi slo tpart top pow", unused)
        blk = ctx.enter_context(nc.Block())

        @blk.sync
        def _(sp):
            def load(row, k):
                sp.dma_start(raw[:, k % RING], strips[row.b, k]).then_inc(raw_ready[k % RING], 16)

            def block(row, last=False):
                at_least(sp, chain, (row.b - 2) * E + AT_STATS)
                sp.nop(nofuse=True)
                sp.dma_start(xr[:, row.par], rows(x_old)[row.b]).then_inc(xr_ready[row.par], 16)
                for k in range(K):
                    if kind == 0:
                        sp.wait_ge(mask_ready, row.b * K + k + 1)
                        sp.nop(nofuse=True)
                        sp.dma_start(mask.rearrange("(k j p) (b r) -> b k p j r", j=JC, p=P, r=RB)[row.b, k],
                                     m16[:, k % 2]).then_inc(mask_out[k % 2], 16)
                    elif k + RING < K or not last:
                        sp.wait_ge(lo_ready, row.b * K + k + 1)
                        sp.nop(nofuse=True)
                    if k + RING < K:
                        load(row, k + RING)
                    elif not last:
                        load(row.back(-1), k + RING - K)
                    if k == K - 1 and not (isinstance(row.b, int) and row.b == 0):
                        keep(row.back(1))

            def keep(row):
                sp.wait_ge(chain, row.b * E + AT_TURNED)
                sp.nop(nofuse=True)
                sp.dma_start(rows(x_new)[row.b], xn[:, row.par]).then_inc(kept[row.par], 16)

            if kind == 0:
                sp.dma_start(bias_bc[:, 0], bias.rearrange("(a f) -> a f", a=1).broadcast_to([P, D]))\
                    .then_inc(const_in, 16)
            else:
                sp.dma_start(y[:], w_next.rearrange("(c p) f -> p c f", p=P)).then_inc(const_in, 16)
            if kind == 2:
                for v, a in enumerate(bias):
                    sp.dma_start(a3_bc[:, v], a.rearrange("(o f) -> o f", o=1).broadcast_to([P, D]))\
                        .then_inc(ones_ready, 16)
            block(Row(0, 0))
            block(Row(0, 1))
            with sp.Fori(1, nb // 2 - 1) as pair:
                block(Row(pair, 0))
                block(Row(pair, 1))
            block(Row(nb // 2 - 1, 0))
            block(Row(nb // 2 - 1, 1), last=True)
            if kind == 1:
                load_first_strip(net, sp, 2)
            keep(Row(nb // 2 - 1, 1))
            for q in kept:
                sp.wait_ge(q, 16 * (nb // 2))
            if kind == 0:
                for q in mask_out:
                    sp.wait_ge(q, 16 * (nb * K // 2))

        def raw_wait(engine, row, k):
            engine.wait_ge(raw_ready[k % RING], (row.b * (K // RING) + k // RING + 1) * 16)

        @blk.gpsimd
        def _(pool):
            def products(row):
                b = row.b
                pool.wait_ge(resident, b + 1)
                at_least(pool, scored, b * SC)
                if kind == 1:
                    at_least(pool, vlo_ready, b)
                    pool.tensor_tensor(v32[:, :, 0:D], h[:], net.a2_bc[:].broadcast_to([P, TB, D]), ALU.mult)\
                        .then_inc(prod_ready, 1)
                else:
                    for v in range(2):
                        vec = a3_bc[:, v:v + 1].rearrange("p o (h f) -> p o h f", h=H)
                        pool.tensor_tensor(prod[:, v].rearrange("p t (h f) -> p t h f", h=H),
                                           tiles(WhX, row)[:, :, :, 0:FO], vec.broadcast_to([P, TB, H, FO]),
                                           ALU.mult).then_inc(prod_ready, 1)

            def values(row):
                pool.wait_ge(root_ready, row.b + 1)
                r = rr[:].rearrange("p (t o) -> p t o", o=1)
                pool.tensor_tensor(v32[:, :, 0:D], h[:], r.broadcast_to([P, TB, D]), ALU.mult).then_inc(v_ready, 1)
                pool.tensor_copy(v32[:, :, D:D + 1], r).then_inc(v_ready, 1)

            if kind == 2:
                pool.wait_ge(top_part, 1)
                pool.partition_all_reduce(k_top_all[:], k_top[:], P, RMAX).then_inc(top_done, 1)
                pool.memset(WhX[:, :, :, FO:FH], 1.0).then_inc(prod_ready, 1)
                pool.wait_ge(ones_ready, 32)
            if kind:
                products(Row(0, 0))
                if kind == 1:
                    values(Row(0, 0))
                products(Row(0, 1))
                if kind == 1:
                    values(Row(0, 1))
                with pool.Fori(1, nb // 2) as pair:
                    for par in range(2):
                        products(Row(pair, par))
                        if kind == 1:
                            values(Row(pair, par))

        @blk.scalar
        def _(act):
            def split(row, k):
                raw_wait(act, row, k)
                at_least(act, pe_done, row.b * K + k + 1 - RING)
                act.activation(hi[:, k % RING], raw[:, k % RING], ACT.Copy).then_inc(hi_ready, 1)

            def evacuate(row):
                bank = TB * row.par
                act.wait_ge(pe_done, row.b * K + K)
                at_least(act, chain, (row.b - 1) * E + AT_RESID)
                act.activation(ev[:], ps[:, bank:bank + TB, D:2 * D], ACT.Copy).then_inc(evac_done, 1)

            def deviation(row):
                act.wait_ge(chain, row.b * E + AT_ROOT)
                act.activation(sd[:], mv[:, :, 1], ACT.Sqrt, bias=net.eps[:]).then_inc(sd_ready, 1)

            def turned_hi(row):
                act.wait_ge(turned, row.b + 1)
                if kind == 0:
                    part = HT_hi[:, :, ds(RB * row.b, RB)].rearrange("p c (t n) -> p t c n", t=TB)
                    act.activation(part, turned_tiles, ACT.Copy).then_inc(xhi_ready, 1)
                else:
                    at_least(act, projected, row.b)
                    act.activation(xt_hi[:], turned_tiles, ACT.Copy).then_inc(xhi_ready, 1)

            def projection(row):
                act.wait_ge(projected, row.b + 1)
                bank = ps[:, 5].rearrange("p (t f) -> p t f", t=TB)
                if kind == 1:
                    at_least(act, v_ready, 2 * row.b)
                    act.activation(h[:], bank, ACT.Copy).then_inc(resident, 1)
                else:
                    act.wait_ge(prod_ready, 1)
                    act.activation(tiles(WhX, row)[:, :, :, 0:FO],
                                   ps[:, 5].rearrange("p (t h f) -> p t h f", t=TB, h=H), ACT.Copy)\
                        .then_inc(resident, 1)

            def mantissa(row):
                act.wait_ge(scored, (row.b + 1) * SC)
                at_least(act, v_ready, 2 * row.b)
                act.activation(rr[:], g[:], ACT.Exp).then_inc(root_ready, 1)

            def values_hi(row):
                act.wait_ge(v_ready, 2 * row.b + 2)
                act.activation(tiles(V2, row)[:, :, 0], v32[:], ACT.Copy).then_inc(vhi_ready, 1)

            def block(row, before=2):
                for k in range(K):
                    if before == 0 and kind == 1:
                        part = slice(k * JC, (k + 1) * JC)
                        act.activation(S[:, part, 0:D], net.acc[:, part], ACT.Copy).then_inc(s_hi, 1)
                    if dense:
                        split(row, k)
                    if before == 0 and kind and k == WEIGHTS:
                        act.wait_ge(const_in, 16)
                        act.activation(net.w_hi[:], y[:], ACT.Copy).then_inc(whi_ready, 1)
                    if k == 2:
                        if before > 1 and kind:
                            projection(row.back(2))
                        if before and dense:
                            evacuate(row.back(1))
                    if k == 4:
                        if before > 1 and kind == 1:
                            mantissa(row.back(2))
                        if before:
                            deviation(row.back(1))
                    if k == 6 and before > 1 and kind == 1:
                        values_hi(row.back(2))
                    if k == 7 and before:
                        turned_hi(row.back(1))

            block(Row(0, 0), 0)
            block(Row(0, 1), 1)
            with act.Fori(1, nb // 2) as pair:
                block(Row(pair, 0))
                block(Row(pair, 1))
            last, end = Row(nb // 2 - 1, 0), Row(nb // 2 - 1, 1)
            if kind:
                projection(last)
            if dense:
                evacuate(end)
            deviation(end)
            if kind == 1:
                mantissa(last)
            turned_hi(end)
            if kind == 1:
                values_hi(last)
            if kind:
                projection(end)
            if kind == 1:
                mantissa(end)
                values_hi(end)

        @blk.vector
        def _(dve):
            def split(row, k):
                g_ = row.b * K + k
                if dense:
                    dve.wait_ge(hi_ready, g_ + 1)
                raw_wait(dve, row, k)
                at_least(dve, pe_done, g_ + 1 - RING)
                if dense:
                    dve.tensor_tensor(lo[:, k % RING], raw[:, k % RING], hi[:, k % RING].bitcast(F32),
                                      ALU.subtract).then_inc(lo_ready, 1)
                else:
                    for j in range(JC):
                        last = dve.tensor_scalar(lo[:, k % RING, j], raw[:, k % RING, j],
                                                 net.q2[:, k * JC + j:k * JC + j + 1], None, ALU.mult)
                    last.then_inc(lo_ready, 1)
                if kind == 0:
                    at_least(dve, mask_out[k % 2], (row.b * (K // 2) + k // 2) * 16)
                    dve.tensor_scalar(m16[:, k % 2], raw[:, k % RING], 0.0, None, ALU.is_gt)\
                        .then_inc(mask_ready, 1)

            def weights():
                dve.reduce_max(k_top[:], net.k2[:], AX.X).then_inc(top_part, 1)
                dve.wait_ge(top_done, 1)
                dve.tensor_scalar(e2[:], net.k2[:], k_top_all[:], float(127 + LIFT2), ALU.subtract, ALU.add)\
                    .then_inc(powers, 1)
                dve.wait_ge(powers, 1)
                dve.tensor_scalar(bits[:], e2[:], 0.0, None, ALU.max).then_inc(powers, 1)
                dve.wait_ge(powers, 2)
                dve.tensor_scalar(net.q2[:].bitcast(I32), bits[:], 23, None, ALU.logical_shift_left)\
                    .then_inc(powers, 1)
                dve.wait_ge(powers, 3)

            def sums(row):
                c = Steps(dve, chain, row.b * E)
                banks = ps[:, TB * row.par:TB * row.par + TB]
                dve.wait_ge(pe_done, row.b * K + K)
                if dense:
                    dve.wait_ge(evac_done, row.b + 1)
                c.join()
                if dense:
                    c.step(dve.tensor_tensor(y[:], banks[:, :, 0:D], ev[:], ALU.add))
                else:
                    c.step(dve.reciprocal(r0[:], banks[:, :, D]))
                    c.join()
                    for t in range(TB):
                        c.step(dve.tensor_scalar(y[:, t], banks[:, t, 0:D], r0[:, t:t + 1], 0.0,
                                                 ALU.mult, ALU.max))
                assert c.n == SUMS

            def residual(row):
                c = Steps(dve, chain, row.b * E + AT_RESID)
                c.join()
                if dense:
                    add = bias_bc[:].broadcast_to([P, TB, D]) if kind == 0 else tiles(net.NB, row)
                    c.step(dve.tensor_tensor(y[:], y[:], add, ALU.add))
                    dve.wait_ge(xr_ready[row.par], (row.pair + 1) * 16)
                    c.join()
                    c.step(dve.scalar_tensor_tensor(y[:], y[:], 0.0, xr[:, row.par], ALU.max, ALU.add))
                else:
                    dve.wait_ge(xr_ready[row.par], (row.pair + 1) * 16)
                    c.step(dve.tensor_tensor(y[:], y[:], xr[:, row.par], ALU.add))
                assert c.n == RESID

            def statistics(row):
                c = Steps(dve, chain, row.b * E + AT_STATS)
                c.join()
                for t in range(TB):
                    c.step(dve.bn_stats(stats[:, t], y[:, t]))
                c.join()
                dve.nop(nofuse=True)
                for t in range(TB):
                    c.step(dve.bn_aggr(mv[:, t], stats[:, t]))

            def root(row):
                c = Steps(dve, chain, row.b * E + AT_ROOT)
                dve.wait_ge(sd_ready, row.b + 1)
                c.join()
                c.step(dve.reciprocal(r0[:], sd[:]))
                c.join()
                c.step(dve.tensor_tensor(r1[:], r0[:], r0[:], ALU.mult))
                c.join()
                c.step(dve.scalar_tensor_tensor(r1[:], mv[:, :, 1], net.eps[:], r1[:], ALU.add, ALU.mult))
                c.join()
                c.step(dve.tensor_scalar(r1[:], r1[:], -0.5, 1.5, ALU.mult, ALU.add))
                c.join()
                c.step(dve.tensor_tensor(r1[:], r1[:], r0[:], ALU.mult))
                assert c.n == ROOT

            def apply(row):
                c = Steps(dve, chain, row.b * E + AT_APPLY)
                at_least(dve, kept[row.par], row.pair * 16)
                at_least(dve, turned, row.b - 1)
                c.join()
                for t in range(TB):
                    c.step(dve.tensor_scalar(xn[:, row.par, t], y[:, t], mv[:, t, 0:1], r1[:, t:t + 1],
                                             ALU.subtract, ALU.mult))

            def turned_lo(row):
                c = Steps(dve, chain, row.b * E + AT_TURNED)
                dve.wait_ge(xhi_ready, row.b + 1)
                c.join()
                if kind == 0:
                    pick = lambda m: m[:, :, ds(RB * row.b, RB)].rearrange("p c (t n) -> p t c n", t=TB)
                    c.step(dve.tensor_tensor(pick(HT_lo), turned_tiles, pick(HT_hi).bitcast(F32), ALU.subtract))
                else:
                    c.step(dve.tensor_tensor(xt_lo[:], turned_tiles, xt_hi[:].bitcast(F32), ALU.subtract))

            def scores(row):
                c = Steps(dve, scored, row.b * SC)
                if kind == 1:
                    dve.wait_ge(prod_ready, row.b + 1)
                    c.join()
                    c.step(dve.tensor_reduce(f[:], v32[:, :, 0:D], AX.X, ALU.add))
                    c.join()
                    c.step(dve.tensor_scalar(tiles(net.k2, row), f[:], LOG2E, ROUND, ALU.mult, ALU.add))
                    c.join()
                    c.step(dve.tensor_scalar(tiles(net.k2, row), tiles(net.k2, row), ROUND, None, ALU.subtract))
                    at_least(dve, root_ready, row.b)
                    c.join()
                    c.step(dve.scalar_tensor_tensor(g[:], tiles(net.k2, row), -LN2, f[:], ALU.mult, ALU.add))
                else:
                    dve.wait_ge(prod_ready, 2 * row.b + 3)
                    for v, to in enumerate((net.s_src, net.s_dst)):
                        c.step(dve.tensor_reduce(tiles(to, row).rearrange("p t h -> p (t h)"),
                                                 prod[:, v].rearrange("p t (h f) -> p (t h) f", h=H), AX.X, ALU.add))
                assert c.n == SC

            def values_lo(row):
                dve.wait_ge(vhi_ready, row.b + 1)
                dve.wait_ge(v_ready, 2 * row.b + 2)
                dve.tensor_tensor(tiles(V2, row)[:, :, 1], v32[:], tiles(V2, row)[:, :, 0], ALU.subtract)\
                    .then_inc(vlo_ready, 1)

            def block(row, before=2):
                for k in range(K):
                    if before == 0 and kind == 1:
                        part = slice(k * JC, (k + 1) * JC)
                        dve.wait_ge(s_hi, k + 1)
                        dve.tensor_tensor(S[:, part, D:2 * D], net.acc[:, part], S[:, part, 0:D].bitcast(F32),
                                          ALU.subtract).then_inc(s_lo, 1)
                    split(row, k)
                    if before == 0 and k == WEIGHTS:
                        if kind:
                            dve.wait_ge(whi_ready, 1)
                            dve.tensor_tensor(net.w_lo[:], y[:], net.w_hi[:].bitcast(F32), ALU.subtract)\
                                .then_inc(wlo_ready, 1)
                            dve.wait_ge(wlo_ready, 1)
                        else:
                            dve.wait_ge(const_in, 16)
                    if k == 2 and before:
                        sums(row.back(1))
                        residual(row.back(1))
                    if k == 3:
                        if before:
                            statistics(row.back(1))
                        if before > 1 and kind:
                            scores(row.back(2))
                    if k == 5 and before:
                        root(row.back(1))
                        apply(row.back(1))
                    if k == 7:
                        if before:
                            turned_lo(row.back(1))
                        if before > 1 and kind == 1:
                            values_lo(row.back(2))

            if kind == 2:
                weights()
            block(Row(0, 0), 0)
            block(Row(0, 1), 1)
            with dve.Fori(1, nb // 2) as pair:
                block(Row(pair, 0))
                block(Row(pair, 1))
            last, end = Row(nb // 2 - 1, 0), Row(nb // 2 - 1, 1)
            sums(end)
            residual(end)
            statistics(end)
            root(end)
            apply(end)
            if kind:
                scores(last)
            turned_lo(end)
            if kind == 1:
                values_lo(last)
            if kind:
                scores(end)
            if kind == 1:
                values_lo(end)

        @blk.tensor
        def _(pe):
            def chunk(row, k):
                if kind == 1 and isinstance(row.b, int) and row.b == 0:
                    pe.wait_ge(s_lo, k + 1)
                pe.wait_ge(lo_ready, row.b * K + k + 1)
                if k == 0:
                    at_least(pe, chain, (row.b - 2) * E + AT_RESID)
                for j in range(JC):
                    jt = k * JC + j
                    go, end = jt == 0, jt == net.NT - 1
                    for t in range(TB):
                        bank = TB * row.par + t
                        part = slice(t * P, t * P + P)
                        if dense:
                            if not end:
                                pe.matmul(ps[:, bank, :], hi[:, k % RING, j, part], S[:, jt, :],
                                          start=go, stop=False)
                            last = pe.matmul(ps[:, bank, 0:D], lo[:, k % RING, j, part], S[:, jt, 0:D],
                                             start=False, stop=False)
                            if end:
                                last = pe.matmul(ps[:, bank, :], hi[:, k % RING, j, part], S[:, jt, :],
                                                 start=False, stop=True)
                        else:
                            for q in range(2):
                                last = pe.matmul(ps[:, bank, 0:D + 1], lo[:, k % RING, j, part], V[:, jt, q],
                                                 start=go and q == 0, stop=end and q == 1)
                last.then_inc(pe_done, 1)

            def turn(row):
                pe.wait_ge(chain, row.b * E + AT_TURNED)
                for t in range(TB):
                    for c in range(DC):
                        at = (t * DC + c) * P
                        last = pe.transpose(ps[:, 4, at:at + P], xn[:, row.par, t, c * P:c * P + P], net.ident[:])
                last.then_inc(turned, 1)

            def project_block(row):
                pe.wait_ge(chain, row.b * E + E)
                at_least(pe, resident, row.b)
                project(pe, net, 5, xt_hi, xt_lo).then_inc(projected, 1)

            def block(row, before=True):
                for k in range(K):
                    chunk(row, k)
                    if k == 4 and before:
                        turn(row.back(1))
                    if k == 6 and before and kind:
                        if isinstance(row.b, int):
                            pe.wait_ge(wlo_ready, 1)
                        project_block(row.back(1))

            block(Row(0, 0), False)
            block(Row(0, 1))
            with pe.Fori(1, nb // 2) as pair:
                block(Row(pair, 0))
                block(Row(pair, 1))
            end = Row(nb // 2 - 1, 1)
            turn(end)
            if kind:
                project_block(end)


def stage_quadratic(net, w1, w1_t, w2, b1, w_a_t, a2):
    nc, ps, nt = net.nc, net.ps, net.NT
    net.start(net.AT_ACC)
    acc = net.acc = net.take("acc", [P, nt, D], F32)
    net.start(net.AT_NB)
    NB = net.NB = net.take("NB", [P, nt, D], F32)
    net.start(net.AT_FREE)
    raw = net.take("w2raw", [P, 2, DC, 2, D], F32)
    whi = net.take("w2hi", [P, 2, DC, 2 * D], F32R)
    wlo = net.take("w2lo", [P, 2, DC, 2 * D], F32R)
    node = net.take("node", [P, nt, KQ], F32)
    C1 = KQ + D
    first_raw = net.take("w1raw", [P, DC, C1], F32)
    first_hi = net.take("w1hi", [P, DC, C1], F32R)
    first_lo = net.take("w1lo", [P, DC, C1], F32R)
    w1t_sb = net.take("w1t", [KQ, D], F32)
    b1_sb = net.take("b1", [KQ, D], F32)
    wat = net.take("wat", [2, D], F32)
    a_col = net.take("a_col", [2, 1], F32)
    ones = net.take("ones2", [2, P], F32)
    a_rep = net.take("a_rep", [2, P], F32)
    assert net.at <= net.arena + net.AT_RAW
    pairs = KQ // 2
    with ExitStack() as ctx:
        raw_ready = sems(ctx, nc, "q", "raw0 raw1")
        (w1_in, wb_in, wb, wb_sb, f_hi, f_lo, zeroed, hi_ready, lo_ready, nodes, node_done, nb_done, mm, chain,
         v_in, ones_ready, rep, vec, vec_done) = sems(
            ctx, nc, "q", "w1 wb wbm wbs fhi flo zero hi lo nodes noded nbd mm chain vin ones rep vec vecd")
        blk = ctx.enter_context(nc.Block())
        HT_hi, HT_lo = net.HT_hi, net.HT_lo
        w2v = w2.rearrange("(q k) (c p) f -> q p c k f", k=2, p=P)

        @blk.sync
        def _(sp):
            sp.dma_start(w1t_sb[:], w1_t).then_inc(wb_in, 16)
            sp.dma_start(b1_sb[:], b1).then_inc(wb_in, 16)
            sp.dma_start(first_raw[:, :, 0:KQ], w1.rearrange("(c p) k -> p c k", p=P)).then_inc(w1_in, 16)

            def load(q, par):
                for k in range(2):
                    sp.dma_start(raw[:, par, :, k], w2v[q, :, :, k]).then_inc(raw_ready[par], 16)

            load(0, 0)
            load(1, 1)
            sp.dma_start(wat[:], w_a_t).then_inc(v_in, 16)
            sp.dma_start(a_col[:], a2).then_inc(v_in, 16)
            with sp.Fori(1, pairs // 2) as qq:
                for par in range(2):
                    q = qq * 2 + par
                    sp.wait_ge(lo_ready, q - 1)
                    load(q, par)
            load_first_strip(net, sp, 1)

        @blk.gpsimd
        def _(pool):
            pool.memset(ones[:], 1.0).then_inc(ones_ready, 1)
            pool.memset(acc[:], 0.0).then_inc(zeroed, 1)

        @blk.scalar
        def _(act):
            act.wait_ge(wb, 1)
            act.activation(first_raw[:, :, KQ:C1], ps[:, 0, :].rearrange("p (c f) -> p c f", c=DC), ACT.Copy)\
                .then_inc(wb_sb, 1)
            act.wait_ge(w1_in, 16)
            act.wait_ge(wb_sb, 1)
            act.activation(first_hi[:], first_raw[:], ACT.Copy).then_inc(f_hi, 1)

            def split(q, par, first):
                act.wait_ge(raw_ready[par], (q - par) * 16 + 32)
                if not first:
                    act.wait_ge(mm, (q - 1) * nt)
                act.activation(whi[:, par].rearrange("p c (k f) -> p c k f", k=2), raw[:, par], ACT.Copy)\
                    .then_inc(hi_ready, 1)

            split(0, 0, True)
            split(1, 1, True)
            for n in range(nt):
                act.wait_ge(node_done, n + 1)
                act.activation(NB[:, n], ps[:, n % 8, KQ:C1], ACT.Copy).then_inc(nb_done, 1)
            with act.Fori(1, pairs // 2) as qq:
                for par in range(2):
                    split(qq * 2 + par, par, False)

        @blk.vector
        def _(dve):
            dve.wait_ge(f_hi, 1)
            dve.tensor_tensor(first_lo[:], first_raw[:], first_hi[:].bitcast(F32), ALU.subtract).then_inc(f_lo, 1)
            for par in range(2):
                dve.wait_ge(hi_ready, par + 1)
                dve.tensor_tensor(wlo[:, par].rearrange("p c (k f) -> p c k f", k=2), raw[:, par],
                                  whi[:, par].rearrange("p c (k f) -> p c k f", k=2).bitcast(F32),
                                  ALU.subtract).then_inc(lo_ready, 1)
            dve.wait_ge(v_in, 32)
            dve.wait_ge(ones_ready, 1)
            dve.tensor_scalar(a_rep[:], ones[:], a_col[:], None, ALU.mult).then_inc(rep, 1)
            dve.wait_ge(vec, 1)
            dve.tensor_copy(net.a2_bc[:, 0, :], ps[:, 7, 0:D]).then_inc(vec_done, 1)
            for n in range(nt):
                dve.wait_ge(nodes, n + 1)
                dve.tensor_copy(node[:, n], ps[:, n % 8, 0:KQ]).then_inc(node_done, 1)
            dve.wait_ge(zeroed, 1)
            dve.wait_ge(node_done, nt)

            def weigh(q, n, k):
                dve.scalar_tensor_tensor(acc[:, n], ps[:, n % 8, k * D:(k + 1) * D], node[:, n, ds(2 * q + k, 1)],
                                         acc[:, n], ALU.mult, ALU.add).then_inc(chain, 1)

            def split(q, par):
                dve.wait_ge(hi_ready, q + 1)
                dve.tensor_tensor(wlo[:, par].rearrange("p c (k f) -> p c k f", k=2), raw[:, par],
                                  whi[:, par].rearrange("p c (k f) -> p c k f", k=2).bitcast(F32),
                                  ALU.subtract).then_inc(lo_ready, 1)

            def weigh_all(q, par):
                for n in range(0, nt, 2):
                    base = (q * nt + n) * 2
                    if n == 2 and par is not None:
                        split(q + 1, par)
                    for t in range(2):
                        dve.wait_ge(mm, q * nt + n + t + 1)
                        weigh(q, n + t, 0)
                    for t in range(2):
                        dve.wait_ge(chain, base + t + 1)
                        weigh(q, n + t, 1)

            weigh_all(0, None)
            with dve.Fori(0, (pairs - 2) // 2) as qq:
                weigh_all(qq * 2 + 1, 0)
                weigh_all(qq * 2 + 2, 1)
            weigh_all(pairs - 1, None)

        @blk.tensor
        def _(pe):
            pe.wait_ge(wb_in, 32)
            for c in range(DC):
                last = pe.matmul(ps[:, 0, c * D:(c + 1) * D], w1t_sb[:, c * P:(c + 1) * P], b1_sb[:],
                                 start=True, stop=True)
            last.then_inc(wb, 1)
            pe.wait_ge(f_lo, 1)
            for n in range(nt):
                if n == 4:
                    pe.wait_ge(rep, 1)
                    pe.matmul(ps[:, 7, 0:D], a_rep[:], wat[:], start=True, stop=True).then_inc(vec, 1)
                if n == 7:
                    pe.wait_ge(vec_done, 1)
                if n >= 8:
                    pe.wait_ge(nb_done, n - 7)
                m = 0
                for c in range(DC):
                    cols = slice(n * P, n * P + P)
                    for a, w in ((HT_hi, first_hi), (HT_hi, first_lo), (HT_lo, first_hi)):
                        last = pe.matmul(ps[:, n % 8, 0:C1], a[:, c, cols], w[:, c], start=(m == 0), stop=(m == 5))
                        m += 1
                last.then_inc(nodes, 1)

            def pair(q, par, first):
                pe.wait_ge(lo_ready, q + 1)
                for n in range(nt):
                    if first and n < 8:
                        pe.wait_ge(nb_done, nt - 8 + n + 1)
                    else:
                        pe.wait_ge(chain, (q * nt + n - 8) * 2 + (2 if n % 2 else 3))
                    m = 0
                    for c in range(DC):
                        cols = slice(n * P, n * P + P)
                        for a, w in ((HT_hi, whi), (HT_hi, wlo), (HT_lo, whi)):
                            last = pe.matmul(ps[:, n % 8, :], a[:, c, cols], w[:, par, c], start=(m == 0),
                                             stop=(m == 5))
                            m += 1
                    last.then_inc(mm, 1)

            pair(0, 0, True)
            pair(1, 1, False)
            with pe.Fori(1, pairs // 2) as qq:
                pair(qq * 2, 0, False)
                pair(qq * 2 + 1, 1, False)


def plan_attend(ctx, net, mask, s_rows):
    nck = net.NT // CJ
    net.M = net.place("M", [P, net.NT, IB], BF16, net.arena + net.AT_MASK)
    net.s_bc = net.place("s_bc", [P, 2, IB], F32, END - net.size([P, 2, IB], F32))
    net.m_in = [ctx.enter_context(net.nc.semaphore(f"t_m{i}")) for i in range(nck)]
    net.s_in = sems(ctx, net.nc, "t", "s0 s1")
    net.mask_src = mask.rearrange("(k j p) (b r) -> b k p j r", j=CJ, p=P, r=IB)
    net.s_src_rows = s_rows.rearrange("h (b r) -> b h r", r=IB)
    net.EARLY = nck // 2
    net.AT_VALUES = net.AT_MASK + net.EARLY * CJ * IB * 2


def load_mask(net, sp, b, k):
    sp.dma_start(net.M[:, k * CJ:(k + 1) * CJ], net.mask_src[b, k]).then_inc(net.m_in[k], 16)


def load_scores(net, sp, b, h):
    sp.dma_start(net.s_bc[:, h % 2], net.s_src_rows[b, h:h + 1].broadcast_to([P, IB])).then_inc(net.s_in[h % 2], 16)


def stage_values3(net, s_rows):
    nc, nt = net.nc, net.NT
    WhX = net.WhX
    net.start(net.AT_V3)
    V_pos = net.V_pos = net.take("V_pos", [P, H, nt, 3, FH], BF16)
    V_neg = net.V_neg = net.take("V_neg", [P, H, nt, 2, FH], F16)
    assert net.at <= net.arena + net.AT_MASK
    net.start(net.AT_VALUES)
    G = nt // 2
    UNITS = 2 * H
    v_p = net.take("v_p", [P, 2, G, FH], F32)
    v_n = net.take("v_n", [P, 2, G, FH], F32)
    rest = net.take("rest", [P, 2, G, FH], F32)
    rows = net.take("rows", [P, P], F32)
    mx = net.take("mx", [P, H], F32)
    top = net.take("top3", [P, H], F32)
    lift = net.take("lift", [P, 1], F32)
    unlift = net.take("unlift", [P, 1], F32)
    d, t0, t1, ep, en = (net.take(name, [P, nt, H], F32) for name in ("d", "t0", "t1", "ep", "en"))
    assert net.at - net.arena <= net.AT_WH
    R = nt * H

    with ExitStack() as ctx:
        vp_ready = sems(ctx, nc, "v3", "vp0 vp1")
        (lifts, mx_done, top_done, d_done, exps, vn_ready, hi_done, mid_done, low_done, turned, rows_ready,
         rows_out) = sems(ctx, nc, "v3", "lift mx top d exp vn hi mid low turned rows rout")
        blk = ctx.enter_context(nc.Block())

        def unit(u):
            return u // 2, slice(u % 2 * G, u % 2 * G + G), u % 2

        def factor(m, u):
            h, part, _ = unit(u)
            return m[:, part, h:h + 1].broadcast_to([P, G, FH])

        @blk.sync
        def _(sp):
            for k in range(net.EARLY):
                load_mask(net, sp, 0, k)
            sp.wait_ge(rows_ready, 1)
            sp.dma_start(s_rows.rearrange("h (t p) -> t h p", p=P), rows[0:R, :]).then_inc(rows_out, 16)
            sp.wait_ge(rows_out, 16)
            load_scores(net, sp, 0, 0)
            load_scores(net, sp, 0, 1)

        @blk.gpsimd
        def _(pool):
            pool.memset(lift[:], LIFT3).then_inc(lifts, 1)
            pool.memset(unlift[:], -LIFT3).then_inc(lifts, 1)
            pool.wait_ge(mx_done, 1)
            pool.partition_all_reduce(top[:], mx[:], P, RMAX).then_inc(top_done, 1)
            pool.wait_ge(exps, 2)
            for u in range(UNITS):
                h, part, s = unit(u)
                at_least(pool, low_done, 2 * (u - 1))
                if u % 2:
                    pool.tensor_tensor(v_p[:, s], WhX[:, part, h], factor(ep, u), ALU.mult).then_inc(vp_ready[s], 1)
                pool.tensor_tensor(v_n[:, s], WhX[:, part, h], factor(en, u), ALU.mult).then_inc(vn_ready, 1)

        @blk.tensor
        def _(pe):
            pe.transpose(net.ps[0:R, 0, 0:P], net.s_src[:].rearrange("p t h -> p (t h)"), net.ident[:])\
                .then_inc(turned, 1)

        @blk.scalar
        def _(act):
            act.wait_ge(turned, 1)
            act.activation(rows[0:R, :], net.ps[0:R, 0, 0:P], ACT.Copy).then_inc(rows_ready, 1)
            act.wait_ge(lifts, 2)
            act.wait_ge(d_done, 1)
            act.activation(ep[:], d[:], ACT.Exp).then_inc(exps, 1)
            act.activation(en[:], d[:], ACT.Exp, bias=lift[:], scale=SLOPE).then_inc(exps, 1)
            act.wait_ge(d_done, 4)
            act.activation(net.alpha[:], t0[:], ACT.Exp, scale=1.0 - SLOPE).then_inc(exps, 1)
            act.activation(net.beta[:], t1[:], ACT.Exp, bias=unlift[:], scale=SLOPE - 1.0).then_inc(exps, 1)
            for u in range(UNITS):
                h, part, s = unit(u)
                act.wait_ge(vp_ready[s], u // 2 + 1)
                act.activation(V_pos[:, h, part, 0], v_p[:, s], ACT.Copy).then_inc(hi_done, 1)
                act.wait_ge(vn_ready, u + 1)
                act.activation(V_neg[:, h, part, 0], v_n[:, s], ACT.Copy).then_inc(hi_done, 1)
                act.wait_ge(mid_done, u + 1)
                act.activation(V_pos[:, h, part, 1], rest[:, s], ACT.Copy).then_inc(hi_done, 1)

        @blk.vector
        def _(dve):
            def scale(u):
                h, part, s = unit(u)
                dve.tensor_tensor(v_p[:, s], WhX[:, part, h], factor(ep, u), ALU.mult).then_inc(vp_ready[s], 1)

            dve.reduce_max(mx[:], net.s_dst[:].rearrange("p t h -> p h t"), AX.X).then_inc(mx_done, 1)
            dve.wait_ge(top_done, 1)
            top_bc = top[:].rearrange("p (o h) -> p o h", o=1).broadcast_to([P, nt, H])
            dve.tensor_tensor(d[:], net.s_dst[:], top_bc, ALU.subtract).then_inc(d_done, 1)
            dve.tensor_tensor(t0[:], net.s_src[:], top_bc, ALU.add).then_inc(d_done, 1)
            dve.wait_ge(d_done, 2)
            dve.tensor_scalar(t1[:], t0[:], 0.0, None, ALU.max).then_inc(d_done, 1)
            dve.wait_ge(d_done, 3)
            dve.tensor_scalar(t0[:], t0[:], 0.0, None, ALU.min).then_inc(d_done, 1)
            dve.tensor_scalar(net.s_big[:], net.s_dst[:], BIG, None, ALU.mult).then_inc(d_done, 1)
            dve.wait_ge(exps, 1)
            scale(0)
            for u in range(UNITS):
                h, part, s = unit(u)
                dve.wait_ge(hi_done, 3 * u + 1)
                dve.wait_ge(vp_ready[s], u // 2 + 1)
                dve.tensor_tensor(rest[:, s], v_p[:, s], V_pos[:, h, part, 0], ALU.subtract).then_inc(mid_done, 1)
                if u % 2 and u + 1 < UNITS:
                    dve.wait_ge(low_done, 2 * u)
                    scale(u + 1)
                dve.wait_ge(hi_done, 3 * u + 2)
                dve.tensor_tensor(V_neg[:, h, part, 1], v_n[:, s], V_neg[:, h, part, 0], ALU.subtract)\
                    .then_inc(low_done, 1)
                dve.wait_ge(hi_done, 3 * u + 3)
                dve.wait_ge(mid_done, u + 1)
                dve.tensor_tensor(V_pos[:, h, part, 2], rest[:, s], V_pos[:, h, part, 1], ALU.subtract)\
                    .then_inc(low_done, 1)


def stage_attend(net, x_old, out):
    nc, nt, ps = net.nc, net.NT, net.ps
    nib = net.N // IB
    nck = nt // CJ
    M, m_in, s_in, s_bc = net.M, net.m_in, net.s_in, net.s_bc
    net.start(net.AT_MASK + net.size(M.shape, BF16))
    step = net.take("step", [P, 2, CJ, IB], BF16)
    m_pos = net.take("m_pos", [P, 4, CJ, IB], BF16)
    m_neg = net.take("m_neg", [P, 2, CJ, IB], BF16)
    xblk = net.take("xblk", [P, IT, D], F32)
    q_out = net.take("q_out", [P, IT, FO], F32)
    stats = net.take("stats3", [P, IT, 6], F32)
    mv = net.take("mv3", [P, IT, 2], F32)
    sd, rs, r1, rd = (net.take(name, [P, IT], F32) for name in ("sd3", "rs3", "r13", "rd3"))
    u_less = net.take("u_less", [P, IT, FH], F32)
    assert net.at <= END - net.size(s_bc.shape, F32)
    u_pos = net.place("u_pos", [P, IT, FH], F32, net.spare)
    u_neg = net.place("u_neg", [P, IT, FH], F32, net.spare + net.size([P, IT, FH], F32))
    V_pos, V_neg = net.V_pos, net.V_neg
    WHOLE = (5, 3, 3, 3)
    OPEN = 2
    PARTS = 4
    PT = IT // PARTS
    STAT_PARTS = 4
    DIVIDE_AT, STATS_AT, NORM_AT = 5, 6, 12
    LEAVE = 3 * PARTS
    HEAD = LEAVE + 1
    NORM = 2 * IT + 5
    ROWS = H * HEAD + NORM
    JOIN = 4
    QUOT = JOIN + 2

    with ExitStack() as ctx:
        (x_in, step_ready, pos_ready, neg_ready, pe_done, part_done, chain, joined, sd_ready, normed, finished, o_out) = sems(
            ctx, nc, "t", "x step pos neg pe part chain joined sd normed finished oout")
        blk = ctx.enter_context(nc.Block())
        x_src = x_old.rearrange("(b t p) f -> b p t f", t=IT, p=P)
        o_dst = out.rearrange("(b t p) f -> b p t f", t=IT, p=P)
        NEGS = H * nck - sum(WHOLE)

        def sides(b, h, k):
            return b * NEGS + h * nck - sum(WHOLE[:h + 1]) + k + 1

        def before(b, h):
            return (b, h - 1) if h else (b - 1, H - 1)

        @blk.sync
        def _(sp):
            def block(b, more):
                for h in range(2, H):
                    sp.wait_ge(step_ready, (b * H + h - 1) * nck)
                    sp.nop(nofuse=True)
                    load_scores(net, sp, b, h)
                if more:
                    for h in range(2):
                        sp.wait_ge(step_ready, (b * H + h + 3) * nck)
                        sp.nop(nofuse=True)
                        load_scores(net, sp, b + 1, h)
                        for k in range(nck // 2 * h, nck // 2 * (h + 1)):
                            sp.wait_ge(pe_done, (b * H + H - 1) * nck + k + 1)
                            sp.nop(nofuse=True)
                            load_mask(net, sp, b + 1, k)
                if more:
                    sp.wait_ge(normed, (b + 1) * IT)
                    sp.nop(nofuse=True)
                    sp.dma_start(o_dst[b], xblk[:]).then_inc(o_out, 16)
                    sp.wait_ge(o_out, (b + 1) * 16)
                    sp.nop(nofuse=True)
                    sp.dma_start(xblk[:], x_src[b + 1]).then_inc(x_in, 16)

            for k in range(net.EARLY, nck):
                load_mask(net, sp, 0, k)
            sp.dma_start(xblk[:], x_src[0]).then_inc(x_in, 16)
            with sp.Fori(0, nib - 1) as b:
                block(b, True)
            block(nib - 1, False)
            for half in range(2):
                t = slice(half * IT // 2, (half + 1) * IT // 2)
                sp.wait_ge(chain, nib * ROWS + t.stop)
                sp.dma_start(o_dst[nib - 1, :, t], xblk[:, t]).then_inc(o_out, 16)
            sp.wait_ge(o_out, 16 * (nib + 1))

        @blk.scalar
        def _(act):
            def steps(b, h, k, s):
                g = (b * H + h) * nck + k
                if h or not isinstance(b, int) or b or not isinstance(k, int) or k > 1:
                    act.wait_ge(pos_ready, g - 1)
                for j in range(CJ):
                    last = act.activation(step[:, s, j], s_bc[:, h % 2], ACT.Sigmoid,
                                          bias=net.s_big[:, ds(k * CJ + j, 1), h], scale=BIG)
                last.then_inc(step_ready, 1)

            def deviation(b):
                act.wait_ge(chain, b * ROWS + H * HEAD + 2 * IT)
                act.activation(sd[:], mv[:, :, 1], ACT.Sqrt, bias=net.eps[:]).then_inc(sd_ready, 1)

            def head(b, h, norm):
                act.wait_ge(s_in[h % 2], (b * (H // 2) + h // 2 + 1) * 16)
                for k in range(nck if norm else 4):
                    if norm and k == NORM_AT:
                        deviation(b - 1)
                    steps(b, h, k, k % 2)
                if not norm:
                    with act.Fori(2, nck // 2) as kk:
                        steps(b, h, kk * 2, 0)
                        steps(b, h, kk * 2 + 1, 1)

            for h in range(H):
                head(0, h, False)
            with act.Fori(1, nib) as b:
                for h in range(H):
                    head(b, h, h == 0)
            deviation(nib - 1)

        @blk.gpsimd
        def _(pool):
            def join(b, h):
                done = (b * H + h) * QUOT
                pool.wait_ge(chain, b * ROWS + h * HEAD + LEAVE)
                row = lambda m: m[:, ds(b * IT, IT), h:h + 1].broadcast_to([P, IT, FH])
                pool.tensor_tensor(u_neg[:], u_neg[:], u_less[:], ALU.subtract).then_inc(joined, 1)
                pool.tensor_tensor(u_pos[:], u_pos[:], row(net.alpha), ALU.mult).then_inc(joined, 1)
                pool.wait_ge(joined, done + 1)
                pool.tensor_tensor(u_neg[:], u_neg[:], row(net.beta), ALU.mult).then_inc(joined, 1)
                pool.wait_ge(joined, done + 3)
                pool.tensor_tensor(u_pos[:], u_pos[:], u_neg[:], ALU.add).then_inc(joined, 1)

            def quotient(b, h):
                done = (b * H + h) * QUOT + JOIN
                pool.wait_ge(chain, b * ROWS + h * HEAD + HEAD)
                pool.wait_ge(joined, done)
                pool.tensor_tensor(q_out[:], u_pos[:, :, 0:FO],
                                   rd[:].rearrange("p (t o) -> p t o", o=1).broadcast_to([P, IT, FO]),
                                   ALU.mult).then_inc(joined, 1)
                if h == 0:
                    pool.wait_ge(x_in, (b + 1) * 16)
                pool.wait_ge(joined, done + 1)
                mine = xblk[:, :, h * FO:(h + 1) * FO]
                pool.tensor_tensor(mine, mine, q_out[:], ALU.add).then_inc(joined, 1)

            def apply(b):
                pool.wait_ge(chain, (b + 1) * ROWS)
                pool.nop(nofuse=True)
                for t in range(IT):
                    pool.tensor_scalar(xblk[:, t], xblk[:, t], mv[:, t, 0:1], r1[:, t:t + 1],
                                       ALU.subtract, ALU.mult).then_inc(normed, 1)

            with pool.Fori(0, nib - 1) as b:
                for h in range(H):
                    join(b, h)
                    quotient(b, h)
                apply(b)
            for h in range(H - 1):
                join(nib - 1, h)
                quotient(nib - 1, h)

        @blk.vector
        def _(dve):
            def chunk_mask(k):
                return M[:, k * CJ:(k + 1) * CJ] if isinstance(k, int) else M[:, ds(k * CJ, CJ)]

            def steep(b, h, k, s):
                g = (b * H + h) * nck + k
                dve.wait_ge(step_ready, g + 1)
                if not isinstance(g, int) or g >= 4:
                    dve.wait_ge(pe_done, g - 3)
                dve.tensor_tensor(m_pos[:, s], step[:, s % 2], chunk_mask(k), ALU.mult).then_inc(pos_ready, 1)

            def gentle(b, h, k, s):
                g = (b * H + h) * nck + k
                dve.wait_ge(pos_ready, g + 1)
                dve.wait_ge(pe_done, g - 1)
                dve.tensor_tensor(m_neg[:, s % 2], chunk_mask(k), m_pos[:, s], ALU.subtract).then_inc(neg_ready, 1)

            def finish(b, h):
                c = Steps(dve, finished)
                part = slice(b * IT, b * IT + IT)
                row = lambda m: m[:, part, h:h + 1].broadcast_to([P, IT, FH])
                dve.wait_ge(chain, b * ROWS + h * HEAD + LEAVE)
                c.step(dve.tensor_tensor(u_neg[:], u_neg[:], u_less[:], ALU.subtract))
                c.step(dve.tensor_tensor(u_pos[:], u_pos[:], row(net.alpha), ALU.mult))
                c.join()
                c.step(dve.tensor_tensor(u_neg[:], u_neg[:], row(net.beta), ALU.mult))
                c.join()
                c.step(dve.tensor_tensor(u_pos[:], u_pos[:], u_neg[:], ALU.add))
                c.join()
                dve.reciprocal(rd[:], u_pos[:, :, FO]).then_inc(chain, 1)
                dve.wait_ge(chain, b * ROWS + (h + 1) * HEAD)
                c.step(dve.tensor_tensor(q_out[:], u_pos[:, :, 0:FO],
                                         rd[:].rearrange("p (t o) -> p t o", o=1).broadcast_to([P, IT, FO]),
                                         ALU.mult))
                c.join()
                mine = xblk[:, :, h * FO:(h + 1) * FO]
                c.step(dve.tensor_tensor(mine, mine, q_out[:], ALU.add))
                c.join()

            def leave(b, h):
                c = Steps(dve, chain, b * ROWS + h * HEAD)
                at_least(dve, joined, (b * H + h) * QUOT)
                c.join()
                for part in range(PARTS):
                    t = slice(part * PT, (part + 1) * PT)
                    dve.wait_ge(part_done, (b * H + h) * PARTS + part + 1)
                    for u, q0, q in ((u_pos, 0, 3), (u_less, 5, 2), (u_neg, 3, 2)):
                        c.step(dve.tensor_reduce(u[:, t], ps[:, t, q0 * FH:(q0 + q) * FH]
                                                 .rearrange("p t (q f) -> p t f q", q=q), AX.X, ALU.add))
                assert c.n == LEAVE

            def divide(b, h):
                c = Steps(dve, chain, b * ROWS + h * HEAD + LEAVE)
                dve.wait_ge(joined, (b * H + h) * QUOT + JOIN)
                c.join()
                c.step(dve.reciprocal(rd[:], u_pos[:, :, FO]))

            def statistics(b, part, heads=H):
                n = IT // STAT_PARTS
                c = Steps(dve, chain, b * ROWS + H * HEAD + part * n)
                dve.wait_ge(joined, (b * H + heads) * QUOT)
                at_least(dve, normed, b * IT)
                c.join()
                for t in range(part * n, (part + 1) * n):
                    c.step(dve.bn_stats(stats[:, t], xblk[:, t]))
                if part == STAT_PARTS - 1:
                    c.join()
                    dve.nop(nofuse=True)
                    for t in range(IT):
                        c.step(dve.bn_aggr(mv[:, t], stats[:, t]))

            def norm(b):
                c = Steps(dve, chain, b * ROWS + H * HEAD + 2 * IT)
                dve.wait_ge(sd_ready, b + 1)
                c.join()
                c.step(dve.reciprocal(rs[:], sd[:]))
                c.join()
                c.step(dve.tensor_tensor(r1[:], rs[:], rs[:], ALU.mult))
                c.join()
                c.step(dve.scalar_tensor_tensor(r1[:], mv[:, :, 1], net.eps[:], r1[:], ALU.add, ALU.mult))
                c.join()
                c.step(dve.tensor_scalar(r1[:], r1[:], -0.5, 1.5, ALU.mult, ALU.add))
                c.join()
                c.step(dve.tensor_tensor(r1[:], r1[:], rs[:], ALU.mult))

            def head(b, h, first):
                last = None if first else before(b, h)
                for k in range(nck if h == 0 else 8):
                    if h == 0:
                        dve.wait_ge(m_in[k], (b + 1) * 16)
                    steep(b, h, k, k % 4)
                    if k > WHOLE[h]:
                        gentle(b, h, k - 1, (k - 1) % 4)
                    if last and k == OPEN - 1:
                        leave(*last)
                    if last and k == DIVIDE_AT:
                        divide(*last)
                    if last and h == 0:
                        if STATS_AT <= k < STATS_AT + STAT_PARTS:
                            statistics(b - 1, k - STATS_AT)
                        if k == NORM_AT:
                            norm(b - 1)
                if h:
                    with dve.Fori(2, nck // 4) as kk:
                        for s in range(4):
                            steep(b, h, kk * 4 + s, s)
                            gentle(b, h, kk * 4 + s - 1, (s - 1) % 4)
                gentle(b, h, nck - 1, (nck - 1) % 4)

            for h in range(H):
                head(0, h, h == 0)
            with dve.Fori(1, nib) as b:
                for h in range(H):
                    head(b, h, False)
            leave(nib - 1, H - 1)
            finish(nib - 1, H - 1)
            for part in range(STAT_PARTS):
                statistics(nib - 1, part, H - 1)
            norm(nib - 1)
            c = Steps(dve, chain, nib * ROWS)
            c.join()
            for t in range(IT):
                c.step(dve.tensor_scalar(xblk[:, t], xblk[:, t], mv[:, t, 0:1], r1[:, t:t + 1],
                                         ALU.subtract, ALU.mult))

        @blk.tensor
        def _(pe):
            def tile(h, jt, t, j, k, s, go=False, stop=False):
                part = slice(t * P, t * P + P)
                vp = V_pos[:, h, ds(jt, 1)].rearrange("p o q f -> p (o q f)")
                vn = V_neg[:, h, ds(jt, 1)].rearrange("p o q f -> p (o q f)")
                last = pe.matmul(ps[:, t, 0:3 * FH], m_pos[:, s, j, part], vp, start=go, stop=stop)
                if k is None:
                    return pe.matmul(ps[:, t, 3 * FH:5 * FH], m_neg[:, s % 2, j, part], vn, start=False, stop=stop,
                                     skip_group_check=True)
                pe.matmul(ps[:, t, 3 * FH:5 * FH], M[:, jt, part], vn, start=False, stop=False, skip_group_check=True)
                return pe.matmul(ps[:, t, 5 * FH:7 * FH], m_pos[:, s, j, part], vn, start=False, stop=stop,
                                 skip_group_check=True)

            def opening(b, h, first):
                pe.wait_ge(pos_ready, (b * H + h) * nck + OPEN)
                for t in range(IT):
                    if not first and t % PT == 0:
                        lb, lh = before(b, h)
                        pe.wait_ge(chain, lb * ROWS + lh * HEAD + (t // PT + 1) * 3)
                    for k in range(OPEN):
                        for j in range(CJ):
                            last = tile(h, k * CJ + j, t, j, k, k, go=k + j == 0)
                last.then_inc(pe_done, OPEN)

            def whole(b, h, k, s):
                pe.wait_ge(pos_ready, (b * H + h) * nck + k + 1)
                for j in range(CJ):
                    for t in range(IT):
                        last = tile(h, k * CJ + j, t, j, k, s)
                last.then_inc(pe_done, 1)

            def closing(b, h):
                k = nck - 1
                pe.wait_ge(neg_ready, sides(b, h, k))
                for t in range(IT):
                    for j in range(CJ):
                        last = tile(h, k * CJ + j, t, j, None, k % 4, stop=j == CJ - 1)
                    if t % PT == PT - 1:
                        last.then_inc(part_done, 1)
                pe.wait_ge(part_done, (b * H + h + 1) * PARTS)
                pe.nop(nofuse=True).then_inc(pe_done, 1)

            def cut(b, h, k, s):
                pe.wait_ge(neg_ready, sides(b, h, k))
                for j in range(CJ):
                    for t in range(IT):
                        last = tile(h, k * CJ + j, t, j, None, s)
                last.then_inc(pe_done, 1)

            def head(b, h, first):
                opening(b, h, first)
                for k in range(OPEN, 8):
                    (whole if k < WHOLE[h] else cut)(b, h, k, k % 4)
                with pe.Fori(2, nck // 4 - 1) as kk:
                    for s in range(4):
                        cut(b, h, kk * 4 + s, s)
                for k in range(nck - 4, nck - 1):
                    cut(b, h, k, k % 4)
                closing(b, h)

            for h in range(H):
                head(0, h, h == 0)
            with pe.Fori(1, nib) as b:
                for h in range(H):
                    head(b, h, False)


def network(nc, x, adj_t, w0, b0, w1, w1_t, w2, b1, w_gat, w_a_t, a_dst2, w_heads, a3_src, a3_dst, out):
    n = x.shape[0]
    net = Net(nc, n)
    mask = nc.dram_tensor("mask", [n, n], BF16).ap()
    x1, x2, x3 = (nc.dram_tensor(f"x{i}", [n, D], F32).ap() for i in (1, 2, 3))
    s_rows = nc.dram_tensor("s_rows", [H, n], F32).ap()
    with ExitStack() as ctx:
        for kind in range(3):
            plan_strips(ctx, net, kind, adj_t if kind < 2 else mask)
        plan_attend(ctx, net, mask, s_rows)
        stage_project0(net, x, w0)
        stage_aggregate(net, 0, mask, x, x1, None, b0)
        stage_quadratic(net, w1, w1_t, w2, b1, w_a_t, a_dst2)
        stage_aggregate(net, 1, None, x1, x2, w_gat, None)
        stage_aggregate(net, 2, mask, x2, x3, w_heads, (a3_src, a3_dst))
        stage_values3(net, s_rows)
        stage_attend(net, x3, out)



def kernel(x, adj, L0_gnn_W, L0_gnn_b, L1_gnn_W1, L1_gnn_W2, L1_gnn_b, L2_gnn_w, L2_gnn_w_a, L2_gnn_a,
           L3_gnn_W, L3_gnn_a):
    import numpy as _np
    import concourse.bacc as _bacc
    from concourse import mybir as _mybir
    from concourse.bass_utils import run_bass_kernel_spmd as _run

    heads, _, fo = L3_gnn_W.shape
    laid = {
        "x": x,
        "adj_t": _np.transpose(adj),
        "w0": L0_gnn_W,
        "b0": L0_gnn_b,
        "w1": L1_gnn_W1,
        "w1_t": _np.transpose(L1_gnn_W1),
        "w2": L1_gnn_W2,
        "b1": L1_gnn_b,
        "w_gat": L2_gnn_w,
        "w_a_t": _np.transpose(L2_gnn_w_a),
        "a_dst2": L2_gnn_a[L2_gnn_a.shape[0] // 2:],
        "w_heads": _np.transpose(L3_gnn_W, (1, 0, 2)).reshape(-1, heads * fo),
        "a3_src": L3_gnn_a[:, :fo, 0].reshape(-1),
        "a3_dst": L3_gnn_a[:, fo:, 0].reshape(-1),
    }
    nc = _bacc.Bacc("TRN2", target_bir_lowering=False, num_devices=1)
    arrays, args = {}, []
    for name, a in laid.items():
        a = _np.ascontiguousarray(a)
        arrays[f"in_{name}"] = a
        args.append(nc.dram_tensor(f"in_{name}", a.shape, _mybir.dt.from_np(a.dtype), kind="ExternalInput").ap())
    args.append(nc.dram_tensor("out_0", x.shape, _mybir.dt.from_np(_np.dtype("float32")), kind="ExternalOutput").ap())
    network(nc, *args)
    return _run(nc, [arrays], core_ids=[0]).results[0]["out_0"]
```
